# Optimizing a Trainium2 kernel written in Bass

```python
import numpy as np
import jax
import jax.numpy as jnp

def _softmax(x, axis=-1):
    return jax.nn.softmax(x, axis=axis)

def _gelu(x):
    return jax.nn.gelu(x, approximate=True)

def _silu(x):
    return jax.nn.silu(x)

def _sigmoid(x):
    return jax.nn.sigmoid(x)

def _layernorm(x, axis=-1, eps=1e-05):
    m = jnp.mean(x, axis=axis, keepdims=True)
    v = jnp.var(x, axis=axis, keepdims=True)
    return (x - m) / jnp.sqrt(v + eps)

def _scatter_add(tgt, idx, src, axis=0):
    return tgt.at[idx].add(src)

def _segment_sum(src, seg, n):
    return jax.ops.segment_sum(src, seg, n)
kernel_name = 'mk_decoder_postln_d2_seqx_r8_9111bf'

def setup_inputs(seed: int=0):
    np.random.seed(seed)
    _w = jnp.asarray

    def _rec_inputs():
        import jax
        import jax.numpy as jnp
        _rk = jax.random.key(seed)
        x = -0.0005207 + 1.001 * jax.random.normal(jax.random.fold_in(_rk, 1), (32, 64, 128), jnp.float32)
        _lenS = 64 - jax.random.randint(jax.random.fold_in(_rk, 7), (32,), 0, max(1, 64 // 4) + 1, jnp.int32)
        _lenS2 = 64 - jax.random.randint(jax.random.fold_in(_rk, 8), (32,), 0, max(1, 64 // 4) + 1, jnp.int32)
        _ctx_512P = jax.random.normal(jax.random.fold_in(_rk, 11), (32, 16, 64), jnp.float32)
        _ctx_512c = jax.random.dirichlet(jax.random.fold_in(_rk, 511), 0.3 * jnp.ones((16,), jnp.float32), (32, 64))
        _ctx_512t = jnp.einsum('bsk,bkd->bsd', _ctx_512c, _ctx_512P)
        _ctx_512t = _ctx_512t * jax.lax.rsqrt(jnp.mean(jnp.square(_ctx_512t)) + 1e-12) * 0.953939
        ctx_512 = 0.502058 + 0.29099 * (_ctx_512t + 0.3 * jax.random.normal(jax.random.fold_in(_rk, 611), (32, 64, 64), jnp.float32))
        itok_BxS2xS_0_7 = jax.random.randint(jax.random.fold_in(_rk, 12), (32, 64, 64), 0, 8, jnp.int32)
        return (x, ctx_512, itok_BxS2xS_0_7)
    x, ctx_512, itok_BxS2xS_0_7 = _rec_inputs()

    def _L0_attn_setup():
        import jax, jax.numpy as jnp
        import numpy as np
        B, L = (2, 128)
        D_MODEL, D_CKV, D_CQ = (128, 32, 64)
        N_HEAD, D_HEAD, D_ROPE = (8, 64, 32)
        N_IDX_HEAD = 4
        K_TS, LW = (96, 64)
        ROPE_BASE = 10000.0

        def _pope(x, angles):
            cos, sin = (jnp.cos(angles), jnp.sin(angles))
            mu1, mu2 = jnp.split(jax.nn.softplus(x), 2, axis=-1)
            return jnp.concatenate([mu1 * cos - mu2 * sin, mu1 * sin + mu2 * cos], axis=-1)

        def _forward(x, W_dkv, W_uk, W_uv, W_dq, W_uq, W_qr, W_kr, W_out, idx_wq, idx_wk, idx_w, raw_delta):
            B_, L_, _ = x.shape
            c_kv = x @ W_dkv
            q_i = (x @ idx_wq).reshape(B_, L_, N_IDX_HEAD, D_HEAD)
            k_i = x @ idx_wk
            s_i = jax.nn.relu(jnp.einsum('bthd,bsd->bths', q_i, k_i))
            I = jnp.einsum('bths,h->bts', s_i, idx_w)
            qpos = jnp.arange(L_)[:, None]
            kpos = jnp.arange(L_)[None, :]
            local = (kpos >= qpos - LW + 1) & (kpos <= qpos)
            causal = kpos > qpos
            I = jnp.where(local[None], jnp.inf, I)
            I = jnp.where(causal[None], -jnp.inf, I)
            kk = min(K_TS, L_)
            _, idx = jax.lax.top_k(I, kk)
            bi = jnp.arange(B_)[:, None, None]
            key_c = (c_kv @ W_uk)[bi, idx].reshape(B_, L_, kk, N_HEAD, D_HEAD)
            value = (c_kv @ W_uv)[bi, idx].reshape(B_, L_, kk, N_HEAD, D_HEAD)
            c_q = x @ W_dq
            query_c = (c_q @ W_uq).reshape(B_, L_, N_HEAD, D_HEAD)
            half = D_ROPE // 2
            theta = 1.0 / ROPE_BASE ** (2.0 * jnp.arange(half, dtype=jnp.float32) / D_ROPE)
            delta = -2.0 * jnp.pi * jax.nn.sigmoid(raw_delta)
            angles_q = jnp.arange(L_, dtype=jnp.float32)[:, None] * theta[None, :] + delta
            query_r = _pope((c_q @ W_qr).reshape(B_, L_, N_HEAD, D_ROPE), angles_q[None, :, None, :])
            kr_sel = (x @ W_kr)[bi, idx]
            angles_k = jnp.arange(kk, dtype=jnp.float32)[:, None] * theta[None, :] + delta
            key_r = _pope(kr_sel, angles_k[None, None, :, :])
            scale = (D_HEAD + D_ROPE) ** (-0.5)
            q_c = query_c.transpose(0, 2, 1, 3)
            q_r = query_r.transpose(0, 2, 1, 3)
            k_c = key_c.transpose(0, 3, 1, 2, 4)
            v = value.transpose(0, 3, 1, 2, 4)
            scores = (jnp.einsum('bhld,bhlkd->bhlk', q_c, k_c) + jnp.einsum('bhld,blkd->bhlk', q_r, key_r)) * scale
            attn = jax.nn.softmax(scores.astype(jnp.float32), axis=-1).astype(v.dtype)
            out = jnp.einsum('bhlk,bhlkd->bhld', attn, v)
            out = out.transpose(0, 2, 1, 3).reshape(B_, L_, N_HEAD * D_HEAD)
            return out @ W_out
        key = jax.random.key(seed)
        ks = jax.random.split(key, 14)

        def w(k, shape, fan_in):
            return jax.random.normal(k, shape, dtype=jnp.float32) * fan_in ** (-0.5)
        return {'x': jax.random.normal(ks[0], (B, L, D_MODEL), dtype=jnp.float32), 'W_dkv': w(ks[1], (D_MODEL, D_CKV), D_MODEL), 'W_uk': w(ks[2], (D_CKV, N_HEAD * D_HEAD), D_CKV), 'W_uv': w(ks[3], (D_CKV, N_HEAD * D_HEAD), D_CKV), 'W_dq': w(ks[4], (D_MODEL, D_CQ), D_MODEL), 'W_uq': w(ks[5], (D_CQ, N_HEAD * D_HEAD), D_CQ), 'W_qr': w(ks[6], (D_CQ, N_HEAD * D_ROPE), D_CQ), 'W_kr': w(ks[7], (D_MODEL, D_ROPE), D_MODEL), 'W_out': w(ks[8], (N_HEAD * D_HEAD, D_MODEL), N_HEAD * D_HEAD), 'idx_wq': w(ks[9], (D_MODEL, N_IDX_HEAD * D_HEAD), D_MODEL), 'idx_wk': w(ks[10], (D_MODEL, D_HEAD), D_MODEL), 'idx_w': jnp.ones((N_IDX_HEAD,), dtype=jnp.float32), 'raw_delta': jax.random.normal(ks[11], (D_ROPE // 2,), dtype=jnp.float32) * 0.1}
    _L0_attn_all = _L0_attn_setup()
    _L0_attn_in = {k: v for k, v in _L0_attn_all.items() if k in ('W_dkv', 'W_uk', 'W_uv', 'W_dq', 'W_uq', 'W_qr', 'W_kr', 'W_out', 'idx_wq', 'idx_wk', 'idx_w', 'raw_delta')}
    del _L0_attn_all

    def _L0_xattn_setup():
        import jax, jax.numpy as jnp
        import numpy as np
        key = jax.random.key(seed)
        k1, k2, k3, k4, k5 = jax.random.split(key, 5)
        B, K, S, E, I, D = (4, 2, 64, 8, 128, 256)
        x = jax.random.normal(k1, (B, S, I), dtype=jnp.float32)
        weights = jax.random.uniform(k2, (B, K, S), dtype=jnp.float32)
        ensembles = jax.random.randint(k3, (B, K, S), 0, E, dtype=jnp.int64)
        lim1 = float(np.sqrt(6.0 / (D + I)))
        proj_in = jax.random.uniform(k4, (E, D, I), dtype=jnp.float32, minval=-lim1, maxval=lim1)
        proj_out = jax.random.uniform(k5, (E, I, D), dtype=jnp.float32, minval=-lim1, maxval=lim1)
        return {'x': x, 'weights': weights, 'ensembles': ensembles, 'proj_in': proj_in, 'proj_out': proj_out}
    _L0_xattn_all = _L0_xattn_setup()
    _L0_xattn_in = {k: v for k, v in _L0_xattn_all.items() if k in ('proj_in', 'proj_out')}
    del _L0_xattn_all

    def _L0_ffn_setup():
        import jax, jax.numpy as jnp
        import numpy as np
        DIM = 128
        HIDDEN = 512
        N_EXPERTS = 8
        K = 2
        TEMP = 1.0

        def _expert_ffn(xf, wa, ba, wb, bb):
            h = xf @ wa.T + ba
            h1, h2 = jnp.split(h, 2, axis=-1)
            h = jax.nn.silu(h1) * h2
            return h @ wb.T + bb
        key = jax.random.key(seed)
        ks = jax.random.split(key, 7)
        s = 0.02
        x = jax.random.normal(ks[0], (4, 256, DIM), dtype=jnp.float32)
        router_w = jax.random.normal(ks[1], (N_EXPERTS, DIM), dtype=jnp.float32) * s
        router_b = jnp.zeros((N_EXPERTS,), dtype=jnp.float32)
        w1 = jax.random.normal(ks[2], (N_EXPERTS, 2 * HIDDEN, DIM), dtype=jnp.float32) * s
        b1 = jnp.zeros((N_EXPERTS, 2 * HIDDEN), dtype=jnp.float32)
        w2 = jax.random.normal(ks[3], (N_EXPERTS, DIM, HIDDEN), dtype=jnp.float32) * s
        b2 = jnp.zeros((N_EXPERTS, DIM), dtype=jnp.float32)
        return {'x': x, 'router_w': router_w, 'router_b': router_b, 'w1': w1, 'b1': b1, 'w2': w2, 'b2': b2}
    _L0_ffn_all = _L0_ffn_setup()
    _L0_ffn_in = {k: v for k, v in _L0_ffn_all.items() if k in ('router_w', 'router_b', 'w1', 'b1', 'w2', 'b2')}
    del _L0_ffn_all

    def _L1_attn_setup():
        import jax, jax.numpy as jnp
        import numpy as np
        import math
        B = 2
        L = 256
        D_MODEL = 128
        D_STATE = 16
        D_CONV = 4
        D_INNER = 2 * D_MODEL
        DT_RANK = math.ceil(D_MODEL / 16)
        DT_MIN, DT_MAX = (0.001, 0.1)

        def _dt_bias(k):
            dt = jnp.exp(jax.random.uniform(k, (D_INNER,)) * (math.log(DT_MAX) - math.log(DT_MIN)) + math.log(DT_MIN))
            dt = jnp.clip(dt, 0.0001, None)
            return (dt + jnp.log(-jnp.expm1(-dt))).astype(jnp.float32)

        def _causal_conv(x, w, b):
            out = jax.lax.conv_general_dilated(x, w[:, None, :], (1,), [(D_CONV - 1, 0)], dimension_numbers=('NCH', 'OIH', 'NCH'), feature_group_count=D_INNER)
            return out + b[None, :, None]

        def _selective_scan(u, dt, A, Bm, Cm, Dp, z):
            h0 = jnp.zeros((u.shape[0], u.shape[1], A.shape[1]), u.dtype)

            def step(h, inp):
                dt_l, u_l, B_l, C_l = inp
                h = jnp.exp(dt_l[..., None] * A) * h + (dt_l * u_l)[..., None] * B_l[:, None, :]
                return (h, jnp.einsum('bdn,bn->bd', h, C_l))
            xs = tuple((jnp.moveaxis(a, -1, 0) for a in (dt, u, Bm, Cm)))
            _, ys = jax.lax.scan(step, h0, xs)
            y = jnp.moveaxis(ys, 0, -1) + Dp[None, :, None] * u
            return y * jax.nn.silu(z)

        def _mamba_dir(xz, conv_w, conv_b, x_proj_w, dt_proj_w, dt_proj_b, A_log, Dp):
            x, z = jnp.split(xz, 2, axis=1)
            x = jax.nn.silu(_causal_conv(x, conv_w, conv_b))
            x_dbl = jnp.einsum('bdl,ed->bel', x, x_proj_w)
            dtv = x_dbl[:, :DT_RANK]
            Bm = x_dbl[:, DT_RANK:DT_RANK + D_STATE]
            Cm = x_dbl[:, DT_RANK + D_STATE:]
            dtv = jax.nn.softplus(jnp.einsum('brl,dr->bdl', dtv, dt_proj_w) + dt_proj_b[None, :, None])
            return _selective_scan(x, dtv, -jnp.exp(A_log), Bm, Cm, Dp, z)
        key = jax.random.key(seed)
        ks = jax.random.split(key, 14)
        nrm = lambda k, shape, s: (jax.random.normal(k, shape) * s).astype(jnp.float32)
        dt_std = DT_RANK ** (-0.5)
        A_log = jnp.log(jnp.broadcast_to(jnp.arange(1, D_STATE + 1, dtype=jnp.float32), (D_INNER, D_STATE)))
        return {'hidden_states': jax.random.normal(ks[0], (B, L, D_MODEL), dtype=jnp.float32), 'in_proj_w': nrm(ks[1], (2 * D_INNER, D_MODEL), D_MODEL ** (-0.5)), 'conv_w': nrm(ks[2], (D_INNER, D_CONV), 0.5), 'conv_b': nrm(ks[3], (D_INNER,), 0.1), 'x_proj_w': nrm(ks[4], (DT_RANK + 2 * D_STATE, D_INNER), D_INNER ** (-0.5)), 'dt_proj_w': jax.random.uniform(ks[5], (D_INNER, DT_RANK), minval=-dt_std, maxval=dt_std).astype(jnp.float32), 'dt_proj_b': _dt_bias(ks[6]), 'A_log': A_log, 'D': jnp.ones((D_INNER,), jnp.float32), 'conv_wb': nrm(ks[7], (D_INNER, D_CONV), 0.5), 'conv_bb': nrm(ks[8], (D_INNER,), 0.1), 'x_proj_wb': nrm(ks[9], (DT_RANK + 2 * D_STATE, D_INNER), D_INNER ** (-0.5)), 'dt_proj_wb': jax.random.uniform(ks[10], (D_INNER, DT_RANK), minval=-dt_std, maxval=dt_std).astype(jnp.float32), 'dt_proj_bb': _dt_bias(ks[11]), 'A_b_log': A_log, 'D_b': jnp.ones((D_INNER,), jnp.float32), 'out_proj_w': nrm(ks[12], (D_MODEL, D_INNER), D_INNER ** (-0.5))}
    _L1_attn_all = _L1_attn_setup()
    _L1_attn_in = {k: v for k, v in _L1_attn_all.items() if k in ('in_proj_w', 'conv_w', 'conv_b', 'x_proj_w', 'dt_proj_w', 'dt_proj_b', 'A_log', 'D', 'conv_wb', 'conv_bb', 'x_proj_wb', 'dt_proj_wb', 'dt_proj_bb', 'A_b_log', 'D_b', 'out_proj_w')}
    del _L1_attn_all

    def _L1_xattn_setup():
        import jax, jax.numpy as jnp
        import numpy as np
        H, D, C1, C2, S, M, B, W = (16, 32, 128, 64, 256, 64, 2, 4)

        def _ln(x, g, b):
            m = jnp.mean(x, -1, keepdims=True)
            v = jnp.var(x, -1, keepdims=True)
            return (x - m) * jax.lax.rsqrt(v + 1e-05) * g + b

        def _mha(x, y, wq, wk, wv, li1_w, li1_b, lnx_g, lnx_b, lny_g, lny_b, ln3_g, ln3_b, li2_w, li2_b, li3_w, li3_b, causal):
            xn = _ln(x, lnx_g, lnx_b)
            yn = _ln(y, lny_g, lny_b)
            q = jnp.einsum('bsc,hcd->bhsd', xn, wq)
            k = jnp.einsum('btc,hcd->bhtd', yn, wk)
            v = jnp.einsum('btc,hcd->bhtd', yn, wv)
            a = jax.nn.softmax(jnp.einsum('bhsd,bhtd->bhst', q, k) * D ** (-0.5), axis=-1)
            if causal:
                s, t = (a.shape[-2], a.shape[-1])
                mask = (jnp.arange(t)[None, :] > jnp.arange(s)[:, None]).astype(a.dtype)
                a = a * mask
            o = jnp.einsum('bhst,bhtd->bhsd', a, v)
            o = o.transpose(0, 2, 1, 3).reshape(x.shape[0], x.shape[1], H * D)
            x_out = x + o @ li1_w + li1_b
            h = jax.nn.gelu(_ln(x_out, ln3_g, ln3_b) @ li2_w + li2_b, approximate=False)
            return x_out + h @ li3_w + li3_b
        key = jax.random.key(seed)
        ks = iter(jax.random.split(key, 64))

        def w(shape, scale=0.02):
            return jax.random.normal(next(ks), shape, jnp.float32) * scale
        inp = {'xx': jax.random.normal(next(ks), (B, S, C1), jnp.float32), 'ee': jax.random.normal(next(ks), (B, M, C2), jnp.float32), 'ln1_g': jnp.ones(C1, jnp.float32), 'ln1_b': jnp.zeros(C1, jnp.float32), 'ln2_g': jnp.ones(C1, jnp.float32), 'ln2_b': jnp.zeros(C1, jnp.float32)}
        for pfx, cy in (('a1', C1), ('a2', C2)):
            inp[pfx + '_wq'] = w((H, C1, D))
            inp[pfx + '_wk'] = w((H, cy, D))
            inp[pfx + '_wv'] = w((H, cy, D))
            inp[pfx + '_li1_w'] = w((H * D, C1))
            inp[pfx + '_li1_b'] = jnp.zeros(C1, jnp.float32)
            inp[pfx + '_lnx_g'] = jnp.ones(C1, jnp.float32)
            inp[pfx + '_lnx_b'] = jnp.zeros(C1, jnp.float32)
            inp[pfx + '_lny_g'] = jnp.ones(cy, jnp.float32)
            inp[pfx + '_lny_b'] = jnp.zeros(cy, jnp.float32)
            inp[pfx + '_ln3_g'] = jnp.ones(C1, jnp.float32)
            inp[pfx + '_ln3_b'] = jnp.zeros(C1, jnp.float32)
            inp[pfx + '_li2_w'] = w((C1, C1 * W))
            inp[pfx + '_li2_b'] = jnp.zeros(C1 * W, jnp.float32)
            inp[pfx + '_li3_w'] = w((C1 * W, C1))
            inp[pfx + '_li3_b'] = jnp.zeros(C1, jnp.float32)
        inp['training'] = 0
        return inp
    _L1_xattn_all = _L1_xattn_setup()
    _L1_xattn_in = {k: v for k, v in _L1_xattn_all.items() if k in ('ln1_g', 'ln1_b', 'ln2_g', 'ln2_b', 'a1_wq', 'a1_wk', 'a1_wv', 'a1_li1_w', 'a1_li1_b', 'a1_lnx_g', 'a1_lnx_b', 'a1_lny_g', 'a1_lny_b', 'a1_ln3_g', 'a1_ln3_b', 'a1_li2_w', 'a1_li2_b', 'a1_li3_w', 'a1_li3_b', 'a2_wq', 'a2_wk', 'a2_wv', 'a2_li1_w', 'a2_li1_b', 'a2_lnx_g', 'a2_lnx_b', 'a2_lny_g', 'a2_lny_b', 'a2_ln3_g', 'a2_ln3_b', 'a2_li2_w', 'a2_li2_b', 'a2_li3_w', 'a2_li3_b')}
    del _L1_xattn_all

    def _L1_ffn_setup():
        import jax, jax.numpy as jnp
        import numpy as np
        B, N, C, H, REG = (1, 2309, 128, 16, 5)
        D = C // H
        key = jax.random.key(seed)
        k0, k1, k2, k3 = jax.random.split(key, 4)
        x = jax.random.normal(k0, (B, N, C), dtype=jnp.float32)
        g_info = jax.random.normal(k1, (12, 2, C), dtype=jnp.float32)
        W_qkv = jax.random.normal(k2, (C, 3 * C), dtype=jnp.float32) * 0.02
        W_proj = jax.random.normal(k3, (C, C), dtype=jnp.float32) * 0.02
        b_proj = jnp.zeros((C,), dtype=jnp.float32)
        return {'x': x, 'g_info': g_info, 'W_qkv': W_qkv, 'W_proj': W_proj, 'b_proj': b_proj}
    _L1_ffn_all = _L1_ffn_setup()
    _L1_ffn_in = {k: v for k, v in _L1_ffn_all.items() if k in ('g_info', 'W_qkv', 'W_proj', 'b_proj')}
    del _L1_ffn_all
    return {'x': x, 'ctx_512': ctx_512, 'itok_BxS2xS_0_7': itok_BxS2xS_0_7, 'L0_attn_W_dkv': _L0_attn_in['W_dkv'], 'L0_attn_W_uk': _L0_attn_in['W_uk'], 'L0_attn_W_uv': _L0_attn_in['W_uv'], 'L0_attn_W_dq': _L0_attn_in['W_dq'], 'L0_attn_W_uq': _L0_attn_in['W_uq'], 'L0_attn_W_qr': _L0_attn_in['W_qr'], 'L0_attn_W_kr': _L0_attn_in['W_kr'], 'L0_attn_W_out': _L0_attn_in['W_out'], 'L0_attn_idx_wq': _L0_attn_in['idx_wq'], 'L0_attn_idx_wk': _L0_attn_in['idx_wk'], 'L0_attn_idx_w': _L0_attn_in['idx_w'], 'L0_attn_raw_delta': _L0_attn_in['raw_delta'], 'L0_xattn_proj_in': _L0_xattn_in['proj_in'], 'L0_xattn_proj_out': _L0_xattn_in['proj_out'], 'L0_ffn_router_w': _L0_ffn_in['router_w'], 'L0_ffn_router_b': _L0_ffn_in['router_b'], 'L0_ffn_w1': _L0_ffn_in['w1'], 'L0_ffn_b1': _L0_ffn_in['b1'], 'L0_ffn_w2': _L0_ffn_in['w2'], 'L0_ffn_b2': _L0_ffn_in['b2'], 'L1_attn_in_proj_w': _L1_attn_in['in_proj_w'], 'L1_attn_conv_w': _L1_attn_in['conv_w'], 'L1_attn_conv_b': _L1_attn_in['conv_b'], 'L1_attn_x_proj_w': _L1_attn_in['x_proj_w'], 'L1_attn_dt_proj_w': _L1_attn_in['dt_proj_w'], 'L1_attn_dt_proj_b': _L1_attn_in['dt_proj_b'], 'L1_attn_A_log': _L1_attn_in['A_log'], 'L1_attn_D': _L1_attn_in['D'], 'L1_attn_conv_wb': _L1_attn_in['conv_wb'], 'L1_attn_conv_bb': _L1_attn_in['conv_bb'], 'L1_attn_x_proj_wb': _L1_attn_in['x_proj_wb'], 'L1_attn_dt_proj_wb': _L1_attn_in['dt_proj_wb'], 'L1_attn_dt_proj_bb': _L1_attn_in['dt_proj_bb'], 'L1_attn_A_b_log': _L1_attn_in['A_b_log'], 'L1_attn_D_b': _L1_attn_in['D_b'], 'L1_attn_out_proj_w': _L1_attn_in['out_proj_w'], 'L1_xattn_ln1_g': _L1_xattn_in['ln1_g'], 'L1_xattn_ln1_b': _L1_xattn_in['ln1_b'], 'L1_xattn_ln2_g': _L1_xattn_in['ln2_g'], 'L1_xattn_ln2_b': _L1_xattn_in['ln2_b'], 'L1_xattn_a1_wq': _L1_xattn_in['a1_wq'], 'L1_xattn_a1_wk': _L1_xattn_in['a1_wk'], 'L1_xattn_a1_wv': _L1_xattn_in['a1_wv'], 'L1_xattn_a1_li1_w': _L1_xattn_in['a1_li1_w'], 'L1_xattn_a1_li1_b': _L1_xattn_in['a1_li1_b'], 'L1_xattn_a1_lnx_g': _L1_xattn_in['a1_lnx_g'], 'L1_xattn_a1_lnx_b': _L1_xattn_in['a1_lnx_b'], 'L1_xattn_a1_lny_g': _L1_xattn_in['a1_lny_g'], 'L1_xattn_a1_lny_b': _L1_xattn_in['a1_lny_b'], 'L1_xattn_a1_ln3_g': _L1_xattn_in['a1_ln3_g'], 'L1_xattn_a1_ln3_b': _L1_xattn_in['a1_ln3_b'], 'L1_xattn_a1_li2_w': _L1_xattn_in['a1_li2_w'], 'L1_xattn_a1_li2_b': _L1_xattn_in['a1_li2_b'], 'L1_xattn_a1_li3_w': _L1_xattn_in['a1_li3_w'], 'L1_xattn_a1_li3_b': _L1_xattn_in['a1_li3_b'], 'L1_xattn_a2_wq': _L1_xattn_in['a2_wq'], 'L1_xattn_a2_wk': _L1_xattn_in['a2_wk'], 'L1_xattn_a2_wv': _L1_xattn_in['a2_wv'], 'L1_xattn_a2_li1_w': _L1_xattn_in['a2_li1_w'], 'L1_xattn_a2_li1_b': _L1_xattn_in['a2_li1_b'], 'L1_xattn_a2_lnx_g': _L1_xattn_in['a2_lnx_g'], 'L1_xattn_a2_lnx_b': _L1_xattn_in['a2_lnx_b'], 'L1_xattn_a2_lny_g': _L1_xattn_in['a2_lny_g'], 'L1_xattn_a2_lny_b': _L1_xattn_in['a2_lny_b'], 'L1_xattn_a2_ln3_g': _L1_xattn_in['a2_ln3_g'], 'L1_xattn_a2_ln3_b': _L1_xattn_in['a2_ln3_b'], 'L1_xattn_a2_li2_w': _L1_xattn_in['a2_li2_w'], 'L1_xattn_a2_li2_b': _L1_xattn_in['a2_li2_b'], 'L1_xattn_a2_li3_w': _L1_xattn_in['a2_li3_w'], 'L1_xattn_a2_li3_b': _L1_xattn_in['a2_li3_b'], 'L1_ffn_g_info': _L1_ffn_in['g_info'], 'L1_ffn_W_qkv': _L1_ffn_in['W_qkv'], 'L1_ffn_W_proj': _L1_ffn_in['W_proj'], 'L1_ffn_b_proj': _L1_ffn_in['b_proj']}

def reference(x, ctx_512, itok_BxS2xS_0_7, L0_attn_W_dkv, L0_attn_W_uk, L0_attn_W_uv, L0_attn_W_dq, L0_attn_W_uq, L0_attn_W_qr, L0_attn_W_kr, L0_attn_W_out, L0_attn_idx_wq, L0_attn_idx_wk, L0_attn_idx_w, L0_attn_raw_delta, L0_xattn_proj_in, L0_xattn_proj_out, L0_ffn_router_w, L0_ffn_router_b, L0_ffn_w1, L0_ffn_b1, L0_ffn_w2, L0_ffn_b2, L1_attn_in_proj_w, L1_attn_conv_w, L1_attn_conv_b, L1_attn_x_proj_w, L1_attn_dt_proj_w, L1_attn_dt_proj_b, L1_attn_A_log, L1_attn_D, L1_attn_conv_wb, L1_attn_conv_bb, L1_attn_x_proj_wb, L1_attn_dt_proj_wb, L1_attn_dt_proj_bb, L1_attn_A_b_log, L1_attn_D_b, L1_attn_out_proj_w, L1_xattn_ln1_g, L1_xattn_ln1_b, L1_xattn_ln2_g, L1_xattn_ln2_b, L1_xattn_a1_wq, L1_xattn_a1_wk, L1_xattn_a1_wv, L1_xattn_a1_li1_w, L1_xattn_a1_li1_b, L1_xattn_a1_lnx_g, L1_xattn_a1_lnx_b, L1_xattn_a1_lny_g, L1_xattn_a1_lny_b, L1_xattn_a1_ln3_g, L1_xattn_a1_ln3_b, L1_xattn_a1_li2_w, L1_xattn_a1_li2_b, L1_xattn_a1_li3_w, L1_xattn_a1_li3_b, L1_xattn_a2_wq, L1_xattn_a2_wk, L1_xattn_a2_wv, L1_xattn_a2_li1_w, L1_xattn_a2_li1_b, L1_xattn_a2_lnx_g, L1_xattn_a2_lnx_b, L1_xattn_a2_lny_g, L1_xattn_a2_lny_b, L1_xattn_a2_ln3_g, L1_xattn_a2_ln3_b, L1_xattn_a2_li2_w, L1_xattn_a2_li2_b, L1_xattn_a2_li3_w, L1_xattn_a2_li3_b, L1_ffn_g_info, L1_ffn_W_qkv, L1_ffn_W_proj, L1_ffn_b_proj):
    import jax
    import jax.numpy as jnp

    def _L0_attn_ref(x, W_dkv, W_uk, W_uv, W_dq, W_uq, W_qr, W_kr, W_out, idx_wq, idx_wk, idx_w, raw_delta):
        import jax, jax.numpy as jnp
        import numpy as np
        B, L = (2, 128)
        D_MODEL, D_CKV, D_CQ = (128, 32, 64)
        N_HEAD, D_HEAD, D_ROPE = (8, 64, 32)
        N_IDX_HEAD = 4
        K_TS, LW = (96, 64)
        ROPE_BASE = 10000.0

        def _pope(x, angles):
            cos, sin = (jnp.cos(angles), jnp.sin(angles))
            mu1, mu2 = jnp.split(jax.nn.softplus(x), 2, axis=-1)
            return jnp.concatenate([mu1 * cos - mu2 * sin, mu1 * sin + mu2 * cos], axis=-1)

        def _forward(x, W_dkv, W_uk, W_uv, W_dq, W_uq, W_qr, W_kr, W_out, idx_wq, idx_wk, idx_w, raw_delta):
            B_, L_, _ = x.shape
            c_kv = x @ W_dkv
            q_i = (x @ idx_wq).reshape(B_, L_, N_IDX_HEAD, D_HEAD)
            k_i = x @ idx_wk
            s_i = jax.nn.relu(jnp.einsum('bthd,bsd->bths', q_i, k_i))
            I = jnp.einsum('bths,h->bts', s_i, idx_w)
            qpos = jnp.arange(L_)[:, None]
            kpos = jnp.arange(L_)[None, :]
            local = (kpos >= qpos - LW + 1) & (kpos <= qpos)
            causal = kpos > qpos
            I = jnp.where(local[None], jnp.inf, I)
            I = jnp.where(causal[None], -jnp.inf, I)
            kk = min(K_TS, L_)
            _, idx = jax.lax.top_k(I, kk)
            bi = jnp.arange(B_)[:, None, None]
            key_c = (c_kv @ W_uk)[bi, idx].reshape(B_, L_, kk, N_HEAD, D_HEAD)
            value = (c_kv @ W_uv)[bi, idx].reshape(B_, L_, kk, N_HEAD, D_HEAD)
            c_q = x @ W_dq
            query_c = (c_q @ W_uq).reshape(B_, L_, N_HEAD, D_HEAD)
            half = D_ROPE // 2
            theta = 1.0 / ROPE_BASE ** (2.0 * jnp.arange(half, dtype=jnp.float32) / D_ROPE)
            delta = -2.0 * jnp.pi * jax.nn.sigmoid(raw_delta)
            angles_q = jnp.arange(L_, dtype=jnp.float32)[:, None] * theta[None, :] + delta
            query_r = _pope((c_q @ W_qr).reshape(B_, L_, N_HEAD, D_ROPE), angles_q[None, :, None, :])
            kr_sel = (x @ W_kr)[bi, idx]
            angles_k = jnp.arange(kk, dtype=jnp.float32)[:, None] * theta[None, :] + delta
            key_r = _pope(kr_sel, angles_k[None, None, :, :])
            scale = (D_HEAD + D_ROPE) ** (-0.5)
            q_c = query_c.transpose(0, 2, 1, 3)
            q_r = query_r.transpose(0, 2, 1, 3)
            k_c = key_c.transpose(0, 3, 1, 2, 4)
            v = value.transpose(0, 3, 1, 2, 4)
            scores = (jnp.einsum('bhld,bhlkd->bhlk', q_c, k_c) + jnp.einsum('bhld,blkd->bhlk', q_r, key_r)) * scale
            attn = jax.nn.softmax(scores.astype(jnp.float32), axis=-1).astype(v.dtype)
            out = jnp.einsum('bhlk,bhlkd->bhld', attn, v)
            out = out.transpose(0, 2, 1, 3).reshape(B_, L_, N_HEAD * D_HEAD)
            return out @ W_out
        return _forward(x, W_dkv, W_uk, W_uv, W_dq, W_uq, W_qr, W_kr, W_out, idx_wq, idx_wk, idx_w, raw_delta)

    def _L0_xattn_ref(x, weights, ensembles, proj_in, proj_out):
        import jax, jax.numpy as jnp
        import numpy as np
        E = proj_in.shape[0]
        h = jax.nn.relu(jnp.einsum('edi,bsi->bsed', proj_in, x))
        o = jnp.einsum('eid,bsed->bsei', proj_out, h)
        onehot = jax.nn.one_hot(ensembles, E, dtype=x.dtype)
        gate = jnp.einsum('bks,bkse->bse', weights, onehot)
        return jnp.einsum('bsei,bse->bsi', o, gate)

    def _L0_ffn_ref(x, router_w, router_b, w1, b1, w2, b2):
        import jax, jax.numpy as jnp
        import numpy as np
        DIM = 128
        HIDDEN = 512
        N_EXPERTS = 8
        K = 2
        TEMP = 1.0

        def _expert_ffn(xf, wa, ba, wb, bb):
            h = xf @ wa.T + ba
            h1, h2 = jnp.split(h, 2, axis=-1)
            h = jax.nn.silu(h1) * h2
            return h @ wb.T + bb
        b, t, d = x.shape
        logits = (x @ router_w.T + router_b) / TEMP
        topk_val, topk_idx = jax.lax.top_k(logits, K)
        weights = jax.nn.softmax(topk_val, axis=-1)
        xf = x.reshape(-1, d)
        outs = jax.vmap(_expert_ffn, in_axes=(None, 0, 0, 0, 0))(xf, w1, b1, w2, b2)
        outs = jnp.transpose(outs, (1, 0, 2))
        idx = topk_idx.reshape(-1, K)
        gathered = jnp.take_along_axis(outs, idx[:, :, None], axis=1)
        combined = (gathered * weights.reshape(-1, K, 1)).sum(axis=1)
        return combined.reshape(b, t, d)

    def _L1_attn_ref(hidden_states, in_proj_w, conv_w, conv_b, x_proj_w, dt_proj_w, dt_proj_b, A_log, D, conv_wb, conv_bb, x_proj_wb, dt_proj_wb, dt_proj_bb, A_b_log, D_b, out_proj_w):
        import jax, jax.numpy as jnp
        import numpy as np
        import math
        B = 2
        L = 256
        D_MODEL = 128
        D_STATE = 16
        D_CONV = 4
        D_INNER = 2 * D_MODEL
        DT_RANK = math.ceil(D_MODEL / 16)
        DT_MIN, DT_MAX = (0.001, 0.1)

        def _dt_bias(k):
            dt = jnp.exp(jax.random.uniform(k, (D_INNER,)) * (math.log(DT_MAX) - math.log(DT_MIN)) + math.log(DT_MIN))
            dt = jnp.clip(dt, 0.0001, None)
            return (dt + jnp.log(-jnp.expm1(-dt))).astype(jnp.float32)

        def _causal_conv(x, w, b):
            out = jax.lax.conv_general_dilated(x, w[:, None, :], (1,), [(D_CONV - 1, 0)], dimension_numbers=('NCH', 'OIH', 'NCH'), feature_group_count=D_INNER)
            return out + b[None, :, None]

        def _selective_scan(u, dt, A, Bm, Cm, Dp, z):
            h0 = jnp.zeros((u.shape[0], u.shape[1], A.shape[1]), u.dtype)

            def step(h, inp):
                dt_l, u_l, B_l, C_l = inp
                h = jnp.exp(dt_l[..., None] * A) * h + (dt_l * u_l)[..., None] * B_l[:, None, :]
                return (h, jnp.einsum('bdn,bn->bd', h, C_l))
            xs = tuple((jnp.moveaxis(a, -1, 0) for a in (dt, u, Bm, Cm)))
            _, ys = jax.lax.scan(step, h0, xs)
            y = jnp.moveaxis(ys, 0, -1) + Dp[None, :, None] * u
            return y * jax.nn.silu(z)

        def _mamba_dir(xz, conv_w, conv_b, x_proj_w, dt_proj_w, dt_proj_b, A_log, Dp):
            x, z = jnp.split(xz, 2, axis=1)
            x = jax.nn.silu(_causal_conv(x, conv_w, conv_b))
            x_dbl = jnp.einsum('bdl,ed->bel', x, x_proj_w)
            dtv = x_dbl[:, :DT_RANK]
            Bm = x_dbl[:, DT_RANK:DT_RANK + D_STATE]
            Cm = x_dbl[:, DT_RANK + D_STATE:]
            dtv = jax.nn.softplus(jnp.einsum('brl,dr->bdl', dtv, dt_proj_w) + dt_proj_b[None, :, None])
            return _selective_scan(x, dtv, -jnp.exp(A_log), Bm, Cm, Dp, z)
        xz = jnp.einsum('bld,ed->bel', hidden_states, in_proj_w)
        out_f = _mamba_dir(xz, conv_w, conv_b, x_proj_w, dt_proj_w, dt_proj_b, A_log, D)
        out_b = _mamba_dir(xz[..., ::-1], conv_wb, conv_bb, x_proj_wb, dt_proj_wb, dt_proj_bb, A_b_log, D_b)
        y = out_f + out_b[..., ::-1]
        return jnp.einsum('bdl,od->blo', y, out_proj_w)

    def _L1_xattn_ref(xx, ee, ln1_g, ln1_b, ln2_g, ln2_b, a1_wq, a1_wk, a1_wv, a1_li1_w, a1_li1_b, a1_lnx_g, a1_lnx_b, a1_lny_g, a1_lny_b, a1_ln3_g, a1_ln3_b, a1_li2_w, a1_li2_b, a1_li3_w, a1_li3_b, a2_wq, a2_wk, a2_wv, a2_li1_w, a2_li1_b, a2_lnx_g, a2_lnx_b, a2_lny_g, a2_lny_b, a2_ln3_g, a2_ln3_b, a2_li2_w, a2_li2_b, a2_li3_w, a2_li3_b, training):
        import jax, jax.numpy as jnp
        import numpy as np
        H, D, C1, C2, S, M, B, W = (16, 32, 128, 64, 256, 64, 2, 4)

        def _ln(x, g, b):
            m = jnp.mean(x, -1, keepdims=True)
            v = jnp.var(x, -1, keepdims=True)
            return (x - m) * jax.lax.rsqrt(v + 1e-05) * g + b

        def _mha(x, y, wq, wk, wv, li1_w, li1_b, lnx_g, lnx_b, lny_g, lny_b, ln3_g, ln3_b, li2_w, li2_b, li3_w, li3_b, causal):
            xn = _ln(x, lnx_g, lnx_b)
            yn = _ln(y, lny_g, lny_b)
            q = jnp.einsum('bsc,hcd->bhsd', xn, wq)
            k = jnp.einsum('btc,hcd->bhtd', yn, wk)
            v = jnp.einsum('btc,hcd->bhtd', yn, wv)
            a = jax.nn.softmax(jnp.einsum('bhsd,bhtd->bhst', q, k) * D ** (-0.5), axis=-1)
            if causal:
                s, t = (a.shape[-2], a.shape[-1])
                mask = (jnp.arange(t)[None, :] > jnp.arange(s)[:, None]).astype(a.dtype)
                a = a * mask
            o = jnp.einsum('bhst,bhtd->bhsd', a, v)
            o = o.transpose(0, 2, 1, 3).reshape(x.shape[0], x.shape[1], H * D)
            x_out = x + o @ li1_w + li1_b
            h = jax.nn.gelu(_ln(x_out, ln3_g, ln3_b) @ li2_w + li2_b, approximate=False)
            return x_out + h @ li3_w + li3_b
        x = _ln(xx, ln1_g, ln1_b)
        x = x + _mha(x, x, a1_wq, a1_wk, a1_wv, a1_li1_w, a1_li1_b, a1_lnx_g, a1_lnx_b, a1_lny_g, a1_lny_b, a1_ln3_g, a1_ln3_b, a1_li2_w, a1_li2_b, a1_li3_w, a1_li3_b, causal=True)
        x = _ln(x, ln2_g, ln2_b)
        return x + _mha(x, ee, a2_wq, a2_wk, a2_wv, a2_li1_w, a2_li1_b, a2_lnx_g, a2_lnx_b, a2_lny_g, a2_lny_b, a2_ln3_g, a2_ln3_b, a2_li2_w, a2_li2_b, a2_li3_w, a2_li3_b, causal=False)

    def _L1_ffn_ref(x, g_info, W_qkv, W_proj, b_proj):
        import jax, jax.numpy as jnp
        import numpy as np
        B, N, C, H, REG = (1, 2309, 128, 16, 5)
        D = C // H
        Bx, Nx, Cx = x.shape
        scale = D ** (-0.5)
        qkv = (x @ W_qkv).reshape(Bx, Nx, 3, H, D)
        q, k, v = (qkv[:, :, 0], qkv[:, :, 1], qkv[:, :, 2])
        g_layer = g_info[0].reshape(-1, H, D)
        q_g = g_layer[0]
        q_pure = q[:, REG:]
        q_n = q_pure / jnp.linalg.norm(q_pure, axis=-1, keepdims=True)
        qg_n = q_g / jnp.linalg.norm(q_g, axis=-1, keepdims=True)
        sim = (qg_n[None, None] * q_n).sum(-1).mean(-1)
        sim = (sim - sim.min()) / (sim.max() - sim.min())
        pos = sim > 0.9
        logits = jnp.einsum('bqhd,bkhd->bhqk', q * scale, k)

        def masked_attn(tok_mask):
            key_mask = jnp.concatenate([jnp.ones((Bx, REG), bool), tok_mask], axis=1)
            l = jnp.where(key_mask[:, None, None, :], logits, -jnp.inf)
            a = jax.nn.softmax(l, axis=-1)
            return jnp.einsum('bhqk,bkhd->bqhd', a, v)
        x_pos = masked_attn(pos)
        x_neg = masked_attn(~pos)
        reg_out = (x_pos[:, :REG] + x_neg[:, :REG]) * 0.5
        tok_out = jnp.where(pos[:, :, None, None], x_pos[:, REG:], x_neg[:, REG:])
        out = jnp.concatenate([reg_out, tok_out], axis=1).reshape(Bx, Nx, Cx)
        return out @ W_proj + b_proj
    x = _layernorm(x + _L0_attn_ref(x, L0_attn_W_dkv, L0_attn_W_uk, L0_attn_W_uv, L0_attn_W_dq, L0_attn_W_uq, L0_attn_W_qr, L0_attn_W_kr, L0_attn_W_out, L0_attn_idx_wq, L0_attn_idx_wk, L0_attn_idx_w, L0_attn_raw_delta), axis=-1)
    x = _layernorm(x + _L0_xattn_ref(x, ctx_512, itok_BxS2xS_0_7, L0_xattn_proj_in, L0_xattn_proj_out), axis=-1)
    x = _layernorm(x + _L0_ffn_ref(x, L0_ffn_router_w, L0_ffn_router_b, L0_ffn_w1, L0_ffn_b1, L0_ffn_w2, L0_ffn_b2), axis=-1)
    x = _layernorm(x + _L1_attn_ref(x, L1_attn_in_proj_w, L1_attn_conv_w, L1_attn_conv_b, L1_attn_x_proj_w, L1_attn_dt_proj_w, L1_attn_dt_proj_b, L1_attn_A_log, L1_attn_D, L1_attn_conv_wb, L1_attn_conv_bb, L1_attn_x_proj_wb, L1_attn_dt_proj_wb, L1_attn_dt_proj_bb, L1_attn_A_b_log, L1_attn_D_b, L1_attn_out_proj_w), axis=-1)
    x = _layernorm(x + _L1_xattn_ref(x, ctx_512, L1_xattn_ln1_g, L1_xattn_ln1_b, L1_xattn_ln2_g, L1_xattn_ln2_b, L1_xattn_a1_wq, L1_xattn_a1_wk, L1_xattn_a1_wv, L1_xattn_a1_li1_w, L1_xattn_a1_li1_b, L1_xattn_a1_lnx_g, L1_xattn_a1_lnx_b, L1_xattn_a1_lny_g, L1_xattn_a1_lny_b, L1_xattn_a1_ln3_g, L1_xattn_a1_ln3_b, L1_xattn_a1_li2_w, L1_xattn_a1_li2_b, L1_xattn_a1_li3_w, L1_xattn_a1_li3_b, L1_xattn_a2_wq, L1_xattn_a2_wk, L1_xattn_a2_wv, L1_xattn_a2_li1_w, L1_xattn_a2_li1_b, L1_xattn_a2_lnx_g, L1_xattn_a2_lnx_b, L1_xattn_a2_lny_g, L1_xattn_a2_lny_b, L1_xattn_a2_ln3_g, L1_xattn_a2_ln3_b, L1_xattn_a2_li2_w, L1_xattn_a2_li2_b, L1_xattn_a2_li3_w, L1_xattn_a2_li3_b, 0), axis=-1)
    x = _layernorm(x + _L1_ffn_ref(x, L1_ffn_g_info, L1_ffn_W_qkv, L1_ffn_W_proj, L1_ffn_b_proj), axis=-1)
    return x

_drawn_inputs = setup_inputs


def setup_inputs(seed=0):
    import zlib

    import numpy as np

    out = dict(_drawn_inputs(seed))
    spreads = {'L0_attn_idx_w': (1.0, 0.2),
     'L0_ffn_router_b': (0.0, 0.1),
     'L0_ffn_b1': (0.0, 0.8),
     'L0_ffn_b2': (0.0, 0.1),
     'L1_attn_D': (1.0, 0.2),
     'L1_attn_D_b': (1.0, 0.2),
     'L1_xattn_ln1_g': (1.0, 0.2),
     'L1_xattn_ln1_b': (0.0, 0.1),
     'L1_xattn_ln2_g': (1.0, 0.2),
     'L1_xattn_ln2_b': (0.0, 0.1),
     'L1_xattn_a1_li1_b': (0.0, 0.362),
     'L1_xattn_a1_lnx_g': (1.0, 0.6),
     'L1_xattn_a1_lnx_b': (0.0, 0.8),
     'L1_xattn_a1_lny_g': (1.0, 0.6),
     'L1_xattn_a1_lny_b': (0.0, 0.8),
     'L1_xattn_a1_ln3_g': (1.0, 0.6),
     'L1_xattn_a1_ln3_b': (0.0, 0.8),
     'L1_xattn_a1_li2_b': (0.0, 0.8),
     'L1_xattn_a1_li3_b': (0.0, 0.387),
     'L1_xattn_a2_li1_b': (0.0, 0.301),
     'L1_xattn_a2_lnx_g': (1.0, 0.6),
     'L1_xattn_a2_lnx_b': (0.0, 0.8),
     'L1_xattn_a2_lny_g': (1.0, 0.6),
     'L1_xattn_a2_lny_b': (0.0, 0.8),
     'L1_xattn_a2_ln3_g': (1.0, 0.6),
     'L1_xattn_a2_ln3_b': (0.0, 0.8),
     'L1_xattn_a2_li2_b': (0.0, 0.8),
     'L1_xattn_a2_li3_b': (0.0, 0.295),
     'L1_ffn_b_proj': (0.0, 0.1)}
    factors = {'L0_attn_raw_delta': 64.0,
     'L0_ffn_w1': 5.08,
     'L0_ffn_w2': 4.941,
     'L1_attn_dt_proj_w': 3.337,
     'L1_attn_dt_proj_wb': 8.0,
     'L1_attn_dt_proj_bb': 3.299,
     'L1_attn_A_b_log': 3.388,
     'L1_xattn_a1_wq': 8.0,
     'L1_xattn_a1_wk': 8.0,
     'L1_xattn_a1_wv': 5.57,
     'L1_xattn_a1_li1_w': 5.837,
     'L1_xattn_a1_li2_w': 3.107,
     'L1_xattn_a1_li3_w': 2.82,
     'L1_xattn_a2_wq': 8.0,
     'L1_xattn_a2_wk': 8.0,
     'L1_xattn_a2_wv': 4.088,
     'L1_xattn_a2_li1_w': 4.095,
     'L1_xattn_a2_li2_w': 3.1,
     'L1_xattn_a2_li3_w': 2.971,
     'L1_ffn_g_info': 64.0}
    for name, (base, spread) in spreads.items():
        noise = np.random.default_rng([zlib.crc32(name.encode()), seed]).standard_normal(out[name].shape)
        drawn = base * np.exp(spread * noise) if base else spread * noise
        out[name] = jnp.asarray(drawn.astype(out[name].dtype))
    for name, factor in factors.items():
        out[name] = (out[name] * factor).astype(out[name].dtype)
    return out
```

```python
from contextlib import ExitStack, contextmanager

import numpy as np

import concourse.bass as bass
from concourse import mybir

F32 = mybir.dt.float32
BF16 = mybir.dt.bfloat16
I32 = mybir.dt.int32
ALU = mybir.AluOpType
ACT = mybir.ActivationFunctionType
AX = mybir.AxisListType.X

P = 128
SEQ = 64
NSEQ = 32
TOK = SEQ * NSEQ
CH = 512
NCH = TOK // CH
BCH = CH // SEQ
PAIR = 2 * SEQ
NPAIR = CH // PAIR
BIG = float(2.0 ** 100)
EXPERTS = 8
STATE = 16
REG = 5


def rope_tables():
    half = 16
    theta = (np.float32(1.0) / np.float32(10000.0) ** (np.float32(2.0) * np.arange(half, dtype=np.float32) / np.float32(32.0)))
    a = (np.arange(SEQ, dtype=np.float32)[None, :] * theta.astype(np.float32)[:, None]).astype(np.float64)
    c, s = np.cos(a), np.sin(a)
    return np.concatenate([c, c, -s, s]).astype(np.float32), np.concatenate([-s, -s, -c, c]).astype(np.float32)


def constants():
    p = np.arange(P)
    u, w = rope_tables()
    eye = np.eye(P, dtype=np.float32)
    row = np.zeros((2, P), np.float32)
    row[0, p % 32 == 8] = 1
    row[1, p % 32 == 9] = 1
    two = lambda a, b: np.array([[a], [b]], np.float32)
    return {
        "ident": eye,
        "center": eye - np.float32(1 / P),
        "mean": np.full((P, P), 1 / P, np.float32),
        "center64": np.eye(64, dtype=np.float32) - np.float32(1 / 64),
        "mean64": np.full((64, 64), 1 / 64, np.float32),
        "later": (np.arange(SEQ)[None, :] > (p % SEQ)[:, None]).astype(np.float32),
        "ropeU": u, "ropeW": w,
        "ones": np.ones((P, P), np.float32),
        "fold": (np.arange(96)[:, None] % 32 == np.arange(32)[None, :]).astype(np.float32),
        "fold64": (np.arange(64)[:, None] % 32 == np.arange(64)[None, :] % 32).astype(np.float32),
        "heads8": (p[:, None] // 8 == p[None, :] // 8).astype(np.float32),
        "maskrow": row,
        "negclass": np.where(p % 32 == 8, BIG, np.where(p % 32 == 9, -BIG, 0)).astype(np.float32)[:, None],
        "regscale": np.where(p % SEQ < REG, 0.5, 1.0).astype(np.float32)[:, None],
        "prio": np.broadcast_to(EXPERTS - np.arange(EXPERTS, dtype=np.float32), (P, EXPERTS)),
        "eps": np.full((P, 1), 1e-5, np.float32),
        "qa": two(-BIG, BIG), "qc": two(0, -BIG), "ka": two(-1, 1), "kc": two(1, 0),
    }


def tiles(w):
    return w.reshape(-1, P, w.shape[-1]).transpose(1, 0, 2)


def attn0_parts(a):
    uq = a["L0_attn_W_uq"].reshape(64, 8, 64)
    qr = a["L0_attn_W_qr"].reshape(64, 8, 2, 16)
    kr = a["L0_attn_W_kr"].reshape(P, 2, 16)
    order = [0, 1, 1, 0]
    return {
        "wdq": a["L0_attn_W_dq"],
        "wkv": np.concatenate([kr[:, order].reshape(P, 64), a["L0_attn_W_dkv"]], 1),
        "qr4": qr[:, :, order].reshape(64, 8, 64),
        "uqT": uq.transpose(2, 1, 0),
        "ukT": a["L0_attn_W_uk"].reshape(32, 8, 64).transpose(2, 1, 0),
        "uvT": a["L0_attn_W_uv"].reshape(32, 8, 64).transpose(2, 1, 0),
        "wo": a["L0_attn_W_out"].reshape(8, 64, P).transpose(1, 0, 2),
        "delta": np.concatenate([a["L0_attn_raw_delta"]] * 4)[:, None],
    }


def moe_parts(a):
    return {
        "pin": a["L0_xattn_proj_in"].reshape(EXPERTS * 256, P).T,
        "pout": a["L0_xattn_proj_out"].reshape(EXPERTS, P, 2, P).transpose(3, 0, 2, 1),
    }


def ffn_parts(a):
    return {
        "router": a["L0_ffn_router_w"].T,
        "router_b": np.broadcast_to(a["L0_ffn_router_b"], (P, EXPERTS)),
        "b1": a["L0_ffn_b1"].reshape(EXPERTS, 8, P).transpose(2, 0, 1),
        "b2": a["L0_ffn_b2"].T,
        "w1": a["L0_ffn_w1"].reshape(EXPERTS * 1024, P).T,
        "w2": a["L0_ffn_w2"].reshape(EXPERTS, P, 4, P).transpose(3, 0, 2, 1),
    }


def mamba_parts(a):
    out = {"inT": a["L1_attn_in_proj_w"].T,
           "outT": a["L1_attn_out_proj_w"].reshape(P, 2, P).transpose(2, 1, 0)}
    for d, (s, al, dp) in enumerate((("", "A_log", "D"), ("b", "A_b_log", "D_b"))):
        xp = a[f"L1_attn_x_proj_w{s}"]
        bc = xp[8:40]
        out[f"xproj{d}"] = np.concatenate([bc, bc, bc, xp[0:8]]).T.reshape(2, P, 104).transpose(1, 0, 2)
        dt = np.zeros((104, 256), np.float32)
        dt[96:104] = a[f"L1_attn_dt_proj_w{s}"].T
        out[f"dtw{d}"] = dt
        out[f"dtb{d}"] = a[f"L1_attn_dt_proj_b{s}"].reshape(2, P).T
        out[f"convw{d}"] = tiles(a[f"L1_attn_conv_w{s}"])
        out[f"convb{d}"] = a[f"L1_attn_conv_b{s}"].reshape(2, P).T
        out[f"alog{d}"] = tiles(a["L1_attn_" + al])
        out[f"dskip{d}"] = a["L1_attn_" + dp].reshape(2, P).T
    return out


def cross_parts(a):
    x = lambda n: a["L1_xattn_" + n]
    col = lambda n: x(n)[:, None]
    out = {"ln1_g": col("ln1_g"), "ln1_b": col("ln1_b"), "ln2_g": col("ln2_g"), "ln2_b": col("ln2_b")}
    for m in ("a1_", "a2_"):
        for n in ("wq", "wk", "wv"):
            w = x(m + n)
            out[m + n] = w.transpose(1, 0, 2).reshape(w.shape[1], 512)
        out[m + "li1"] = tiles(x(m + "li1_w"))
        out[m + "li2"] = x(m + "li2_w")
        out[m + "li3"] = tiles(x(m + "li3_w"))
        out[m + "li2_b"] = x(m + "li2_b").reshape(4, P).T
        for n in ("li1_b", "li3_b", "lnx_g", "lnx_b", "lny_g", "lny_b", "ln3_g", "ln3_b"):
            out[m + n] = col(m + n)
    return out


def last_parts(a):
    w = a["L1_ffn_W_qkv"].reshape(P, 3, 16, 8)
    wide = np.zeros((P, 3, 16, 32), np.float32)
    wide[..., :8] = w
    proj = np.zeros((16, 32, P), np.float32)
    proj[:, :8] = a["L1_ffn_W_proj"].reshape(16, 8, P)
    return {
        "qnat": w[:, 0].reshape(P, P),
        "qg": a["L1_ffn_g_info"][0, 0][:, None],
        "wide": wide.reshape(P, 3, 512),
        "proj": tiles(proj.reshape(512, P)),
        "projb": a["L1_ffn_b_proj"][:, None],
    }


PACKS = [("const", lambda a: constants()), ("attn0", attn0_parts), ("moe", moe_parts), ("ffn", ffn_parts),
         ("mamba", mamba_parts), ("cross", cross_parts), ("last", last_parts)]


def pack(parts):
    where, at = {}, 0
    for name, a in parts.items():
        n = int(np.prod(a.shape[1:]))
        where[name] = (a.shape[0], at, tuple(a.shape[1:]))
        at += n
    whole = np.zeros((P, at), np.float32)
    for name, a in parts.items():
        rows, c, shape = where[name]
        whole[:rows, c:c + int(np.prod(shape))] = a.reshape(rows, -1)
    return whole, where


class Core:

    def __init__(self, nc, ctx):
        self.nc, self.ctx, self.sems, self.w = nc, ctx, [], {}

    def keep(self, name, shape, dt=F32):
        return self.ctx.enter_context(self.nc.sbuf_tensor(name, shape, dt))

    def sem(self, name):
        s = self.stage_ctx.enter_context(self.nc.semaphore(name))
        self.sems.append(s)
        return s

    @contextmanager
    def stage(self):
        with ExitStack() as self.stage_ctx:
            self.sems = []
            yield
            nums = sorted(s.num for s in self.sems)
            runs = [n for n in nums if n - 1 not in nums], [n for n in nums if n + 1 not in nums]
            for a, b in zip(*runs):
                self.nc.gpsimd.sem_clear(range(a, b + 1))
            self.nc.all_engine_barrier()


class Count:

    def __init__(self, eng, sem):
        self.eng, self.sem, self.n = eng, sem, 0

    def __call__(self, ins):
        self.n += 1
        ins.then_inc(self.sem, 1)
        self.eng.wait_ge(self.sem, self.n)


def groups(ap, k=SEQ):
    return ap.rearrange("p (g k) -> p g k", k=k)


def spread(ap, n):
    return ap.unsqueeze(2).to_broadcast([ap.shape[0], ap.shape[1], n])


def layer_norm(k, tag, outs, src=None, total=None, rows=P, halves=2):
    nc, w = k.nc, k.w
    center, mean = (w["center"], w["mean"]) if rows == P else (w["center64"], w["mean64"])
    n = CH // halves
    summed, centered, squared, meaned, rooted, chain = (k.sem(f"{tag}_{s}") for s in (
        "summed", "centered", "squared", "meaned", "rooted", "chain"))
    with ExitStack() as ctx:
        sq = ctx.enter_context(nc.sbuf_tensor(f"{tag}_sq", [rows, CH], F32))
        rstd = ctx.enter_context(nc.sbuf_tensor(f"{tag}_rstd", [rows, CH], F32))
        tmp = ctx.enter_context(nc.sbuf_tensor(f"{tag}_tmp", [rows, CH], F32))
        z = total["z"] if total else src
        block = ctx.enter_context(nc.Block())
        cut = lambda t, h: t[0:rows, h * n:(h + 1) * n]
        cps = lambda h: k.ps[h][0:rows, 0:n]
        vps = lambda h: k.ps[2 + h][0:rows, 0:n]

        @block.tensor
        def _(pe):
            for h in range(halves):
                if total:
                    pe.wait_ge(summed, h + 1)
                nc.tensor.matmul(cps(h), center[0:rows], cut(z, h), start=True, stop=True).then_inc(centered, 1)
            for h in range(halves):
                pe.wait_ge(squared, h + 1)
                nc.tensor.matmul(vps(h), mean[0:rows], cut(sq, h), start=True, stop=True).then_inc(meaned, 1)

        @block.scalar
        def _(act):
            for h in range(halves):
                act.wait_ge(centered, h + 1)
                nc.scalar.activation(cut(sq, h), cps(h), ACT.Square).then_inc(squared, 1)
            for h in range(halves):
                act.wait_ge(meaned, h + 1)
                nc.scalar.activation(cut(rstd, h), vps(h), ACT.Ln, bias=w["eps"][0:rows]).then_inc(rooted, 1)
                act.wait_ge(rooted, 2 * h + 1)
                nc.scalar.activation(cut(rstd, h), cut(rstd, h), ACT.Exp, scale=-0.5).then_inc(rooted, 1)

        @block.vector
        def _(dve):
            link = Count(dve, chain)
            for h in range(halves if total else 0):
                parts = total["parts"]
                for i, part in enumerate(parts):
                    dst = cut(z, h)
                    first = cut(total["psum"], h) if i == 0 else dst
                    if i == 0 and total.get("bias") is not None:
                        ins = nc.vector.scalar_tensor_tensor(dst, first, total["bias"], cut(part, h), ALU.add, ALU.add)
                    else:
                        ins = nc.vector.tensor_tensor(dst, first, cut(part, h), ALU.add)
                    if i + 1 < len(parts):
                        link(ins)
                ins.then_inc(summed, 1)
            for h in range(halves):
                dve.wait_ge(rooted, 2 * h + 2)
                for dst, gain, shift in outs:
                    if gain is None:
                        nc.vector.tensor_tensor(cut(dst, h), cps(h), cut(rstd, h), ALU.mult)
                    else:
                        link(nc.vector.scalar_tensor_tensor(cut(tmp, h), cps(h), gain, cut(rstd, h), ALU.mult, ALU.mult))
                        link(nc.vector.tensor_scalar(cut(dst, h), cut(tmp, h), shift, None, ALU.add))


def attention(k, tag, q, key, v, scale, narrow, out, masked=False, regs=None):
    nc, w = k.nc, k.w
    G = 8 if narrow else 16
    NX = 2 if regs is not None else 0
    NT = 2 if narrow else 4
    scored, lowered, expd, maskd, normed, turned, turned_sb, mixed, mixed_sb, chain = (k.sem(f"{tag}_{s}") for s in (
        "scored", "lowered", "expd", "maskd", "normed", "turned", "turned_sb", "mixed", "mixed_sb", "chain"))
    with ExitStack() as ctx:
        sb = lambda n, s: ctx.enter_context(nc.sbuf_tensor(f"{tag}_{n}", s, F32))
        prob = sb("prob", [P, 2, (G + NX) * SEQ])
        kept = sb("kept", [P, 2, G * SEQ]) if masked else prob
        probT = sb("probT", [P, 2, (G + NX) * SEQ])
        top = sb("top", [P, 2, G + NX])
        whole = sb("whole", [P, 2, G + NX])
        block = ctx.enter_context(nc.Block())

        def score_views(p):
            if narrow:
                return [(groups(k.ps[p % 2][:, 0:512]), 0)]
            views = [(k.ps_all[:, 0:4, 0:256].rearrange("p n (g k) -> p n g k", k=SEQ), 0)]
            if NX:
                views.append((groups(k.ps[0][:, 256:256 + NX * SEQ]), G))
            return views

        def turn_bank(p, c):
            if narrow:
                return k.ps[2 + p % 2][:, c * P:(c + 1) * P]
            if c == 8:
                return k.ps[1][:, 256:384]
            return k.ps[4 + c // 4][:, c % 4 * P:(c % 4 + 1) * P]

        def mix(p, b):
            base = (4 if narrow else 6) + b
            n = NT * SEQ
            return k.ps[base][:, p % 2 * n:(p % 2 + 1) * n].rearrange("p (t q) -> p t q", t=NT)

        @block.tensor
        def _(pe):
            def score(p):
                if narrow and p >= 2:
                    pe.wait_ge(lowered, p - 1)
                if not narrow and p >= 1:
                    pe.wait_ge(lowered, p)
                for b in range(2):
                    tok = slice(p * PAIR + b * SEQ, p * PAIR + (b + 1) * SEQ)
                    if narrow:
                        for hp in range(4):
                            ins = nc.tensor.matmul(k.ps[p % 2][:, hp * P + b * SEQ:hp * P + (b + 1) * SEQ],
                                                   q[:, hp, 2 * p + b].rearrange("r h q -> r (h q)"), key[:, tok], start=True, stop=True)
                        continue
                    for t in range(4):
                        for j in range(4):
                            at = (t // 2) * P + b * SEQ
                            ins = nc.tensor.matmul(k.ps[j][t % 2 * 64:t % 2 * 64 + 64, at:at + SEQ],
                                                   q[32 * j:32 * j + 32, t, tok], key[32 * j:32 * j + 32, t, tok],
                                                   start=True, stop=True)
                        if NX:
                            ins = nc.tensor.matmul(k.ps[0][32 * t:32 * t + 32, 256 + b * SEQ:256 + (b + 1) * SEQ],
                                                   regs[:, t, 2 * p + b, :], key[:, t, tok], start=True, stop=True)
                ins.then_inc(scored, 1)

            score(0)
            for p in range(NPAIR):
                if p + 1 < NPAIR:
                    score(p + 1)
                pe.wait_ge(normed, p + 1)
                if p >= (2 if narrow else 1):
                    pe.wait_ge(turned_sb, p - 1 if narrow else p)
                for c in range((G + NX) // 2):
                    src = prob if c >= G // 2 else kept
                    ins = nc.tensor.transpose(turn_bank(p, c), src[:, p % 2, c * P:(c + 1) * P], w["ident"])
                ins.then_inc(turned, 1)
                pe.wait_ge(turned_sb, p + 1)
                if p >= 2:
                    pe.wait_ge(mixed_sb, p - 1)
                for b in range(2):
                    rows = slice(b * SEQ, (b + 1) * SEQ)
                    for t in range(NT):
                        for j in range(4):
                            h = 4 * t + j
                            if narrow:
                                vh, c, half = v[rows, p, :], h // 2, h % 2
                            else:
                                vh, c, half = v[rows, p, 32 * h:32 * h + 32], 2 * j + t // 2, t % 2
                            at = c * P + half * SEQ
                            o = mix(p, b)[32 * j:32 * j + 32, t, :]
                            ins = nc.tensor.matmul(o, vh, probT[rows, p % 2, at:at + SEQ], start=True, stop=not NX,
                                                   tile_position=(b * SEQ, 32 * j))
                            if NX:
                                at = 8 * P + 32 * t + REG * j
                                ins = nc.tensor.matmul(o[:, 0:REG], vh, probT[rows, p % 2, at:at + REG], start=False,
                                                       stop=True, tile_position=(b * SEQ, 32 * j))
                ins.then_inc(mixed, 1)

        @block.vector
        def _(dve):
            link = Count(dve, chain)

            def lower(p):
                dve.wait_ge(scored, p + 1)
                if p >= 2:
                    dve.wait_ge(turned, p - 1)
                for view, g0 in score_views(p):
                    n = G if g0 == 0 else NX
                    dst = top[:, p % 2, g0:g0 + n]
                    if len(view.shape) == 4:
                        dst = dst.rearrange("p (n g) -> p n g", n=4)
                    ins = nc.vector.tensor_reduce(dst, view, AX, ALU.max)
                link(ins)
                for view, g0 in score_views(p):
                    n = G if g0 == 0 else NX
                    if len(view.shape) == 4:
                        for j in range(4):
                            ins = nc.vector.tensor_tensor(groups(prob[:, p % 2, j * 256:(j + 1) * 256]), view[:, j],
                                                          spread(top[:, p % 2, 4 * j:4 * j + 4], SEQ), ALU.subtract)
                    else:
                        ins = nc.vector.tensor_tensor(groups(prob[:, p % 2, g0 * SEQ:(g0 + n) * SEQ]), view,
                                                      spread(top[:, p % 2, g0:g0 + n], SEQ), ALU.subtract)
                ins.then_inc(lowered, 1)

            def norm(p):
                dve.wait_ge(expd, p + 1)
                link(nc.vector.tensor_reduce(whole[:, p % 2, :], groups(prob[:, p % 2, :]), AX, ALU.add))
                link(nc.vector.reciprocal(whole[:, p % 2, :], whole[:, p % 2, :]))
                if NX:
                    link(nc.vector.tensor_scalar(whole[:, p % 2, 0:G], whole[:, p % 2, 0:G], w["regscale"], None, ALU.mult))
                    link(nc.vector.tensor_scalar(whole[:, p % 2, G:], whole[:, p % 2, G:], 0.5, None, ALU.mult))
                if masked:
                    dve.wait_ge(maskd, p + 1)
                nc.vector.tensor_tensor(groups(kept[:, p % 2, :]), groups(kept[:, p % 2, :]),
                                        spread(whole[:, p % 2, :], SEQ), ALU.mult).then_inc(normed, 1)

            lower(0)
            for p in range(NPAIR):
                if p + 1 < NPAIR:
                    lower(p + 1)
                norm(p)

        @block.gpsimd
        def _(pool):
            for p in range(NPAIR if masked else 0):
                pool.wait_ge(expd, p + 1)
                if p >= 2:
                    pool.wait_ge(turned, p - 1)
                nc.gpsimd.tensor_tensor(groups(kept[:, p % 2, :]), groups(prob[:, p % 2, :]),
                                        w["later"].unsqueeze(1).to_broadcast([P, G, SEQ]), ALU.mult).then_inc(maskd, 1)

        @block.scalar
        def _(act):
            def exp(p):
                act.wait_ge(lowered, p + 1)
                nc.scalar.activation(prob[:, p % 2, :], prob[:, p % 2, :], ACT.Exp, scale=scale).then_inc(expd, 1)

            exp(0)
            for p in range(NPAIR):
                if p + 1 < NPAIR:
                    exp(p + 1)
                act.wait_ge(turned, p + 1)
                if p >= 2:
                    act.wait_ge(mixed, p - 1)
                if narrow:
                    nc.scalar.activation(probT[:, p % 2, :], k.ps[2 + p % 2][:, 0:512], ACT.Copy).then_inc(turned_sb, 1)
                else:
                    if NX:
                        nc.scalar.activation(probT[:, p % 2, 8 * P:], k.ps[1][:, 256:384], ACT.Copy)
                    nc.scalar.activation(probT[:, p % 2, 0:8 * P].rearrange("p (n c) -> p n c", n=2),
                                         k.ps_all[:, 4:6, :], ACT.Copy).then_inc(turned_sb, 1)
                act.wait_ge(mixed, p + 1)
                for b in range(2):
                    ins = nc.scalar.activation(out[:, :, p * PAIR + b * SEQ:p * PAIR + (b + 1) * SEQ], mix(p, b), ACT.Copy)
                ins.then_inc(mixed_sb, 1)


def load(k, aps, where):
    nc = k.nc
    loaded = k.sem("loaded")
    with nc.Block() as block:
        @block.sync
        def _(sp):
            for name, _ in PACKS:
                sp.dma_start(k.packs[name][:, :], aps[name]).then_inc(loaded, 16)
            sp.wait_ge(loaded, 16 * len(PACKS))
    for name, _ in PACKS:
        for part, (rows, at, shape) in where[name].items():
            n = int(np.prod(shape))
            ap = k.packs[name][0:rows, at:at + n]
            if len(shape) == 2:
                ap = ap.rearrange("p (a b) -> p a b", b=shape[1])
            if len(shape) == 3:
                ap = ap.rearrange("p (a b c) -> p a b c", b=shape[1], c=shape[2])
            k.w[part] = ap


def setup(k):
    nc, w = k.nc, k.w
    wq = k.keep("wq0", [64, 8, 96])
    wvo = k.keep("wvo0", [P, 2, P])
    rope = k.keep("rope", [64, SEQ])
    decay = k.keep("decay", [P, 2, 2, STATE])
    guide = k.keep("guide", [P, 2])
    foldb = k.keep("foldb", [96, 32], BF16)
    k.w.update(wq0=wq, wvo0=wvo, rope=rope, decay=decay, guide=guide, foldb=foldb)
    s_pe, s_act, s_dve = k.sem("setup_pe"), k.sem("setup_act"), k.sem("setup_dve")
    with nc.sbuf_tensor("turn", [64, 8], F32) as turn, nc.sbuf_tensor("unit", [P, 4], F32) as unit, \
            nc.sbuf_tensor("ropet", [64, SEQ], F32) as ropet, nc.Block() as block:
        @block.tensor
        def _(pe):
            for h in range(8):
                nc.tensor.matmul(k.ps[0][0:64, 32 * h:32 * h + 32], w["uqT"][:, h, :], w["ukT"][:, h, :], start=True, stop=True)
            for h in range(8):
                j, t = h % 4, h // 4
                ins = nc.tensor.matmul(k.ps[1][32 * j:32 * j + 32, t * P:(t + 1) * P], w["uvT"][:, h, :], w["wo"][:, h, :],
                                       start=True, stop=True)
            ins.then_inc(s_pe, 1)
            pe.wait_ge(s_act, 1)
            nc.tensor.matmul(k.ps[2][:, 0:1], w["heads8"], unit[:, 0:1], start=True, stop=True).then_inc(s_pe, 1)

        @block.scalar
        def _(act):
            link = Count(act, s_act)
            link(nc.scalar.activation(unit[:, 0:1], w["qg"], ACT.Square))
            act.wait_ge(s_pe, 2)
            link(nc.scalar.activation(unit[:, 1:2], k.ps[2][:, 0:1], ACT.Ln))
            link(nc.scalar.activation(unit[:, 2:3], unit[:, 1:2], ACT.Exp, scale=-0.5))
            for d in range(2):
                link(nc.scalar.activation(decay[:, d], w[f"alog{d}"], ACT.Exp))
            link(nc.scalar.activation(turn[:, 0:1], w["delta"], ACT.Exp, scale=-1.0))
            nc.scalar.activation(wq[:, :, 64:96], k.ps[0][0:64, 0:256].rearrange("p (h c) -> p h c", h=8), ACT.Copy)
            link(nc.scalar.activation(wvo[:, :, :], k.ps[1][:, 0:256].rearrange("p (t c) -> p t c", t=2), ACT.Copy))
            act.wait_ge(s_dve, 3)
            link(nc.scalar.activation(turn[:, 4:5], turn[:, 3:4], ACT.Sin))
            link(nc.scalar.activation(turn[:, 5:6], turn[:, 2:3], ACT.Sin, scale=3.141592))

        @block.vector
        def _(dve):
            link = Count(dve, s_dve)
            dve.wait_ge(s_act, 6)
            link(nc.vector.tensor_scalar(turn[:, 1:2], turn[:, 0:1], 1.0, None, ALU.add))
            link(nc.vector.reciprocal(turn[:, 2:3], turn[:, 1:2]))
            link(nc.vector.tensor_scalar(turn[:, 3:4], turn[:, 2:3], 2 * 3.141592, -3.141592, ALU.mult, ALU.add))
            link(nc.vector.tensor_scalar(decay[:, :], decay[:, :], -1.0, None, ALU.mult))
            link(nc.vector.scalar_tensor_tensor(guide[:, 0:1], w["qg"], 1.0 / 16, unit[:, 2:3], ALU.mult, ALU.mult))
            link(nc.vector.tensor_copy(guide[:, 1:2], guide[:, 0:1]))
            link(nc.vector.tensor_copy(foldb[:, :], w["fold"]))
            link(nc.vector.tensor_copy(wq[:, :, 0:64], w["qr4"]))
            dve.wait_ge(s_act, 9)
            link(nc.vector.tensor_tensor(turn[:, 6:7], turn[:, 5:6], turn[:, 5:6], ALU.mult))
            link(nc.vector.tensor_scalar(turn[:, 7:8], turn[:, 6:7], -2.0, 1.0, ALU.mult, ALU.add))
            link(nc.vector.tensor_scalar(ropet[:, :], w["ropeU"], turn[:, 7:8], None, ALU.mult))
            link(nc.vector.scalar_tensor_tensor(rope[:, :], w["ropeW"], turn[:, 4:5], ropet[:, :], ALU.mult, ALU.add))


def attn0(k):
    nc, w, X = k.nc, k.w, k.X
    with ExitStack() as ctx:
        sb = lambda n, s: ctx.enter_context(nc.sbuf_tensor(f"a0_{n}", s, F32))
        lat, Q, K, V, O = sb("lat", [64, CH]), sb("q", [96, 4, BCH, 2, SEQ]), sb("k", [96, CH]), sb("v", [P, NPAIR, 32]), sb("o", [P, 2, CH])
        with nc.sbuf_tensor("a0_soft", [64, 2, CH], F32) as soft, nc.sbuf_tensor("a0_kr", [64, CH], F32) as kr:
            raw, latd, bounded, logd, turned, vdone, folded = (k.sem(f"a0_{s}") for s in (
                "raw", "latd", "bounded", "logd", "turned", "vdone", "folded"))
            chain, achain = k.sem("a0_chain"), k.sem("a0_achain")
            table = w["rope"][:, :].unsqueeze(1).to_broadcast([64, BCH, SEQ])
            bank = lambda i: k.ps[i % 4]
            with nc.Block() as block:
                @block.tensor
                def _(pe):
                    nc.tensor.matmul(k.ps[4][0:64, :], w["wdq"], X[:, :], start=True, stop=True).then_inc(latd, 1)
                    nc.tensor.matmul(bank(0)[0:96, :], w["wkv"], X[:, :], start=True, stop=True).then_inc(raw, 1)
                    for p in range(NPAIR):
                        ins = nc.tensor.matmul(k.ps[5][:, 32 * p:32 * p + 32], X[:, p * PAIR:(p + 1) * PAIR], w["wkv"][:, 64:96],
                                               start=True, stop=True)
                    ins.then_inc(vdone, 1)
                    pe.wait_ge(latd, 2)
                    for h in range(8):
                        if h >= 3:
                            pe.wait_ge(turned, h - 2)
                        nc.tensor.matmul(bank(h + 1)[0:96, :], w["wq0"][:, h, :], lat[:, :], start=True, stop=True).then_inc(raw, 1)
                    pe.wait_ge(turned, 1)
                    nc.tensor.matmul(k.ps[6][0:64, :], w["fold64"], kr[:, :], start=True, stop=True).then_inc(folded, 1)

                @block.scalar
                def _(act):
                    act.wait_ge(latd, 1)
                    nc.scalar.activation(lat[:, :], k.ps[4][0:64, :], ACT.Copy).then_inc(latd, 1)
                    link = Count(act, achain)
                    for i in range(9):
                        dst = groups(K[64:96, :]) if i == 0 else Q[64:96, (i - 1) // 2, :, (i - 1) % 2, :]
                        act.wait_ge(bounded, i + 1)
                        link(nc.scalar.activation(soft[:, i % 2, :], soft[:, i % 2, :], ACT.Exp))
                        nc.scalar.activation(dst, groups(bank(i)[64:96, :]), ACT.Copy)
                        nc.scalar.activation(soft[:, i % 2, :], soft[:, i % 2, :], ACT.Ln, bias=1.0).then_inc(logd, 1)
                    act.wait_ge(vdone, 1)
                    nc.scalar.activation(V[:, :, :], k.ps[5][:, 0:P].rearrange("p (n c) -> p n c", c=32), ACT.Copy)
                    act.wait_ge(folded, 1)
                    nc.scalar.activation(K[0:64, :], k.ps[6][0:64, :], ACT.Copy)

                @block.vector
                def _(dve):
                    link = Count(dve, chain)

                    def bound(i):
                        dve.wait_ge(raw, i + 1)
                        nc.vector.tensor_scalar(soft[:, i % 2, :], bank(i)[0:64, :], 40.0, None, ALU.min).then_inc(bounded, 1)

                    bound(0)
                    for i in range(9):
                        if i + 1 < 9:
                            bound(i + 1)
                        dve.wait_ge(logd, i + 1)
                        link(nc.vector.tensor_tensor(soft[:, i % 2, :], bank(i)[0:64, :], soft[:, i % 2, :], ALU.max))
                        dst = groups(kr[:, :]) if i == 0 else Q[0:64, (i - 1) // 2, :, (i - 1) % 2, :]
                        ins = nc.vector.tensor_tensor(dst, groups(soft[:, i % 2, :]), table, ALU.mult)
                        ins.then_inc(turned, 1)
                        dve.wait_ge(turned, i + 1)
        attention(k, "a0a", Q, K, V, float(96 ** -0.5), True, O)
        done = k.sem("a0_out")
        with nc.Block() as block:
            @block.tensor
            def _(pe):
                for t in range(2):
                    nc.tensor.matmul(k.ps[7][:, :], w["wvo0"][:, t, :], O[:, t, :], start=t == 0, stop=t == 1)
    layer_norm(k, "a0n", [(X, None, None)], total={"z": k.Z, "psum": k.ps[7], "parts": [X]})


def moe(k):
    nc, w, X = k.nc, k.w, k.X
    sent, picked, gated, gates_sb, hidden, scaled = (k.sem(f"moe_{s}") for s in (
        "sent", "picked", "gated", "gates_sb", "hidden", "scaled"))
    NT = 2 * EXPERTS
    with ExitStack() as ctx:
        sb = lambda n, s, dt=F32: ctx.enter_context(nc.sbuf_tensor(f"moe_{n}", s, dt))
        weight, pick = sb("weight", [P, 256]), sb("pick", [P, 256], I32)
        mine = sb("mine", [P, EXPERTS, 256])
        gate, H = sb("gate", [P, EXPERTS, CH]), sb("h", [P, 4, CH])
        block = ctx.enter_context(nc.Block())
        cols = bass.ds(k.chunk * 256, 256)

        @block.sync
        def _(sp):
            sp.dma_start(weight[:, :], k.aps["gatew"][:, cols]).then_inc(sent, 16)
            sp.dma_start(pick[:, :], k.aps["pick"][:, cols]).then_inc(sent, 16)

        @block.tensor
        def _(pe):
            def hide(i):
                if i >= 4:
                    pe.wait_ge(scaled, i - 3)
                nc.tensor.matmul(k.ps[i % 4][:, :], w["pin"][:, i * P:(i + 1) * P], X[:, :], start=True, stop=True).then_inc(hidden, 1)

            hide(0)
            hide(1)
            for e in range(EXPERTS):
                pe.wait_ge(picked, e + 1)
                if e >= 2:
                    pe.wait_ge(gates_sb, e - 1)
                for s in range(2):
                    rows = slice(64 * s, 64 * s + 64)
                    ins = nc.tensor.matmul(k.ps[4 + 2 * (e % 2) + s][:, 0:256], w["ones"][rows], mine[rows, e, :],
                                           start=True, stop=True, tile_position=(64 * s, 0))
                ins.then_inc(gated, 1)
            pe.wait_ge(gates_sb, EXPERTS)
            for i in range(NT):
                if i + 2 < NT:
                    hide(i + 2)
                pe.wait_ge(scaled, i + 1)
                nc.tensor.matmul(k.ps[7][:, :], w["pout"][:, i // 2, i % 2, :], H[:, i % 4, :], start=i == 0, stop=i == NT - 1)

        @block.scalar
        def _(act):
            for e in range(EXPERTS):
                act.wait_ge(gated, e + 1)
                b = 4 + 2 * (e % 2)
                dst = gate[:, e, :].rearrange("p (n s q) -> p s n q", s=2, q=SEQ)
                for s in range(2):
                    ins = nc.scalar.activation(dst[:, s], groups(k.ps[b + s][:, 0:256]), ACT.Copy)
                ins.then_inc(gates_sb, 1)

        @block.vector
        def _(dve):
            dve.wait_ge(sent, 32)
            for e in range(EXPERTS):
                nc.vector.scalar_tensor_tensor(mine[:, e, :], pick[:, :], float(e), weight[:, :], ALU.is_equal,
                                               ALU.mult).then_inc(picked, 1)
            for i in range(NT):
                dve.wait_ge(hidden, i + 1)
                dve.wait_ge(gates_sb, i // 2 + 1)
                nc.vector.scalar_tensor_tensor(H[:, i % 4, :], k.ps[i % 4][:, :], 0.0, gate[:, i // 2, :], ALU.max,
                                               ALU.mult).then_inc(scaled, 1)
    layer_norm(k, "moen", [(X, None, None)], total={"z": k.Z, "psum": k.ps[7], "parts": [X]})


def ffn(k):
    nc, w, X = k.nc, k.w, k.X
    T = CH // P
    with ExitStack() as ctx:
        sb = lambda n, s, dt=F32: ctx.enter_context(nc.sbuf_tensor(f"ffn_{n}", s, dt))
        L, hot, eq, hot2 = (sb(n, [P, T, EXPERTS]) for n in ("l", "hot", "eq", "hot2"))
        best, second, pr, ex = (sb(n, [P, T]) for n in ("best", "second", "pr", "ex"))
        G = sb("g", [P, EXPERTS, T])
        gate, S, H, O, acc = (sb("gate", [P, EXPERTS, CH]), sb("s", [P, 2, CH]), sb("h", [P, 2, 4, CH]), sb("o", [P, 2, CH]),
                              sb("acc", [P, CH]))
        logits, chain, raised, chosen, gated, gates_sb = (k.sem(f"ffn_{s}") for s in (
            "logits", "chain", "raised", "chosen", "gated", "gates_sb"))
        with nc.Block() as block:
            @block.tensor
            def _(pe):
                for t in range(T):
                    ins = nc.tensor.matmul(k.ps[0][:, 8 * t:8 * t + 8], X[:, t * P:(t + 1) * P], w["router"], start=True, stop=True)
                ins.then_inc(logits, 1)
                pe.wait_ge(chosen, 1)
                for e in range(EXPERTS):
                    if e >= 2:
                        pe.wait_ge(gates_sb, e - 1)
                    for t in range(T):
                        ins = nc.tensor.matmul(k.ps[1 + e % 2][:, t * P:(t + 1) * P], G[:, e, t:t + 1].to_broadcast([P, P]),
                                               w["ident"], start=True, stop=True)
                    ins.then_inc(gated, 1)

            @block.scalar
            def _(act):
                act.wait_ge(chain, 13)
                nc.scalar.activation(ex[:, :], ex[:, :], ACT.Exp).then_inc(raised, 1)
                for e in range(EXPERTS):
                    act.wait_ge(gated, e + 1)
                    nc.scalar.activation(gate[:, e, :], k.ps[1 + e % 2][:, :], ACT.Copy).then_inc(gates_sb, 1)

            @block.vector
            def _(dve):
                link = Count(dve, chain)
                prio = w["prio"].unsqueeze(1).to_broadcast([P, T, EXPERTS])
                tt, full = nc.vector.tensor_tensor, (lambda a: spread(a[:, :], EXPERTS))

                def first_of(m, onehot):
                    link(nc.vector.tensor_reduce(m[:, :], L[:, :, :], AX, ALU.max))
                    link(tt(eq[:, :, :], L[:, :, :], full(m), ALU.is_equal))
                    link(tt(eq[:, :, :], eq[:, :, :], prio, ALU.mult))
                    link(nc.vector.tensor_reduce(pr[:, :], eq[:, :, :], AX, ALU.max))
                    link(tt(onehot[:, :, :], prio, full(pr), ALU.is_equal))

                dve.wait_ge(logits, 1)
                link(tt(L[:, :, :], k.ps[0][:, 0:8 * T].rearrange("p (t e) -> p t e", e=EXPERTS),
                        w["router_b"].unsqueeze(1).to_broadcast([P, T, EXPERTS]), ALU.add))
                first_of(best, hot)
                link(nc.vector.scalar_tensor_tensor(L[:, :, :], hot[:, :, :], -BIG, L[:, :, :], ALU.mult, ALU.add))
                first_of(second, hot2)
                link(tt(ex[:, :], second[:, :], best[:, :], ALU.subtract))
                dve.wait_ge(raised, 1)
                link(nc.vector.tensor_scalar(best[:, :], ex[:, :], 1.0, None, ALU.add))
                link(nc.vector.reciprocal(best[:, :], best[:, :]))
                link(tt(ex[:, :], ex[:, :], best[:, :], ALU.mult))
                link(tt(hot[:, :, :], hot[:, :, :], full(best), ALU.mult))
                link(tt(hot2[:, :, :], hot2[:, :, :], full(ex), ALU.mult))
                tt(G[:, :, :].rearrange("p e t -> p t e"), hot[:, :, :], hot2[:, :, :], ALU.add).then_inc(chosen, 1)

        up, silud, hidden, down, weighed, summed = (k.sem(f"ffn_{s}") for s in (
            "up", "silud", "hidden", "down", "weighed", "summed"))
        with nc.Block() as block:
            @block.tensor
            def _(pe):
                def give(e):
                    pe.wait_ge(hidden, 4 * e + 4)
                    if e >= 2:
                        pe.wait_ge(weighed, e - 1)
                    for f in range(4):
                        ins = nc.tensor.matmul(k.ps[4 + e % 2][:, :], w["w2"][:, e, f, :], H[:, e % 2, f, :], start=f == 0, stop=f == 3)
                    ins.then_inc(down, 1)

                for e in range(EXPERTS):
                    for f in range(4):
                        i = 4 * e + f
                        if i >= 2:
                            pe.wait_ge(hidden, i - 1)
                        for half in range(2):
                            at = e * 1024 + (4 * half + f) * P
                            ins = nc.tensor.matmul(k.ps[2 * half + i % 2][:, :], w["w1"][:, at:at + P], X[:, :], start=True, stop=True)
                        ins.then_inc(up, 1)
                    if e:
                        give(e - 1)
                give(EXPERTS - 1)

            @block.scalar
            def _(act):
                for i in range(4 * EXPERTS):
                    e, f = divmod(i, 4)
                    act.wait_ge(up, i + 1)
                    if i >= 2:
                        act.wait_ge(hidden, i - 1)
                    nc.scalar.activation(S[:, i % 2, :], k.ps[i % 2][:, :], ACT.Silu, bias=w["b1"][:, e, f:f + 1]).then_inc(silud, 1)
                nc.scalar.preload_act_table_set("natural_log_exp_and_others")

            @block.vector
            def _(dve):
                def weigh(e):
                    dve.wait_ge(down, e + 1)
                    if e >= 2:
                        dve.wait_ge(summed, e - 1)
                    nc.vector.scalar_tensor_tensor(O[:, e % 2, :], k.ps[4 + e % 2][:, :], w["b2"][:, e:e + 1], gate[:, e, :],
                                                   ALU.add, ALU.mult).then_inc(weighed, 1)

                for e in range(EXPERTS):
                    if e >= 2:
                        dve.wait_ge(down, e - 1)
                    for f in range(4):
                        i = 4 * e + f
                        dve.wait_ge(silud, i + 1)
                        nc.vector.scalar_tensor_tensor(H[:, e % 2, f, :], k.ps[2 + i % 2][:, :], w["b1"][:, e, 4 + f:5 + f],
                                                       S[:, i % 2, :], ALU.add, ALU.mult).then_inc(hidden, 1)
                    if e:
                        weigh(e - 1)
                weigh(EXPERTS - 1)

            @block.gpsimd
            def _(pool):
                for e in range(EXPERTS):
                    pool.wait_ge(weighed, e + 1)
                    if e == 0:
                        nc.gpsimd.tensor_copy(acc[:, :], O[:, 0, :]).then_inc(summed, 1)
                    else:
                        pool.wait_ge(summed, e)
                        nc.gpsimd.tensor_tensor(acc[:, :], acc[:, :], O[:, e % 2, :], ALU.add).then_inc(summed, 1)
        layer_norm(k, "ffnn", [(X, None, None)], total={"z": k.Z, "psum": acc, "parts": [X]})


def mamba(k):
    nc, w, X = k.nc, k.w, k.X
    with ExitStack() as ctx:
        sb = lambda n, s, dt=F32: ctx.enter_context(nc.sbuf_tensor(f"mb_{n}", s, dt))
        U, ZS = sb("u", [P, 2, 2, CH]), sb("zs", [P, 2, 2, CH])
        back = lambda ap: groups(ap)[:, :, ::-1]
        turned, cleared, inx, inz, padded, convd, chain, actd = (k.sem(f"mb_{s}") for s in (
            "turned", "cleared", "inx", "inz", "padded", "convd", "chain", "actd"))
        with nc.sbuf_tensor("mb_xr", [P, CH], F32) as XR, nc.sbuf_tensor("mb_pad", [P, 4, BCH, SEQ + 3], F32) as pad, \
                nc.sbuf_tensor("mb_conv", [P, 2, CH], F32) as conv, nc.Block() as block:
            @block.tensor
            def _(pe):
                for i in range(4):
                    d, t = divmod(i, 2)
                    if i == 2:
                        pe.wait_ge(turned, 1)
                    src = XR if d else X
                    nc.tensor.matmul(k.ps[i][:, :], w["inT"][:, t * P:(t + 1) * P], src[:, :], start=True, stop=True).then_inc(inx, 1)
                    nc.tensor.matmul(k.ps[4 + i][:, :], w["inT"][:, (2 + t) * P:(3 + t) * P], src[:, :], start=True,
                                     stop=True).then_inc(inz, 1)

            @block.gpsimd
            def _(pool):
                nc.gpsimd.memset(pad[:, :, :, 0:3].rearrange("p i b l -> p (i b) l"), 0.0).then_inc(cleared, 1)

            @block.scalar
            def _(act):
                for i in range(4):
                    act.wait_ge(inx, i + 1)
                    nc.scalar.activation(pad[:, i, :, 3:], groups(k.ps[i][:, :]), ACT.Copy).then_inc(padded, 1)
                for i in range(4):
                    d, t = divmod(i, 2)
                    act.wait_ge(inz, i + 1)
                    nc.scalar.activation(ZS[:, d, t, :], k.ps[4 + i][:, :], ACT.Silu)
                for i in range(4):
                    d, t = divmod(i, 2)
                    act.wait_ge(convd, i + 1)
                    nc.scalar.activation(U[:, d, t, :], conv[:, i % 2, :], ACT.Silu, bias=w[f"convb{d}"][:, t:t + 1]).then_inc(actd, 1)
                nc.scalar.preload_act_table_set("natural_log_exp_and_others")

            @block.vector
            def _(dve):
                link = Count(dve, chain)
                nc.vector.tensor_copy(groups(XR[:, :]), back(X[:, :])).then_inc(turned, 1)
                dve.wait_ge(cleared, 1)
                for i in range(4):
                    d, t = divmod(i, 2)
                    dve.wait_ge(padded, i + 1)
                    if i >= 2:
                        dve.wait_ge(actd, i - 1)
                    cw, dst = w[f"convw{d}"], groups(conv[:, i % 2, :])
                    link(nc.vector.tensor_scalar(dst, pad[:, i, :, 0:SEQ], cw[:, t, 0:1], None, ALU.mult))
                    for j in range(1, 4):
                        ins = nc.vector.scalar_tensor_tensor(dst, pad[:, i, :, j:j + SEQ], cw[:, t, j:j + 1], dst, ALU.mult, ALU.add)
                        if j < 3:
                            link(ins)
                    ins.then_inc(convd, 1)

        DT, DU = sb("dt", [P, 2, 2, CH]), sb("du", [P, 2, 2, CH])
        BC = sb("bc", [96, 2, CH], BF16)
        xproj, cut, rates, rated, soft, fed = (k.sem(f"mb_{s}") for s in ("xproj", "cut", "rates", "rated", "soft", "fed"))
        bchain, achain = k.sem("mb_bchain"), k.sem("mb_achain")
        with nc.sbuf_tensor("mb_low", [104, 2, CH], F32) as low, nc.sbuf_tensor("mb_mid", [96, 2, CH], BF16) as mid, nc.Block() as block:
            @block.tensor
            def _(pe):
                for d in range(2):
                    for t in range(2):
                        ins = nc.tensor.matmul(k.ps[d][0:104, :], w[f"xproj{d}"][:, t, :], U[:, d, t, :], start=t == 0, stop=t == 1)
                    ins.then_inc(xproj, 1)
                for d in range(2):
                    pe.wait_ge(cut, d + 1)
                    for t in range(2):
                        nc.tensor.matmul(k.ps[2 + 2 * d + t][:, :], w[f"dtw{d}"][96:104, t * P:(t + 1) * P], low[96:104, d, :],
                                         start=True, stop=True, tile_position=(96, 0)).then_inc(rates, 1)

            @block.scalar
            def _(act):
                for d in range(2):
                    act.wait_ge(xproj, d + 1)
                    nc.scalar.activation(low[96:104, d, :], k.ps[d][96:104, :], ACT.Copy).then_inc(cut, 1)
                link = Count(act, achain)
                for i in range(4):
                    d, t = divmod(i, 2)
                    act.wait_ge(rated, i + 1)
                    link(nc.scalar.activation(DT[:, d, t, :], DT[:, d, t, :], ACT.Exp))
                    nc.scalar.activation(DT[:, d, t, :], DT[:, d, t, :], ACT.Ln, bias=1.0).then_inc(soft, 1)

            @block.vector
            def _(dve):
                link = Count(dve, bchain)
                for d in range(2):
                    dve.wait_ge(xproj, d + 1)
                    link(nc.vector.tensor_copy(BC[:, d, :], k.ps[d][0:96, :]))
                    link(nc.vector.tensor_tensor(low[0:96, d, :], k.ps[d][0:96, :], BC[:, d, :], ALU.subtract))
                    nc.vector.tensor_copy(BC[32:64, d, :], low[32:64, d, :])
                    link(nc.vector.tensor_copy(mid[64:96, d, :], low[64:96, d, :]))
                    nc.vector.tensor_tensor(BC[64:96, d, :], low[64:96, d, :], mid[64:96, d, :], ALU.subtract)
                    for t in range(2):
                        i = 2 * d + t
                        dve.wait_ge(rates, i + 1)
                        nc.vector.tensor_scalar(DT[:, d, t, :], k.ps[2 + i][:, :], w[f"dtb{d}"][:, t:t + 1], 40.0, ALU.add,
                                                ALU.min).then_inc(rated, 1)
                for i in range(4):
                    d, t = divmod(i, 2)
                    dve.wait_ge(soft, i + 1)
                    link(nc.vector.scalar_tensor_tensor(DT[:, d, t, :], k.ps[2 + i][:, :], w[f"dtb{d}"][:, t:t + 1], DT[:, d, t, :],
                                                        ALU.add, ALU.max))
                    nc.vector.tensor_tensor(DU[:, d, t, :], DT[:, d, t, :], U[:, d, t, :], ALU.mult).then_inc(fed, 1)

        NI = 2 * STATE
        ins_rep, outs_rep, in_sb, decayed, started, fed_in, ran, read, added = (k.sem(f"mb_{s}") for s in (
            "ins_rep", "outs_rep", "in_sb", "decayed", "started", "fed_in", "ran", "read", "added"))
        with nc.sbuf_tensor("mb_da", [P, 2, 2 * CH], F32) as dA, nc.sbuf_tensor("mb_dbu", [P, 2, 2 * CH], F32) as dBu, \
                nc.sbuf_tensor("mb_st", [P, 2 * CH], F32) as st, nc.sbuf_tensor("mb_hc", [P, 2, 2 * CH], F32) as hC, \
                nc.sbuf_tensor("mb_br", [P, 2, CH], F32) as bR, nc.Block() as block:
            @block.tensor
            def _(pe):
                def replicate(i):
                    d, n = divmod(i, STATE)
                    if i >= 2:
                        pe.wait_ge(in_sb, i - 1)
                    nc.tensor.matmul(k.ps[i % 2][:, :], w["foldb"][:, n:n + 1].to_broadcast([96, P]), BC[:, d, :], start=True,
                                     stop=True).then_inc(ins_rep, 1)
                    if i >= 2:
                        pe.wait_ge(read, i - 1)
                    nc.tensor.matmul(k.ps[2 + i % 2][:, :], w["foldb"][:, 16 + n:17 + n].to_broadcast([96, P]), BC[:, d, :],
                                     start=True, stop=True).then_inc(outs_rep, 1)

                replicate(0)
                for i in range(NI):
                    d, n = divmod(i, STATE)
                    if i + 1 < NI:
                        replicate(i + 1)
                    pe.wait_ge(read, i + 1)
                    for t in range(2):
                        ins = nc.tensor.matmul(k.ps[4 + 2 * d + t][:, :], w["ident"], hC[:, i % 2, t * CH:(t + 1) * CH],
                                               start=n == 0, stop=n == STATE - 1)
                    ins.then_inc(added, 1)

            @block.scalar
            def _(act):
                for i in range(NI):
                    d, n = divmod(i, STATE)
                    act.wait_ge(ins_rep, i + 1)
                    if i >= 2:
                        act.wait_ge(fed_in, i - 1)
                    nc.scalar.activation(bR[:, i % 2, :], k.ps[i % 2][:, :], ACT.Copy).then_inc(in_sb, 1)
                    if i >= 2:
                        act.wait_ge(ran, i - 1)
                    for t in range(2):
                        ins = nc.scalar.activation(dA[:, i % 2, t * CH:(t + 1) * CH], DT[:, d, t, :], ACT.Exp,
                                                   scale=w["decay"][:, d, t, n:n + 1])
                    ins.then_inc(decayed, 1)

            @block.gpsimd
            def _(pool):
                for i in range(NI):
                    d, n = divmod(i, STATE)
                    pool.wait_ge(in_sb, i + 1)
                    if i >= 2:
                        pool.wait_ge(ran, i - 1)
                    nc.gpsimd.tensor_tensor(dBu[:, i % 2, :].rearrange("p (t c) -> p t c", t=2), DU[:, d],
                                            bR[:, i % 2, :].unsqueeze(1).to_broadcast([P, 2, CH]), ALU.mult).then_inc(fed_in, 1)
                    pool.wait_ge(decayed, i + 1)
                    nc.gpsimd.memset(dA[:, i % 2, ::SEQ], 0.0).then_inc(started, 1)

            @block.vector
            def _(dve):
                for i in range(NI):
                    dve.wait_ge(fed_in, i + 1)
                    dve.wait_ge(started, i + 1)
                    if i >= 1:
                        dve.wait_ge(read, i)
                    nc.vector.tensor_tensor_scan(st[:, :], dA[:, i % 2, :], dBu[:, i % 2, :], 0.0, ALU.mult, ALU.add).then_inc(ran, 1)
                    dve.wait_ge(ran, i + 1)
                    dve.wait_ge(outs_rep, i + 1)
                    if i >= 2:
                        dve.wait_ge(added, i - 1)
                    nc.vector.tensor_tensor(hC[:, i % 2, :].rearrange("p (t c) -> p t c", t=2),
                                            st[:, :].rearrange("p (t c) -> p t c", t=2),
                                            k.ps[2 + i % 2][:, :].unsqueeze(1).to_broadcast([P, 2, CH]), ALU.mult).then_inc(read, 1)

        skipped, gatedy, outd, dchain = (k.sem(f"mb_{s}") for s in ("skipped", "gatedy", "outd", "dchain"))
        with nc.Block() as block:
            @block.vector
            def _(dve):
                for i in range(4):
                    d, t = divmod(i, 2)
                    nc.vector.scalar_tensor_tensor(DU[:, d, t, :], U[:, d, t, :], w[f"dskip{d}"][:, t:t + 1], k.ps[4 + i][:, :],
                                                   ALU.mult, ALU.add).then_inc(skipped, 1)
                link = Count(dve, dchain)
                dve.wait_ge(outd, 1)
                link(nc.vector.tensor_tensor(k.Z[:, :], k.ps[0][:, :], X[:, :], ALU.add))
                dve.wait_ge(outd, 2)
                link(nc.vector.tensor_tensor(groups(k.Z[:, :]), groups(k.Z[:, :]), back(k.ps[1][:, :]), ALU.add))

            @block.gpsimd
            def _(pool):
                for i in range(4):
                    d, t = divmod(i, 2)
                    pool.wait_ge(skipped, i + 1)
                    nc.gpsimd.tensor_tensor(DU[:, d, t, :], DU[:, d, t, :], ZS[:, d, t, :], ALU.mult).then_inc(gatedy, 1)

            @block.tensor
            def _(pe):
                for i in range(4):
                    d, t = divmod(i, 2)
                    pe.wait_ge(gatedy, i + 1)
                    ins = nc.tensor.matmul(k.ps[d][:, :], w["outT"][:, t, :], DU[:, d, t, :], start=t == 0, stop=t == 1)
                    if t:
                        ins.then_inc(outd, 1)
    layer_norm(k, "mbn", [(X, None, None)], src=k.Z)


def project(k, tag, jobs):
    nc = k.nc
    done, by_act, by_dve = (k.sem(f"{tag}_{s}") for s in ("done", "by_act", "by_dve"))
    bank = lambda i, dst: k.ps[i % 8][:dst.shape[0], 0:dst.shape[1]]
    with nc.Block() as block:
        @block.tensor
        def _(pe):
            for i, (dst, terms) in enumerate(jobs):
                if i >= 8:
                    pe.wait_ge(by_dve if i % 2 else by_act, (i - 8) // 2 + 1)
                for n, (a, b) in enumerate(terms):
                    ins = nc.tensor.matmul(bank(i, dst), a, b, start=n == 0, stop=n == len(terms) - 1)
                ins.then_inc(done, 1)

        @block.scalar
        def _(act):
            for i in range(0, len(jobs), 2):
                act.wait_ge(done, i + 1)
                nc.scalar.activation(jobs[i][0], bank(i, jobs[i][0]), ACT.Copy).then_inc(by_act, 1)

        @block.vector
        def _(dve):
            for i in range(1, len(jobs), 2):
                dve.wait_ge(done, i + 1)
                nc.vector.tensor_copy(jobs[i][0], bank(i, jobs[i][0])).then_inc(by_dve, 1)


def mha(k, m, tag, x, xn, yn, yrows, masked, xo, parts, outs):
    nc, w = k.nc, k.w
    y = lambda t: t[0:yrows]
    with ExitStack() as ctx:
        sb = lambda n, s: ctx.enter_context(nc.sbuf_tensor(f"{tag}_{n}", s, F32))
        O = sb("o", [P, 4, CH])
        with nc.sbuf_tensor(f"{tag}_q", [P, 4, CH], F32) as Q, nc.sbuf_tensor(f"{tag}_k", [P, 4, CH], F32) as K, \
                nc.sbuf_tensor(f"{tag}_v", [P, NPAIR, 512], F32) as V:
            jobs = [(Q[:, t, :], [(w[m + "wq"][:, t * P:(t + 1) * P], xn[:, :])]) for t in range(4)]
            jobs += [(K[:, t, :], [(w[m + "wk"][:, t * P:(t + 1) * P], y(yn)[:, :])]) for t in range(4)]
            jobs += [(V[:, p, :], [(y(yn)[:, p * PAIR:(p + 1) * PAIR], w[m + "wv"])]) for p in range(NPAIR)]
            project(k, f"{tag}_in", jobs)
            attention(k, f"{tag}_at", Q, K, V, float(32 ** -0.5), False, O, masked=masked)
        with nc.Block() as block:
            @block.tensor
            def _(pe):
                for t in range(4):
                    nc.tensor.matmul(k.ps[7][:, :], w[m + "li1"][:, t, :], O[:, t, :], start=t == 0, stop=t == 3)
    with nc.sbuf_tensor(f"{tag}_hn", [P, CH], F32) as hn, nc.sbuf_tensor(f"{tag}_h", [P, 4, CH], F32) as H:
        layer_norm(k, f"{tag}_n3", [(hn, w[m + "ln3_g"], w[m + "ln3_b"])],
                   total={"z": xo, "psum": k.ps[7], "bias": w[m + "li1_b"], "parts": [x]})
        up, gelud = k.sem(f"{tag}_up"), k.sem(f"{tag}_gelud")
        with nc.Block() as block:
            @block.tensor
            def _(pe):
                for f in range(4):
                    nc.tensor.matmul(k.ps[f][:, :], w[m + "li2"][:, f * P:(f + 1) * P], hn[:, :], start=True, stop=True).then_inc(up, 1)
                for f in range(4):
                    pe.wait_ge(gelud, f + 1)
                    nc.tensor.matmul(k.ps[7][:, :], w[m + "li3"][:, f, :], H[:, f, :], start=f == 0, stop=f == 3)

            @block.scalar
            def _(act):
                for f in range(4):
                    act.wait_ge(up, f + 1)
                    nc.scalar.activation(H[:, f, :], k.ps[f][:, :], ACT.Gelu, bias=w[m + "li2_b"][:, f:f + 1]).then_inc(gelud, 1)
                nc.scalar.preload_act_table_set("natural_log_exp_and_others")
    layer_norm(k, f"{tag}_n4", outs, total={"z": k.Z, "psum": k.ps[7], "bias": w[m + "li3_b"], "parts": [xo] + parts})


def cross(k):
    nc, w, X = k.nc, k.w, k.X
    with ExitStack() as ctx:
        sb = lambda n, s: ctx.enter_context(nc.sbuf_tensor(f"ca_{n}", s, F32))
        x1, x3, xn, yn, xo, context = (sb(n, [P, CH]) for n in ("x1", "x3", "xn", "yn", "xo", "context"))
        sent = k.sem("ca_sent")
        with nc.Block() as block:
            @block.sync
            def _(sp):
                sp.dma_start(context[0:64, :], k.aps["ctxT"][:, bass.ds(k.chunk * CH, CH)]).then_inc(sent, 16)
                sp.wait_ge(sent, 16)
        layer_norm(k, "ca1", [(x1, w["ln1_g"], w["ln1_b"])], src=X)
        layer_norm(k, "ca2", [(xn, w["a1_lnx_g"], w["a1_lnx_b"]), (yn, w["a1_lny_g"], w["a1_lny_b"])], src=x1)
        mha(k, "a1_", "ca3", x1, xn, yn, P, True, xo, [x1], [(x3, w["ln2_g"], w["ln2_b"])])
        layer_norm(k, "ca4", [(xn, w["a2_lnx_g"], w["a2_lnx_b"])], src=x3)
        layer_norm(k, "ca5", [(yn, w["a2_lny_g"], w["a2_lny_b"])], src=context, rows=64)
        mha(k, "a2_", "ca6", x3, xn, yn, 64, False, xo, [x3, X], [(X, None, None)])


def similarity(k):
    nc, w, X = k.nc, k.w, k.X
    names = ("queried", "squared", "summed", "rooted", "aligned", "similar", "kept")
    queried, squared, summed, rooted, aligned, similar, kept = (k.sem(f"si_{s}") for s in names)
    cols = bass.ds(k.chunk * CH, CH)
    with nc.sbuf_tensor("si_sq", [P, CH], F32) as sq, nc.sbuf_tensor("si_r", [P, CH], F32) as root, nc.Block() as block:
        @block.tensor
        def _(pe):
            nc.tensor.matmul(k.ps[0][:, :], w["qnat"], X[:, :], start=True, stop=True).then_inc(queried, 1)
            pe.wait_ge(squared, 1)
            nc.tensor.matmul(k.ps[1][:, :], w["heads8"], sq[:, :], start=True, stop=True).then_inc(summed, 1)
            pe.wait_ge(aligned, 1)
            nc.tensor.matmul(k.ps[2][0:2, :], w["guide"][:, :], root[:, :], start=True, stop=True).then_inc(similar, 1)

        @block.scalar
        def _(act):
            act.wait_ge(queried, 1)
            nc.scalar.activation(sq[:, :], k.ps[0][:, :], ACT.Square).then_inc(squared, 1)
            act.wait_ge(summed, 1)
            nc.scalar.activation(root[:, :], k.ps[1][:, :], ACT.Ln).then_inc(rooted, 1)
            act.wait_ge(rooted, 1)
            nc.scalar.activation(root[:, :], root[:, :], ACT.Exp, scale=-0.5).then_inc(rooted, 1)

        @block.sync
        def _(sp):
            sp.dma_start(k.final[:, cols], X[:, :]).then_inc(kept, 16)
            sp.wait_ge(kept, 16)

        @block.vector
        def _(dve):
            dve.wait_ge(rooted, 2)
            nc.vector.tensor_tensor(root[:, :], root[:, :], k.ps[0][:, :], ALU.mult).then_inc(aligned, 1)
            dve.wait_ge(similar, 1)
            nc.vector.tensor_copy(k.sim[:, cols], k.ps[2][0:2, :])


def last(k):
    nc, w = k.nc, k.w
    Qx = k.keep("qx", [P, 4, BCH, 32])
    seqs = lambda t: t[:, :].rearrange("p (b q) -> p b q", q=SEQ)
    with k.stage():
        chain, cleared = k.sem("cl_chain"), k.sem("cl_cleared")
        with nc.sbuf_tensor("cl_span", [2, 4], F32) as span, nc.Block() as block:
            @block.gpsimd
            def _(pool):
                nc.gpsimd.memset(Qx[:, :, :, :].rearrange("p t b c -> p (t b c)"), 0.0)

            @block.vector
            def _(dve):
                link = Count(dve, chain)
                ts = nc.vector.tensor_scalar
                toks = seqs(k.sim)[:, :, REG:]
                link(nc.vector.tensor_reduce(span[:, 0:1], toks, mybir.AxisListType.XY, ALU.min))
                link(nc.vector.tensor_reduce(span[:, 1:2], toks, mybir.AxisListType.XY, ALU.max))
                link(nc.vector.tensor_tensor(span[:, 2:3], span[:, 1:2], span[:, 0:1], ALU.subtract))
                link(nc.vector.reciprocal(span[:, 3:4], span[:, 2:3]))
                link(ts(k.sim[:, :], k.sim[:, :], span[:, 0:1], span[:, 3:4], ALU.subtract, ALU.mult))
                link(ts(k.sim[:, :], k.sim[:, :], 0.9, None, ALU.is_gt))
                link(nc.vector.memset(seqs(k.sim)[:, :, 0:REG], 1.0))
    with nc.Fori(0, NCH) as chunk:
        with k.stage():
            cols = bass.ds(chunk * CH, CH)
            with ExitStack() as ctx:
                sb = lambda n, s: ctx.enter_context(nc.sbuf_tensor(f"la_{n}", s, F32))
                O, X, Z = sb("o", [P, 4, CH]), k.X, k.Z
                qm, km = sb("qm", [2, CH]), sb("km", [2, CH])
                with nc.sbuf_tensor("la_q", [P, 4, CH], F32) as Q, nc.sbuf_tensor("la_k", [P, 4, CH], F32) as K, \
                        nc.sbuf_tensor("la_v", [P, NPAIR, 512], F32) as V:
                    fetched, mchain = k.sem("la_fetched"), k.sem("la_mchain")
                    with nc.Block() as block:
                        @block.sync
                        def _(sp):
                            sp.dma_start(X[:, :], k.final[:, cols]).then_inc(fetched, 16)
                            sp.wait_ge(fetched, 16)

                        @block.vector
                        def _(dve):
                            link = Count(dve, mchain)
                            ts = nc.vector.tensor_scalar
                            ts(qm[:, :], k.sim[:, cols], w["qa"], w["qc"], ALU.mult, ALU.add)
                            link(ts(km[:, :], k.sim[:, cols], w["ka"], w["kc"], ALU.mult, ALU.add))
                            nc.vector.memset(seqs(km)[:, :, 0:REG], 0.0)
                    wide = w["wide"]
                    tile = lambda n, t: wide[:, n, t * P:(t + 1) * P]
                    jobs = [(Q[:, t, :], [(tile(0, t), X[:, :]), (w["maskrow"], qm[:, :])]) for t in range(4)]
                    jobs += [(K[:, t, :], [(tile(1, t), X[:, :]), (w["maskrow"], km[:, :])]) for t in range(4)]
                    jobs += [(V[:, p, :], [(X[:, p * PAIR:(p + 1) * PAIR], wide[:, 2, :])]) for p in range(NPAIR)]
                    project(k, "la_in", jobs)
                    with nc.Block() as block:
                        @block.vector
                        def _(dve):
                            for j in range(4):
                                rows = slice(32 * j, 32 * j + 32)
                                src = Q[rows, :, :].rearrange("p t (b q) -> p t b q", q=SEQ)[:, :, :, 0:REG]
                                nc.vector.tensor_scalar(Qx[rows, :, :, REG * j:REG * j + REG], src, w["negclass"][rows],
                                                        None, ALU.add)
                    attention(k, "la_at", Q, K, V, float(8 ** -0.5), False, O, regs=Qx)
                with nc.Block() as block:
                    @block.tensor
                    def _(pe):
                        for t in range(4):
                            nc.tensor.matmul(k.ps[7][:, :], w["proj"][:, t, :], O[:, t, :], start=t == 0, stop=t == 3)
                layer_norm(k, "lan", [(X, None, None)], total={"z": Z, "psum": k.ps[7], "bias": w["projb"], "parts": [X]})
            stored = k.sem("stored")
            with nc.Block() as block:
                @block.sync
                def _(sp):
                    sp.dma_start(k.aps["out"][:, cols], k.X[:, :]).then_inc(stored, 16)
                    sp.wait_ge(stored, 16)


STAGES = [attn0, moe, ffn, mamba, cross, similarity]



def build(nc, where, aps, upto=99):
    with ExitStack() as ctx:
        k = Core(nc, ctx)
        psum = ctx.enter_context(nc.psum_tensor("psum", [P, 8, 512], F32))
        k.ps_all = psum
        k.ps = [psum[:, i, :] for i in range(8)]
        k.packs = {name: k.keep(f"pack_{name}", list(aps[name].shape)) for name, _ in PACKS}
        k.aps = aps
        with k.stage():
            load(k, aps, where)
            setup(k)
        k.X, k.Z = k.keep("X", [P, CH]), k.keep("Z", [P, CH])
        k.final = nc.dram_tensor("between", (P, TOK), F32, kind="Internal").ap()
        k.sim = k.keep("sim", [2, TOK])
        with nc.Fori(0, NCH) as chunk:
            k.chunk = chunk
            with k.stage():
                sent = k.sem("x_sent")
                with nc.Block() as block:
                    @block.sync
                    def _(sp):
                        sp.dma_start(k.X[:, :], aps["xT"][:, bass.ds(chunk * CH, CH)]).then_inc(sent, 16)
                        sp.wait_ge(sent, 16)

                    @block.scalar
                    def _(act):
                        nc.scalar.preload_act_table_set("natural_log_exp_and_others")
            for stage in STAGES[:upto]:
                with k.stage():
                    stage(k)
            if upto < 6:
                with k.stage():
                    stored = k.sem("x_stored")
                    with nc.Block() as block:
                        @block.sync
                        def _(sp):
                            sp.dma_start(aps["out"][:, bass.ds(chunk * CH, CH)], k.X[:, :]).then_inc(stored, 16)
                            sp.wait_ge(stored, 16)
        if upto >= 6:
            last(k)


def kernel(**inputs):
    import concourse.bacc as bacc
    from concourse.bass_utils import run_bass_kernel_spmd

    a = {n: np.asarray(v) for n, v in inputs.items()}
    arrays, where, aps = {}, {}, {}
    for name, parts in PACKS:
        arrays[f"pack_{name}_dram"], where[name] = pack(parts(a))
    arrays["xT_dram"] = np.ascontiguousarray(a["x"].reshape(TOK, P).T)
    arrays["ctxT_dram"] = np.ascontiguousarray(a["ctx_512"].reshape(TOK, 64).T)
    for n, src in (("gatew", a["ctx_512"]), ("pick", a["itok_BxS2xS_0_7"])):
        arrays[f"{n}_dram"] = np.ascontiguousarray(src.reshape(NSEQ // 2, P, SEQ).transpose(1, 0, 2).reshape(P, -1))
    nc = bacc.Bacc("TRN2", target_bir_lowering=False, num_devices=1)
    for n, arr in arrays.items():
        ap = nc.dram_tensor(n, arr.shape, mybir.dt.from_np(arr.dtype), kind="ExternalInput").ap()
        aps[n[:-5].removeprefix("pack_")] = ap
    aps["out"] = nc.dram_tensor("out_dram", (P, TOK), F32, kind="ExternalOutput").ap()
    build(nc, where, aps)
    r = run_bass_kernel_spmd(nc, [arrays], core_ids=[0])
    return np.ascontiguousarray(r.results[0]["out_dram"].T).reshape(NSEQ, SEQ, P)
```

```python
from contextlib import ExitStack, contextmanager

import numpy as np

import concourse.bass as bass
from concourse import mybir

F32 = mybir.dt.float32
BF16 = mybir.dt.bfloat16
I32 = mybir.dt.int32
ALU = mybir.AluOpType
ACT = mybir.ActivationFunctionType
AX = mybir.AxisListType.X

P = 128
SEQ = 64
NSEQ = 32
TOK = SEQ * NSEQ
CH = 512
NCH = TOK // CH
BCH = CH // SEQ
PAIR = 2 * SEQ
NPAIR = CH // PAIR
BIG = float(2.0 ** 100)
EXPERTS = 8
STATE = 16
REG = 5


def rope_tables():
    half = 16
    theta = (np.float32(1.0) / np.float32(10000.0) ** (np.float32(2.0) * np.arange(half, dtype=np.float32) / np.float32(32.0)))
    a = (np.arange(SEQ, dtype=np.float32)[None, :] * theta.astype(np.float32)[:, None]).astype(np.float64)
    c, s = np.cos(a), np.sin(a)
    return np.concatenate([c, c, -s, s]).astype(np.float32), np.concatenate([-s, -s, -c, c]).astype(np.float32)


def constants():
    p = np.arange(P)
    u, w = rope_tables()
    eye = np.eye(P, dtype=np.float32)
    row = np.zeros((2, P), np.float32)
    row[0, p % 32 == 8] = 1
    row[1, p % 32 == 9] = 1
    two = lambda a, b: np.array([[a], [b]], np.float32)
    return {
        "ident": eye,
        "center": eye - np.float32(1 / P),
        "mean": np.full((P, P), 1 / P, np.float32),
        "center64": np.eye(64, dtype=np.float32) - np.float32(1 / 64),
        "mean64": np.full((64, 64), 1 / 64, np.float32),
        "later": (np.arange(SEQ)[None, :] > (p % SEQ)[:, None]).astype(np.float32),
        "ropeU": u, "ropeW": w,
        "ones": np.ones((P, P), np.float32),
        "fold": (np.arange(96)[:, None] % 32 == np.arange(32)[None, :]).astype(np.float32),
        "fold64": (np.arange(64)[:, None] % 32 == np.arange(64)[None, :] % 32).astype(np.float32),
        "heads8": (p[:, None] // 8 == p[None, :] // 8).astype(np.float32),
        "maskrow": row,
        "negclass": np.where(p % 32 == 8, BIG, np.where(p % 32 == 9, -BIG, 0)).astype(np.float32)[:, None],
        "regscale": np.where(p % SEQ < REG, 0.5, 1.0).astype(np.float32)[:, None],
        "prio": np.broadcast_to(EXPERTS - np.arange(EXPERTS, dtype=np.float32), (P, EXPERTS)),
        "eps": np.full((P, 1), 1e-5, np.float32),
        "qa": two(-BIG, BIG), "qc": two(0, -BIG), "ka": two(-1, 1), "kc": two(1, 0),
    }


def tiles(w):
    return w.reshape(-1, P, w.shape[-1]).transpose(1, 0, 2)


def attn0_parts(a):
    uq = a["L0_attn_W_uq"].reshape(64, 8, 64)
    qr = a["L0_attn_W_qr"].reshape(64, 8, 2, 16)
    kr = a["L0_attn_W_kr"].reshape(P, 2, 16)
    order = [0, 1, 1, 0]
    return {
        "wdq": a["L0_attn_W_dq"],
        "wkv": np.concatenate([kr[:, order].reshape(P, 64), a["L0_attn_W_dkv"]], 1),
        "qr4": qr[:, :, order].reshape(64, 8, 64),
        "uqT": uq.transpose(2, 1, 0),
        "ukT": a["L0_attn_W_uk"].reshape(32, 8, 64).transpose(2, 1, 0),
        "uvT": a["L0_attn_W_uv"].reshape(32, 8, 64).transpose(2, 1, 0),
        "wo": a["L0_attn_W_out"].reshape(8, 64, P).transpose(1, 0, 2),
        "delta": np.concatenate([a["L0_attn_raw_delta"]] * 4)[:, None],
    }


def moe_parts(a):
    return {
        "pin": a["L0_xattn_proj_in"].reshape(EXPERTS * 256, P).T,
        "pout": a["L0_xattn_proj_out"].reshape(EXPERTS, P, 2, P).transpose(3, 0, 2, 1),
    }


def ffn_parts(a):
    return {
        "router": a["L0_ffn_router_w"].T,
        "router_b": np.broadcast_to(a["L0_ffn_router_b"], (P, EXPERTS)),
        "b1": a["L0_ffn_b1"].reshape(EXPERTS, 8, P).transpose(2, 0, 1),
        "b2": a["L0_ffn_b2"].T,
        "w1": a["L0_ffn_w1"].reshape(EXPERTS * 1024, P).T,
        "w2": a["L0_ffn_w2"].reshape(EXPERTS, P, 4, P).transpose(3, 0, 2, 1),
    }


def mamba_parts(a):
    out = {"inT": a["L1_attn_in_proj_w"].T,
           "outT": a["L1_attn_out_proj_w"].reshape(P, 2, P).transpose(2, 1, 0)}
    for d, (s, al, dp) in enumerate((("", "A_log", "D"), ("b", "A_b_log", "D_b"))):
        xp = a[f"L1_attn_x_proj_w{s}"]
        bc = xp[8:40]
        out[f"xproj{d}"] = np.concatenate([bc, bc, bc, xp[0:8]]).T.reshape(2, P, 104).transpose(1, 0, 2)
        dt = np.zeros((104, 256), np.float32)
        dt[96:104] = a[f"L1_attn_dt_proj_w{s}"].T
        out[f"dtw{d}"] = dt
        out[f"dtb{d}"] = a[f"L1_attn_dt_proj_b{s}"].reshape(2, P).T
        out[f"convw{d}"] = tiles(a[f"L1_attn_conv_w{s}"])
        out[f"convb{d}"] = a[f"L1_attn_conv_b{s}"].reshape(2, P).T
        out[f"alog{d}"] = tiles(a["L1_attn_" + al])
        out[f"dskip{d}"] = a["L1_attn_" + dp].reshape(2, P).T
    return out


def cross_parts(a):
    x = lambda n: a["L1_xattn_" + n]
    col = lambda n: x(n)[:, None]
    out = {"ln1_g": col("ln1_g"), "ln1_b": col("ln1_b"), "ln2_g": col("ln2_g"), "ln2_b": col("ln2_b")}
    for m in ("a1_", "a2_"):
        for n in ("wq", "wk", "wv"):
            w = x(m + n)
            out[m + n] = w.transpose(1, 0, 2).reshape(w.shape[1], 512)
        out[m + "li1"] = tiles(x(m + "li1_w"))
        out[m + "li2"] = x(m + "li2_w")
        out[m + "li3"] = tiles(x(m + "li3_w"))
        out[m + "li2_b"] = x(m + "li2_b").reshape(4, P).T
        for n in ("li1_b", "li3_b", "lnx_g", "lnx_b", "lny_g", "lny_b", "ln3_g", "ln3_b"):
            out[m + n] = col(m + n)
    return out


def last_parts(a):
    w = a["L1_ffn_W_qkv"].reshape(P, 3, 16, 8)
    wide = np.zeros((P, 3, 16, 32), np.float32)
    wide[..., :8] = w
    proj = np.zeros((16, 32, P), np.float32)
    proj[:, :8] = a["L1_ffn_W_proj"].reshape(16, 8, P)
    return {
        "qnat": w[:, 0].reshape(P, P),
        "qg": a["L1_ffn_g_info"][0, 0][:, None],
        "wide": wide.reshape(P, 3, 512),
        "proj": tiles(proj.reshape(512, P)),
        "projb": a["L1_ffn_b_proj"][:, None],
    }


PACKS = [("const", lambda a: constants()), ("attn0", attn0_parts), ("moe", moe_parts), ("ffn", ffn_parts),
         ("mamba", mamba_parts), ("cross", cross_parts), ("last", last_parts)]


def pack(parts):
    where, at = {}, 0
    for name, a in parts.items():
        n = int(np.prod(a.shape[1:]))
        where[name] = (a.shape[0], at, tuple(a.shape[1:]))
        at += n
    whole = np.zeros((P, at), np.float32)
    for name, a in parts.items():
        rows, c, shape = where[name]
        whole[:rows, c:c + int(np.prod(shape))] = a.reshape(rows, -1)
    return whole, where


class Core:

    def __init__(self, nc, ctx):
        self.nc, self.ctx, self.sems, self.w = nc, ctx, [], {}

    def keep(self, name, shape, dt=F32):
        return self.ctx.enter_context(self.nc.sbuf_tensor(name, shape, dt))

    def sem(self, name):
        s = self.stage_ctx.enter_context(self.nc.semaphore(name))
        self.sems.append(s)
        return s

    @contextmanager
    def stage(self):
        with ExitStack() as self.stage_ctx:
            self.sems = []
            yield
            nums = sorted(s.num for s in self.sems)
            runs = [n for n in nums if n - 1 not in nums], [n for n in nums if n + 1 not in nums]
            for a, b in zip(*runs):
                self.nc.gpsimd.sem_clear(range(a, b + 1))
            self.nc.all_engine_barrier()


class Count:

    def __init__(self, eng, sem):
        self.eng, self.sem, self.n = eng, sem, 0

    def __call__(self, ins):
        self.n += 1
        ins.then_inc(self.sem, 1)
        self.eng.wait_ge(self.sem, self.n)


def groups(ap, k=SEQ):
    return ap.rearrange("p (g k) -> p g k", k=k)


def spread(ap, n):
    return ap.unsqueeze(2).to_broadcast([ap.shape[0], ap.shape[1], n])


def layer_norm(k, tag, outs, src=None, total=None, rows=P, halves=2):
    nc, w = k.nc, k.w
    center, mean = (w["center"], w["mean"]) if rows == P else (w["center64"], w["mean64"])
    n = CH // halves
    summed, centered, squared, meaned, rooted, chain = (k.sem(f"{tag}_{s}") for s in (
        "summed", "centered", "squared", "meaned", "rooted", "chain"))
    with ExitStack() as ctx:
        sq = ctx.enter_context(nc.sbuf_tensor(f"{tag}_sq", [rows, CH], F32))
        rstd = ctx.enter_context(nc.sbuf_tensor(f"{tag}_rstd", [rows, CH], F32))
        tmp = ctx.enter_context(nc.sbuf_tensor(f"{tag}_tmp", [rows, CH], F32))
        z = total["z"] if total else src
        block = ctx.enter_context(nc.Block())
        cut = lambda t, h: t[0:rows, h * n:(h + 1) * n]
        cps = lambda h: k.ps[h][0:rows, 0:n]
        vps = lambda h: k.ps[2 + h][0:rows, 0:n]

        @block.tensor
        def _(pe):
            for h in range(halves):
                if total:
                    pe.wait_ge(summed, h + 1)
                nc.tensor.matmul(cps(h), center[0:rows], cut(z, h), start=True, stop=True).then_inc(centered, 1)
            for h in range(halves):
                pe.wait_ge(squared, h + 1)
                nc.tensor.matmul(vps(h), mean[0:rows], cut(sq, h), start=True, stop=True).then_inc(meaned, 1)

        @block.scalar
        def _(act):
            for h in range(halves):
                act.wait_ge(centered, h + 1)
                nc.scalar.activation(cut(sq, h), cps(h), ACT.Square).then_inc(squared, 1)
            for h in range(halves):
                act.wait_ge(meaned, h + 1)
                nc.scalar.activation(cut(rstd, h), vps(h), ACT.Ln, bias=w["eps"][0:rows]).then_inc(rooted, 1)
                act.wait_ge(rooted, 2 * h + 1)
                nc.scalar.activation(cut(rstd, h), cut(rstd, h), ACT.Exp, scale=-0.5).then_inc(rooted, 1)

        @block.vector
        def _(dve):
            link = Count(dve, chain)
            for h in range(halves if total else 0):
                parts = total["parts"]
                for i, part in enumerate(parts):
                    dst = cut(z, h)
                    first = cut(total["psum"], h) if i == 0 else dst
                    if i == 0 and total.get("bias") is not None:
                        ins = nc.vector.scalar_tensor_tensor(dst, first, total["bias"], cut(part, h), ALU.add, ALU.add)
                    else:
                        ins = nc.vector.tensor_tensor(dst, first, cut(part, h), ALU.add)
                    if i + 1 < len(parts):
                        link(ins)
                ins.then_inc(summed, 1)
            for h in range(halves):
                dve.wait_ge(rooted, 2 * h + 2)
                for dst, gain, shift in outs:
                    if gain is None:
                        nc.vector.tensor_tensor(cut(dst, h), cps(h), cut(rstd, h), ALU.mult)
                    else:
                        link(nc.vector.scalar_tensor_tensor(cut(tmp, h), cps(h), gain, cut(rstd, h), ALU.mult, ALU.mult))
                        link(nc.vector.tensor_scalar(cut(dst, h), cut(tmp, h), shift, None, ALU.add))


def attention(k, tag, q, key, v, scale, narrow, out, masked=False, regs=None):
    nc, w = k.nc, k.w
    G = 8
    W = G * SEQ
    X = PAIR if regs is not None else 0
    NT = 2 if narrow else 4
    PARTS = 1 if narrow else 2
    NI = NPAIR * PARTS
    extra = lambda i: X and i % PARTS == 0
    scored, lowered, expd, maskd, normed, turned, turned_sb, mixed, mixed_sb, chain = (k.sem(f"{tag}_{s}") for s in (
        "scored", "lowered", "expd", "maskd", "normed", "turned", "turned_sb", "mixed", "mixed_sb", "chain"))
    with ExitStack() as ctx:
        sb = lambda n, s: ctx.enter_context(nc.sbuf_tensor(f"{tag}_{n}", s, F32))
        prob = sb("prob", [P, 2, W + X])
        kept = sb("kept", [P, 2, W]) if masked else prob
        probT = sb("probT", [P, 2, W])
        extraT = sb("extraT", [P, 2, X]) if X else None
        top = sb("top", [P, 2, G + X // SEQ])
        whole = sb("whole", [P, 2, G + X // SEQ])
        block = ctx.enter_context(nc.Block())

        def scores_of(i):
            return k.ps[i % 2][:, 0:W] if narrow else k.ps_all[:, 2 * (i % 2):2 * (i % 2) + 2, 0:256]

        extra_scores, extra_turned = k.ps[0][:, 256:256 + X], k.ps[1][:, 256:256 + X]
        turn_bank = lambda i: k.ps[(2 if narrow else 4) + i % 2]

        def mix(p, b):
            bank = 4 + 2 * (p % 2) + b if narrow else 6 + b
            return k.ps[bank][:, 0:NT * SEQ].rearrange("p (t q) -> p t q", t=NT)

        @block.tensor
        def _(pe):
            def score(i):
                p, part = divmod(i, PARTS)
                if i >= 2:
                    pe.wait_ge(lowered, i - 1)
                    if extra(i - 2):
                        pe.wait_ge(turned_sb, i - 1)
                for b in range(2):
                    tok = slice(p * PAIR + b * SEQ, p * PAIR + (b + 1) * SEQ)
                    if narrow:
                        for hp in range(4):
                            ins = nc.tensor.matmul(k.ps[i % 2][:, hp * P + b * SEQ:hp * P + (b + 1) * SEQ],
                                                   q[:, hp, 2 * p + b].rearrange("r h q -> r (h q)"), key[:, tok],
                                                   start=True, stop=True)
                        continue
                    for t in range(4):
                        for j in range(2 * part, 2 * part + 2):
                            at = (t // 2) * P + b * SEQ
                            ins = nc.tensor.matmul(k.ps[2 * part + j % 2][t % 2 * 64:t % 2 * 64 + 64, at:at + SEQ],
                                                   q[32 * j:32 * j + 32, t, tok], key[32 * j:32 * j + 32, t, tok],
                                                   start=True, stop=True)
                        if extra(i):
                            ins = nc.tensor.matmul(extra_scores[32 * t:32 * t + 32, b * SEQ:(b + 1) * SEQ],
                                                   regs[:, t, 2 * p + b, :], key[:, t, tok], start=True, stop=True)
                ins.then_inc(scored, 1)

            def turn(i):
                pe.wait_ge(normed, i + 1)
                if i >= 2:
                    pe.wait_ge(turned_sb, i - 1)
                for c in range(4):
                    ins = nc.tensor.transpose(turn_bank(i)[:, c * P:(c + 1) * P], kept[:, i % 2, c * P:(c + 1) * P], w["ident"])
                if extra(i):
                    ins = nc.tensor.transpose(extra_turned, prob[:, i % 2, W:], w["ident"])
                ins.then_inc(turned, 1)

            def weigh(i):
                p, part = divmod(i, PARTS)
                pe.wait_ge(turned_sb, i + 1)
                before = 2 if narrow else 1
                if p >= before and part == 0:
                    pe.wait_ge(mixed_sb, p - before + 1)
                for b in range(2):
                    rows = slice(b * SEQ, (b + 1) * SEQ)
                    for t in range(NT):
                        for j in range(4) if narrow else range(2 * part, 2 * part + 2):
                            h = 4 * t + j
                            if narrow:
                                vh, c, half = v[rows, p, :], h // 2, h % 2
                            else:
                                vh, c, half = v[rows, p, 32 * h:32 * h + 32], 2 * (j % 2) + t // 2, t % 2
                            at = c * P + half * SEQ
                            o = mix(p, b)[32 * j:32 * j + 32, t, :]
                            ins = nc.tensor.matmul(o, vh, probT[rows, i % 2, at:at + SEQ], start=True, stop=not X,
                                                   tile_position=(b * SEQ, 32 * j))
                            if X:
                                at = 32 * t + REG * j
                                ins = nc.tensor.matmul(o[:, 0:REG], vh, extraT[rows, p % 2, at:at + REG], start=False,
                                                       stop=True, tile_position=(b * SEQ, 32 * j))
                ins.then_inc(mixed, 1)

            score(0)
            score(1)
            for i in range(NI):
                if i + 2 < NI and not extra(i):
                    score(i + 2)
                turn(i)
                if i:
                    weigh(i - 1)
                if i + 2 < NI and extra(i):
                    score(i + 2)
            weigh(NI - 1)

        @block.vector
        def _(dve):
            link = Count(dve, chain)

            def lower(i):
                dve.wait_ge(scored, i + 1)
                if i >= 2:
                    dve.wait_ge(turned, i - 1)
                    if masked:
                        dve.wait_ge(maskd, i - 1)
                n = 1 if narrow else 2
                four = lambda a: a.rearrange("p (n g k) -> p n g k", n=n, k=SEQ)
                src = four(scores_of(i)) if narrow else scores_of(i).rearrange("p n (g k) -> p n g k", k=SEQ)
                tops = top[:, i % 2, 0:G].rearrange("p (n g) -> p n g", n=n)
                ins = nc.vector.tensor_reduce(tops, src, AX, ALU.max)
                if extra(i):
                    ins = nc.vector.tensor_reduce(top[:, i % 2, G:], groups(extra_scores), AX, ALU.max)
                link(ins)
                ins = nc.vector.tensor_tensor(four(prob[:, i % 2, 0:W]), src,
                                              tops.unsqueeze(3).to_broadcast([P, n, G // n, SEQ]), ALU.subtract)
                if extra(i):
                    ins = nc.vector.tensor_tensor(groups(prob[:, i % 2, W:]), groups(extra_scores),
                                                  spread(top[:, i % 2, G:], SEQ), ALU.subtract)
                ins.then_inc(lowered, 1)

            def norm(i):
                n = W + (X if extra(i) else 0)
                g = n // SEQ
                dve.wait_ge(expd, i + 1)
                link(nc.vector.tensor_reduce(whole[:, i % 2, 0:g], groups(prob[:, i % 2, 0:n]), AX, ALU.add))
                link(nc.vector.reciprocal(whole[:, i % 2, 0:g], whole[:, i % 2, 0:g]))
                if X:
                    ins = nc.vector.tensor_scalar(whole[:, i % 2, 0:G], whole[:, i % 2, 0:G], w["regscale"], None, ALU.mult)
                    if extra(i):
                        ins = nc.vector.tensor_scalar(whole[:, i % 2, G:], whole[:, i % 2, G:], 0.5, None, ALU.mult)
                    link(ins)
                if masked:
                    dve.wait_ge(maskd, i + 1)
                nc.vector.tensor_tensor(groups(kept[:, i % 2, 0:n]), groups(kept[:, i % 2, 0:n]),
                                        spread(whole[:, i % 2, 0:g], SEQ), ALU.mult).then_inc(normed, 1)

            lower(0)
            for i in range(NI):
                if i + 1 < NI:
                    lower(i + 1)
                norm(i)

        @block.gpsimd
        def _(pool):
            for i in range(NI if masked else 0):
                pool.wait_ge(expd, i + 1)
                if i >= 2:
                    pool.wait_ge(turned, i - 1)
                nc.gpsimd.tensor_tensor(groups(kept[:, i % 2, :]), groups(prob[:, i % 2, :]),
                                        w["later"].unsqueeze(1).to_broadcast([P, G, SEQ]), ALU.mult).then_inc(maskd, 1)

        def output(p, act):
            act.wait_ge(mixed, (p + 1) * PARTS)
            for b in range(2):
                ins = nc.scalar.activation(out[:, :, p * PAIR + b * SEQ:p * PAIR + (b + 1) * SEQ], mix(p, b), ACT.Copy)
            ins.then_inc(mixed_sb, 1)

        @block.scalar
        def _(act):
            def exp(i):
                n = W + (X if extra(i) else 0)
                act.wait_ge(lowered, i + 1)
                nc.scalar.activation(prob[:, i % 2, 0:n], prob[:, i % 2, 0:n], ACT.Exp, scale=scale).then_inc(expd, 1)

            exp(0)
            for i in range(NI):
                p, part = divmod(i, PARTS)
                if i + 1 < NI:
                    exp(i + 1)
                act.wait_ge(turned, i + 1)
                if i >= 2:
                    act.wait_ge(mixed, i - 1)
                if extra(i):
                    nc.scalar.activation(extraT[:, p % 2, :], extra_turned, ACT.Copy)
                nc.scalar.activation(probT[:, i % 2, :], turn_bank(i)[:, :], ACT.Copy).then_inc(turned_sb, 1)
                if i >= 1 and (i - 1) % PARTS == PARTS - 1:
                    output((i - 1) // PARTS, act)
            output(NPAIR - 1, act)


def load(k, aps, where):
    nc = k.nc
    loaded = k.sem("loaded")
    with nc.Block() as block:
        @block.sync
        def _(sp):
            for name, _ in PACKS:
                sp.dma_start(k.packs[name][:, :], aps[name]).then_inc(loaded, 16)
            sp.wait_ge(loaded, 16 * len(PACKS))
    for name, _ in PACKS:
        for part, (rows, at, shape) in where[name].items():
            n = int(np.prod(shape))
            ap = k.packs[name][0:rows, at:at + n]
            if len(shape) == 2:
                ap = ap.rearrange("p (a b) -> p a b", b=shape[1])
            if len(shape) == 3:
                ap = ap.rearrange("p (a b c) -> p a b c", b=shape[1], c=shape[2])
            k.w[part] = ap


def setup(k):
    nc, w = k.nc, k.w
    wq = k.keep("wq0", [64, 8, 96])
    wvo = k.keep("wvo0", [P, 2, P])
    rope = k.keep("rope", [64, SEQ])
    decay = k.keep("decay", [P, 2, 2, STATE])
    guide = k.keep("guide", [P, 2])
    foldb = k.keep("foldb", [96, 32], BF16)
    maskrowb = k.keep("maskrowb", [2, P], BF16)
    k.w.update(wq0=wq, wvo0=wvo, rope=rope, decay=decay, guide=guide, foldb=foldb, maskrowb=maskrowb)
    s_pe, s_act, s_dve = k.sem("setup_pe"), k.sem("setup_act"), k.sem("setup_dve")
    with nc.sbuf_tensor("turn", [64, 8], F32) as turn, nc.sbuf_tensor("unit", [P, 4], F32) as unit, \
            nc.sbuf_tensor("ropet", [64, SEQ], F32) as ropet, nc.Block() as block:
        @block.tensor
        def _(pe):
            for h in range(8):
                nc.tensor.matmul(k.ps[0][0:64, 32 * h:32 * h + 32], w["uqT"][:, h, :], w["ukT"][:, h, :], start=True, stop=True)
            for h in range(8):
                j, t = h % 4, h // 4
                ins = nc.tensor.matmul(k.ps[1][32 * j:32 * j + 32, t * P:(t + 1) * P], w["uvT"][:, h, :], w["wo"][:, h, :],
                                       start=True, stop=True)
            ins.then_inc(s_pe, 1)
            pe.wait_ge(s_act, 1)
            nc.tensor.matmul(k.ps[2][:, 0:1], w["heads8"], unit[:, 0:1], start=True, stop=True).then_inc(s_pe, 1)

        @block.scalar
        def _(act):
            link = Count(act, s_act)
            link(nc.scalar.activation(unit[:, 0:1], w["qg"], ACT.Square))
            act.wait_ge(s_pe, 2)
            link(nc.scalar.activation(unit[:, 1:2], k.ps[2][:, 0:1], ACT.Ln))
            link(nc.scalar.activation(unit[:, 2:3], unit[:, 1:2], ACT.Exp, scale=-0.5))
            for d in range(2):
                link(nc.scalar.activation(decay[:, d], w[f"alog{d}"], ACT.Exp))
            link(nc.scalar.activation(turn[:, 0:1], w["delta"], ACT.Exp, scale=-1.0))
            nc.scalar.activation(wq[:, :, 64:96], k.ps[0][0:64, 0:256].rearrange("p (h c) -> p h c", h=8), ACT.Copy)
            link(nc.scalar.activation(wvo[:, :, :], k.ps[1][:, 0:256].rearrange("p (t c) -> p t c", t=2), ACT.Copy))
            act.wait_ge(s_dve, 3)
            link(nc.scalar.activation(turn[:, 4:5], turn[:, 3:4], ACT.Sin))
            link(nc.scalar.activation(turn[:, 5:6], turn[:, 2:3], ACT.Sin, scale=3.141592))

        @block.vector
        def _(dve):
            link = Count(dve, s_dve)
            dve.wait_ge(s_act, 6)
            link(nc.vector.tensor_scalar(turn[:, 1:2], turn[:, 0:1], 1.0, None, ALU.add))
            link(nc.vector.reciprocal(turn[:, 2:3], turn[:, 1:2]))
            link(nc.vector.tensor_scalar(turn[:, 3:4], turn[:, 2:3], 2 * 3.141592, -3.141592, ALU.mult, ALU.add))
            link(nc.vector.tensor_scalar(decay[:, :], decay[:, :], -1.0, -1e-20, ALU.mult, ALU.min))
            link(nc.vector.scalar_tensor_tensor(guide[:, 0:1], w["qg"], 1.0 / 16, unit[:, 2:3], ALU.mult, ALU.mult))
            link(nc.vector.tensor_copy(guide[:, 1:2], guide[:, 0:1]))
            link(nc.vector.tensor_copy(foldb[:, :], w["fold"]))
            link(nc.vector.tensor_copy(maskrowb[:, :], w["maskrow"]))
            link(nc.vector.tensor_copy(wq[:, :, 0:64], w["qr4"]))
            dve.wait_ge(s_act, 9)
            link(nc.vector.tensor_tensor(turn[:, 6:7], turn[:, 5:6], turn[:, 5:6], ALU.mult))
            link(nc.vector.tensor_scalar(turn[:, 7:8], turn[:, 6:7], -2.0, 1.0, ALU.mult, ALU.add))
            link(nc.vector.tensor_scalar(ropet[:, :], w["ropeU"], turn[:, 7:8], None, ALU.mult))
            link(nc.vector.scalar_tensor_tensor(rope[:, :], w["ropeW"], turn[:, 4:5], ropet[:, :], ALU.mult, ALU.add))


def attn0(k):
    nc, w, X = k.nc, k.w, k.X
    with ExitStack() as ctx:
        sb = lambda n, s: ctx.enter_context(nc.sbuf_tensor(f"a0_{n}", s, F32))
        lat, Q, K, V, O = sb("lat", [64, CH]), sb("q", [96, 4, BCH, 2, SEQ]), sb("k", [96, CH]), sb("v", [P, NPAIR, 32]), sb("o", [P, 2, CH])
        with nc.sbuf_tensor("a0_soft", [64, 2, CH], F32) as soft, nc.sbuf_tensor("a0_kr", [64, CH], F32) as kr:
            raw, latd, bounded, logd, turned, vdone, folded = (k.sem(f"a0_{s}") for s in (
                "raw", "latd", "bounded", "logd", "turned", "vdone", "folded"))
            chain, achain = k.sem("a0_chain"), k.sem("a0_achain")
            table = w["rope"][:, :].unsqueeze(1).to_broadcast([64, BCH, SEQ])
            bank = lambda i: k.ps[i % 4]
            with nc.Block() as block:
                @block.tensor
                def _(pe):
                    nc.tensor.matmul(k.ps[4][0:64, :], w["wdq"], X[:, :], start=True, stop=True).then_inc(latd, 1)
                    nc.tensor.matmul(bank(0)[0:96, :], w["wkv"], X[:, :], start=True, stop=True).then_inc(raw, 1)
                    for p in range(NPAIR):
                        ins = nc.tensor.matmul(k.ps[5][:, 32 * p:32 * p + 32], X[:, p * PAIR:(p + 1) * PAIR], w["wkv"][:, 64:96],
                                               start=True, stop=True)
                    ins.then_inc(vdone, 1)
                    pe.wait_ge(latd, 2)
                    for h in range(8):
                        if h >= 3:
                            pe.wait_ge(turned, h - 2)
                        nc.tensor.matmul(bank(h + 1)[0:96, :], w["wq0"][:, h, :], lat[:, :], start=True, stop=True).then_inc(raw, 1)
                    pe.wait_ge(turned, 1)
                    nc.tensor.matmul(k.ps[6][0:64, :], w["fold64"], kr[:, :], start=True, stop=True).then_inc(folded, 1)

                @block.scalar
                def _(act):
                    act.wait_ge(latd, 1)
                    nc.scalar.activation(lat[:, :], k.ps[4][0:64, :], ACT.Copy).then_inc(latd, 1)
                    link = Count(act, achain)
                    for i in range(9):
                        dst = groups(K[64:96, :]) if i == 0 else Q[64:96, (i - 1) // 2, :, (i - 1) % 2, :]
                        act.wait_ge(bounded, i + 1)
                        link(nc.scalar.activation(soft[:, i % 2, :], soft[:, i % 2, :], ACT.Exp))
                        nc.scalar.activation(dst, groups(bank(i)[64:96, :]), ACT.Copy)
                        nc.scalar.activation(soft[:, i % 2, :], soft[:, i % 2, :], ACT.Ln, bias=1.0).then_inc(logd, 1)
                    act.wait_ge(vdone, 1)
                    nc.scalar.activation(V[:, :, :], k.ps[5][:, 0:P].rearrange("p (n c) -> p n c", c=32), ACT.Copy)
                    act.wait_ge(folded, 1)
                    nc.scalar.activation(K[0:64, :], k.ps[6][0:64, :], ACT.Copy)

                @block.vector
                def _(dve):
                    link = Count(dve, chain)

                    def bound(i):
                        dve.wait_ge(raw, i + 1)
                        nc.vector.tensor_scalar(soft[:, i % 2, :], bank(i)[0:64, :], 40.0, None, ALU.min).then_inc(bounded, 1)

                    bound(0)
                    for i in range(9):
                        if i + 1 < 9:
                            bound(i + 1)
                        dve.wait_ge(logd, i + 1)
                        link(nc.vector.tensor_tensor(soft[:, i % 2, :], bank(i)[0:64, :], soft[:, i % 2, :], ALU.max))
                        dst = groups(kr[:, :]) if i == 0 else Q[0:64, (i - 1) // 2, :, (i - 1) % 2, :]
                        ins = nc.vector.tensor_tensor(dst, groups(soft[:, i % 2, :]), table, ALU.mult)
                        ins.then_inc(turned, 1)
                        dve.wait_ge(turned, i + 1)
        attention(k, "a0a", Q, K, V, float(96 ** -0.5), True, O)
        done = k.sem("a0_out")
        with nc.Block() as block:
            @block.tensor
            def _(pe):
                for t in range(2):
                    nc.tensor.matmul(k.ps[7][:, :], w["wvo0"][:, t, :], O[:, t, :], start=t == 0, stop=t == 1)
    layer_norm(k, "a0n", [(X, None, None)], total={"z": k.Z, "psum": k.ps[7], "parts": [X]})


def moe(k):
    nc, w, X = k.nc, k.w, k.X
    sent, picked, gated, gates_sb, hidden, scaled = (k.sem(f"moe_{s}") for s in (
        "sent", "picked", "gated", "gates_sb", "hidden", "scaled"))
    NT = 2 * EXPERTS
    with ExitStack() as ctx:
        sb = lambda n, s, dt=F32: ctx.enter_context(nc.sbuf_tensor(f"moe_{n}", s, dt))
        weight, pick = sb("weight", [P, 256]), sb("pick", [P, 256], I32)
        mine = sb("mine", [P, EXPERTS, 256])
        gate, H = sb("gate", [P, EXPERTS, CH]), sb("h", [P, 4, CH])
        block = ctx.enter_context(nc.Block())
        cols = bass.ds(k.chunk * 256, 256)

        @block.sync
        def _(sp):
            sp.dma_start(weight[:, :], k.aps["gatew"][:, cols]).then_inc(sent, 16)
            sp.dma_start(pick[:, :], k.aps["pick"][:, cols]).then_inc(sent, 16)

        @block.tensor
        def _(pe):
            def hide(i):
                if i >= 4:
                    pe.wait_ge(scaled, i - 3)
                nc.tensor.matmul(k.ps[i % 4][:, :], w["pin"][:, i * P:(i + 1) * P], X[:, :], start=True, stop=True).then_inc(hidden, 1)

            hide(0)
            hide(1)
            for e in range(EXPERTS):
                pe.wait_ge(picked, e + 1)
                if e >= 2:
                    pe.wait_ge(gates_sb, e - 1)
                for s in range(2):
                    rows = slice(64 * s, 64 * s + 64)
                    ins = nc.tensor.matmul(k.ps[4 + 2 * (e % 2) + s][:, 0:256], w["ones"][rows], mine[rows, e, :],
                                           start=True, stop=True, tile_position=(64 * s, 0))
                ins.then_inc(gated, 1)
            pe.wait_ge(gates_sb, EXPERTS)
            for i in range(NT):
                if i + 2 < NT:
                    hide(i + 2)
                pe.wait_ge(scaled, i + 1)
                nc.tensor.matmul(k.ps[7][:, :], w["pout"][:, i // 2, i % 2, :], H[:, i % 4, :], start=i == 0, stop=i == NT - 1)

        @block.scalar
        def _(act):
            for e in range(EXPERTS):
                act.wait_ge(gated, e + 1)
                b = 4 + 2 * (e % 2)
                dst = gate[:, e, :].rearrange("p (n s q) -> p s n q", s=2, q=SEQ)
                for s in range(2):
                    ins = nc.scalar.activation(dst[:, s], groups(k.ps[b + s][:, 0:256]), ACT.Copy)
                ins.then_inc(gates_sb, 1)

        @block.vector
        def _(dve):
            dve.wait_ge(sent, 32)
            for e in range(EXPERTS):
                nc.vector.scalar_tensor_tensor(mine[:, e, :], pick[:, :], float(e), weight[:, :], ALU.is_equal,
                                               ALU.mult).then_inc(picked, 1)
            for i in range(NT):
                dve.wait_ge(hidden, i + 1)
                dve.wait_ge(gates_sb, i // 2 + 1)
                nc.vector.scalar_tensor_tensor(H[:, i % 4, :], k.ps[i % 4][:, :], 0.0, gate[:, i // 2, :], ALU.max,
                                               ALU.mult).then_inc(scaled, 1)
    layer_norm(k, "moen", [(X, None, None)], total={"z": k.Z, "psum": k.ps[7], "parts": [X]})


def ffn(k):
    nc, w, X = k.nc, k.w, k.X
    T = CH // P
    with ExitStack() as ctx:
        sb = lambda n, s, dt=F32: ctx.enter_context(nc.sbuf_tensor(f"ffn_{n}", s, dt))
        L, hot, eq, hot2 = (sb(n, [P, T, EXPERTS]) for n in ("l", "hot", "eq", "hot2"))
        best, second, pr, ex = (sb(n, [P, T]) for n in ("best", "second", "pr", "ex"))
        G = sb("g", [P, EXPERTS, T])
        gate, S, H, O, acc = (sb("gate", [P, EXPERTS, CH]), sb("s", [P, 2, CH]), sb("h", [P, 2, 4, CH]), sb("o", [P, 2, CH]),
                              sb("acc", [P, CH]))
        logits, chain, raised, chosen, gated, gates_sb = (k.sem(f"ffn_{s}") for s in (
            "logits", "chain", "raised", "chosen", "gated", "gates_sb"))
        with nc.Block() as block:
            @block.tensor
            def _(pe):
                for t in range(T):
                    ins = nc.tensor.matmul(k.ps[0][:, 8 * t:8 * t + 8], X[:, t * P:(t + 1) * P], w["router"], start=True, stop=True)
                ins.then_inc(logits, 1)
                pe.wait_ge(chosen, 1)
                for e in range(EXPERTS):
                    if e >= 2:
                        pe.wait_ge(gates_sb, e - 1)
                    for t in range(T):
                        ins = nc.tensor.matmul(k.ps[1 + e % 2][:, t * P:(t + 1) * P], G[:, e, t:t + 1].to_broadcast([P, P]),
                                               w["ident"], start=True, stop=True)
                    ins.then_inc(gated, 1)

            @block.scalar
            def _(act):
                act.wait_ge(chain, 13)
                nc.scalar.activation(ex[:, :], ex[:, :], ACT.Exp).then_inc(raised, 1)
                for e in range(EXPERTS):
                    act.wait_ge(gated, e + 1)
                    nc.scalar.activation(gate[:, e, :], k.ps[1 + e % 2][:, :], ACT.Copy).then_inc(gates_sb, 1)

            @block.vector
            def _(dve):
                link = Count(dve, chain)
                prio = w["prio"].unsqueeze(1).to_broadcast([P, T, EXPERTS])
                tt, full = nc.vector.tensor_tensor, (lambda a: spread(a[:, :], EXPERTS))

                def first_of(m, onehot):
                    link(nc.vector.tensor_reduce(m[:, :], L[:, :, :], AX, ALU.max))
                    link(tt(eq[:, :, :], L[:, :, :], full(m), ALU.is_equal))
                    link(tt(eq[:, :, :], eq[:, :, :], prio, ALU.mult))
                    link(nc.vector.tensor_reduce(pr[:, :], eq[:, :, :], AX, ALU.max))
                    link(tt(onehot[:, :, :], prio, full(pr), ALU.is_equal))

                dve.wait_ge(logits, 1)
                link(tt(L[:, :, :], k.ps[0][:, 0:8 * T].rearrange("p (t e) -> p t e", e=EXPERTS),
                        w["router_b"].unsqueeze(1).to_broadcast([P, T, EXPERTS]), ALU.add))
                first_of(best, hot)
                link(nc.vector.scalar_tensor_tensor(L[:, :, :], hot[:, :, :], -BIG, L[:, :, :], ALU.mult, ALU.add))
                first_of(second, hot2)
                link(tt(ex[:, :], second[:, :], best[:, :], ALU.subtract))
                dve.wait_ge(raised, 1)
                link(nc.vector.tensor_scalar(best[:, :], ex[:, :], 1.0, None, ALU.add))
                link(nc.vector.reciprocal(best[:, :], best[:, :]))
                link(tt(ex[:, :], ex[:, :], best[:, :], ALU.mult))
                link(tt(hot[:, :, :], hot[:, :, :], full(best), ALU.mult))
                link(tt(hot2[:, :, :], hot2[:, :, :], full(ex), ALU.mult))
                tt(G[:, :, :].rearrange("p e t -> p t e"), hot[:, :, :], hot2[:, :, :], ALU.add).then_inc(chosen, 1)

        up, silud, hidden, down, weighed, summed = (k.sem(f"ffn_{s}") for s in (
            "up", "silud", "hidden", "down", "weighed", "summed"))
        with nc.Block() as block:
            @block.tensor
            def _(pe):
                def give(e):
                    pe.wait_ge(hidden, 4 * e + 4)
                    if e >= 2:
                        pe.wait_ge(weighed, e - 1)
                    for f in range(4):
                        ins = nc.tensor.matmul(k.ps[4 + e % 2][:, :], w["w2"][:, e, f, :], H[:, e % 2, f, :], start=f == 0, stop=f == 3)
                    ins.then_inc(down, 1)

                for e in range(EXPERTS):
                    for f in range(4):
                        i = 4 * e + f
                        if i >= 2:
                            pe.wait_ge(hidden, i - 1)
                        for half in range(2):
                            at = e * 1024 + (4 * half + f) * P
                            ins = nc.tensor.matmul(k.ps[2 * half + i % 2][:, :], w["w1"][:, at:at + P], X[:, :], start=True, stop=True)
                        ins.then_inc(up, 1)
                    if e:
                        give(e - 1)
                give(EXPERTS - 1)

            @block.scalar
            def _(act):
                for i in range(4 * EXPERTS):
                    e, f = divmod(i, 4)
                    act.wait_ge(up, i + 1)
                    if i >= 2:
                        act.wait_ge(hidden, i - 1)
                    nc.scalar.activation(S[:, i % 2, :], k.ps[i % 2][:, :], ACT.Silu, bias=w["b1"][:, e, f:f + 1]).then_inc(silud, 1)
                nc.scalar.preload_act_table_set("natural_log_exp_and_others")

            @block.vector
            def _(dve):
                def weigh(e):
                    dve.wait_ge(down, e + 1)
                    if e >= 2:
                        dve.wait_ge(summed, e - 1)
                    nc.vector.scalar_tensor_tensor(O[:, e % 2, :], k.ps[4 + e % 2][:, :], w["b2"][:, e:e + 1], gate[:, e, :],
                                                   ALU.add, ALU.mult).then_inc(weighed, 1)

                for e in range(EXPERTS):
                    if e >= 2:
                        dve.wait_ge(down, e - 1)
                    for f in range(4):
                        i = 4 * e + f
                        dve.wait_ge(silud, i + 1)
                        nc.vector.scalar_tensor_tensor(H[:, e % 2, f, :], k.ps[2 + i % 2][:, :], w["b1"][:, e, 4 + f:5 + f],
                                                       S[:, i % 2, :], ALU.add, ALU.mult).then_inc(hidden, 1)
                    if e:
                        weigh(e - 1)
                weigh(EXPERTS - 1)

            @block.gpsimd
            def _(pool):
                for e in range(EXPERTS):
                    pool.wait_ge(weighed, e + 1)
                    if e == 0:
                        nc.gpsimd.tensor_copy(acc[:, :], O[:, 0, :]).then_inc(summed, 1)
                    else:
                        pool.wait_ge(summed, e)
                        nc.gpsimd.tensor_tensor(acc[:, :], acc[:, :], O[:, e % 2, :], ALU.add).then_inc(summed, 1)
        layer_norm(k, "ffnn", [(X, None, None)], total={"z": k.Z, "psum": acc, "parts": [X]})


def mamba(k):
    nc, w, X = k.nc, k.w, k.X
    with ExitStack() as ctx:
        sb = lambda n, s, dt=F32: ctx.enter_context(nc.sbuf_tensor(f"mb_{n}", s, dt))
        U, ZS = sb("u", [P, 2, 2, CH]), sb("zs", [P, 2, 2, CH])
        back = lambda ap: groups(ap)[:, :, ::-1]
        turned, cleared, inx, inz, padded, convd, chain, actd = (k.sem(f"mb_{s}") for s in (
            "turned", "cleared", "inx", "inz", "padded", "convd", "chain", "actd"))
        with nc.sbuf_tensor("mb_xr", [P, CH], F32) as XR, nc.sbuf_tensor("mb_pad", [P, 4, BCH, SEQ + 3], F32) as pad, \
                nc.sbuf_tensor("mb_conv", [P, 2, CH], F32) as conv, nc.Block() as block:
            @block.tensor
            def _(pe):
                for i in range(4):
                    d, t = divmod(i, 2)
                    if i == 2:
                        pe.wait_ge(turned, 1)
                    src = XR if d else X
                    nc.tensor.matmul(k.ps[i][:, :], w["inT"][:, t * P:(t + 1) * P], src[:, :], start=True, stop=True).then_inc(inx, 1)
                    nc.tensor.matmul(k.ps[4 + i][:, :], w["inT"][:, (2 + t) * P:(3 + t) * P], src[:, :], start=True,
                                     stop=True).then_inc(inz, 1)

            @block.gpsimd
            def _(pool):
                nc.gpsimd.memset(pad[:, :, :, 0:3].rearrange("p i b l -> p (i b) l"), 0.0).then_inc(cleared, 1)

            @block.scalar
            def _(act):
                for i in range(4):
                    act.wait_ge(inx, i + 1)
                    nc.scalar.activation(pad[:, i, :, 3:], groups(k.ps[i][:, :]), ACT.Copy).then_inc(padded, 1)
                for i in range(4):
                    d, t = divmod(i, 2)
                    act.wait_ge(inz, i + 1)
                    nc.scalar.activation(ZS[:, d, t, :], k.ps[4 + i][:, :], ACT.Silu)
                for i in range(4):
                    d, t = divmod(i, 2)
                    act.wait_ge(convd, i + 1)
                    nc.scalar.activation(U[:, d, t, :], conv[:, i % 2, :], ACT.Silu, bias=w[f"convb{d}"][:, t:t + 1]).then_inc(actd, 1)
                nc.scalar.preload_act_table_set("natural_log_exp_and_others")

            @block.vector
            def _(dve):
                link = Count(dve, chain)
                nc.vector.tensor_copy(groups(XR[:, :]), back(X[:, :])).then_inc(turned, 1)
                dve.wait_ge(cleared, 1)
                for i in range(4):
                    d, t = divmod(i, 2)
                    dve.wait_ge(padded, i + 1)
                    if i >= 2:
                        dve.wait_ge(actd, i - 1)
                    cw, dst = w[f"convw{d}"], groups(conv[:, i % 2, :])
                    link(nc.vector.tensor_scalar(dst, pad[:, i, :, 0:SEQ], cw[:, t, 0:1], None, ALU.mult))
                    for j in range(1, 4):
                        ins = nc.vector.scalar_tensor_tensor(dst, pad[:, i, :, j:j + SEQ], cw[:, t, j:j + 1], dst, ALU.mult, ALU.add)
                        if j < 3:
                            link(ins)
                    ins.then_inc(convd, 1)

        DT, DU = sb("dt", [P, 2, 2, CH]), sb("du", [P, 2, 2, CH])
        BC = sb("bc", [96, 2, CH], BF16)
        xproj, cut, rates, rated, soft = (k.sem(f"mb_{s}") for s in ("xproj", "cut", "rates", "rated", "soft"))
        bchain, achain = k.sem("mb_bchain"), k.sem("mb_achain")
        with nc.sbuf_tensor("mb_low", [104, 2, CH], F32) as low, nc.sbuf_tensor("mb_mid", [96, 2, CH], BF16) as mid, nc.Block() as block:
            @block.tensor
            def _(pe):
                for d in range(2):
                    for t in range(2):
                        ins = nc.tensor.matmul(k.ps[d][0:104, :], w[f"xproj{d}"][:, t, :], U[:, d, t, :], start=t == 0, stop=t == 1)
                    ins.then_inc(xproj, 1)
                for d in range(2):
                    pe.wait_ge(cut, d + 1)
                    for t in range(2):
                        nc.tensor.matmul(k.ps[2 + 2 * d + t][:, :], w[f"dtw{d}"][96:104, t * P:(t + 1) * P], low[96:104, d, :],
                                         start=True, stop=True, tile_position=(96, 0)).then_inc(rates, 1)

            @block.scalar
            def _(act):
                for d in range(2):
                    act.wait_ge(xproj, d + 1)
                    nc.scalar.activation(low[96:104, d, :], k.ps[d][96:104, :], ACT.Copy).then_inc(cut, 1)
                link = Count(act, achain)
                for i in range(4):
                    d, t = divmod(i, 2)
                    act.wait_ge(rated, i + 1)
                    link(nc.scalar.activation(DT[:, d, t, :], DT[:, d, t, :], ACT.Exp))
                    nc.scalar.activation(DT[:, d, t, :], DT[:, d, t, :], ACT.Ln, bias=1.0).then_inc(soft, 1)

            @block.vector
            def _(dve):
                link = Count(dve, bchain)
                for d in range(2):
                    dve.wait_ge(xproj, d + 1)
                    link(nc.vector.tensor_copy(BC[:, d, :], k.ps[d][0:96, :]))
                    link(nc.vector.tensor_tensor(low[0:96, d, :], k.ps[d][0:96, :], BC[:, d, :], ALU.subtract))
                    nc.vector.tensor_copy(BC[32:64, d, :], low[32:64, d, :])
                    link(nc.vector.tensor_copy(mid[64:96, d, :], low[64:96, d, :]))
                    nc.vector.tensor_tensor(BC[64:96, d, :], low[64:96, d, :], mid[64:96, d, :], ALU.subtract)
                    for t in range(2):
                        i = 2 * d + t
                        dve.wait_ge(rates, i + 1)
                        nc.vector.tensor_scalar(DT[:, d, t, :], k.ps[2 + i][:, :], w[f"dtb{d}"][:, t:t + 1], 40.0, ALU.add,
                                                ALU.min).then_inc(rated, 1)
                for i in range(4):
                    d, t = divmod(i, 2)
                    dve.wait_ge(soft, i + 1)
                    link(nc.vector.scalar_tensor_tensor(DT[:, d, t, :], k.ps[2 + i][:, :], w[f"dtb{d}"][:, t:t + 1], DT[:, d, t, :],
                                                        ALU.add, ALU.max))
                    link(nc.vector.tensor_tensor(DU[:, d, t, :], DT[:, d, t, :], U[:, d, t, :], ALU.mult))
                    nc.vector.memset(DT[:, d, t, ::SEQ], BIG)

        NI = 2 * STATE
        ins_rep, outs_rep, in_sb, decayed, fed_in, ran, read, added = (k.sem(f"mb_{s}") for s in (
            "ins_rep", "outs_rep", "in_sb", "decayed", "fed_in", "ran", "read", "added"))
        with nc.sbuf_tensor("mb_da", [P, 2, 2 * CH], F32) as dA, nc.sbuf_tensor("mb_dbu", [P, 2, 2 * CH], F32) as dBu, \
                nc.sbuf_tensor("mb_st", [P, 2 * CH], F32) as st, nc.sbuf_tensor("mb_hc", [P, 2, 2 * CH], F32) as hC, \
                nc.sbuf_tensor("mb_br", [P, 2, CH], F32) as bR, nc.Block() as block:
            @block.tensor
            def _(pe):
                def rep_in(i):
                    d, n = divmod(i, STATE)
                    if i >= 2:
                        pe.wait_ge(in_sb, i - 1)
                    nc.tensor.matmul(k.ps[i % 2][:, :], w["foldb"][:, n:n + 1].to_broadcast([96, P]), BC[:, d, :], start=True,
                                     stop=True).then_inc(ins_rep, 1)

                def rep_out(i):
                    d, n = divmod(i, STATE)
                    if i >= 2:
                        pe.wait_ge(read, i - 1)
                    nc.tensor.matmul(k.ps[2 + i % 2][:, :], w["foldb"][:, 16 + n:17 + n].to_broadcast([96, P]), BC[:, d, :],
                                     start=True, stop=True).then_inc(outs_rep, 1)

                def add(i):
                    d, n = divmod(i, STATE)
                    pe.wait_ge(read, i + 1)
                    for t in range(2):
                        ins = nc.tensor.matmul(k.ps[4 + 2 * d + t][:, :], w["ident"], hC[:, i % 2, t * CH:(t + 1) * CH],
                                               start=n == 0, stop=n == STATE - 1)
                    ins.then_inc(added, 1)

                for i in range(2):
                    rep_in(i)
                    rep_out(i)
                for i in range(NI):
                    if i + 2 < NI:
                        rep_in(i + 2)
                    if i + 2 < NI:
                        rep_out(i + 2)
                    add(i)

            @block.scalar
            def _(act):
                for i in range(NI):
                    d, n = divmod(i, STATE)
                    act.wait_ge(ins_rep, i + 1)
                    if i >= 2:
                        act.wait_ge(fed_in, i - 1)
                    nc.scalar.activation(bR[:, i % 2, :], k.ps[i % 2][:, :], ACT.Copy).then_inc(in_sb, 1)
                    if i >= 2:
                        act.wait_ge(ran, i - 1)
                    for t in range(2):
                        ins = nc.scalar.activation(dA[:, i % 2, t * CH:(t + 1) * CH], DT[:, d, t, :], ACT.Exp,
                                                   scale=w["decay"][:, d, t, n:n + 1])
                    ins.then_inc(decayed, 1)

            @block.gpsimd
            def _(pool):
                for i in range(NI):
                    d, n = divmod(i, STATE)
                    pool.wait_ge(in_sb, i + 1)
                    if i >= 2:
                        pool.wait_ge(ran, i - 1)
                    nc.gpsimd.tensor_tensor(dBu[:, i % 2, :].rearrange("p (t c) -> p t c", t=2), DU[:, d],
                                            bR[:, i % 2, :].unsqueeze(1).to_broadcast([P, 2, CH]), ALU.mult).then_inc(fed_in, 1)

            @block.vector
            def _(dve):
                for i in range(NI):
                    dve.wait_ge(fed_in, i + 1)
                    dve.wait_ge(decayed, i + 1)
                    if i >= 1:
                        dve.wait_ge(read, i)
                    nc.vector.tensor_tensor_scan(st[:, :], dA[:, i % 2, :], dBu[:, i % 2, :], 0.0, ALU.mult, ALU.add).then_inc(ran, 1)
                    dve.wait_ge(ran, i + 1)
                    dve.wait_ge(outs_rep, i + 1)
                    if i >= 2:
                        dve.wait_ge(added, i - 1)
                    nc.vector.tensor_tensor(hC[:, i % 2, :].rearrange("p (t c) -> p t c", t=2),
                                            st[:, :].rearrange("p (t c) -> p t c", t=2),
                                            k.ps[2 + i % 2][:, :].unsqueeze(1).to_broadcast([P, 2, CH]), ALU.mult).then_inc(read, 1)

        skipped, gatedy, outd, dchain = (k.sem(f"mb_{s}") for s in ("skipped", "gatedy", "outd", "dchain"))
        with nc.Block() as block:
            @block.vector
            def _(dve):
                for i in range(4):
                    d, t = divmod(i, 2)
                    nc.vector.scalar_tensor_tensor(DU[:, d, t, :], U[:, d, t, :], w[f"dskip{d}"][:, t:t + 1], k.ps[4 + i][:, :],
                                                   ALU.mult, ALU.add).then_inc(skipped, 1)
                link = Count(dve, dchain)
                dve.wait_ge(outd, 1)
                link(nc.vector.tensor_tensor(k.Z[:, :], k.ps[0][:, :], X[:, :], ALU.add))
                dve.wait_ge(outd, 2)
                link(nc.vector.tensor_tensor(groups(k.Z[:, :]), groups(k.Z[:, :]), back(k.ps[1][:, :]), ALU.add))

            @block.gpsimd
            def _(pool):
                for i in range(4):
                    d, t = divmod(i, 2)
                    pool.wait_ge(skipped, i + 1)
                    nc.gpsimd.tensor_tensor(DU[:, d, t, :], DU[:, d, t, :], ZS[:, d, t, :], ALU.mult).then_inc(gatedy, 1)

            @block.tensor
            def _(pe):
                for i in range(4):
                    d, t = divmod(i, 2)
                    pe.wait_ge(gatedy, i + 1)
                    ins = nc.tensor.matmul(k.ps[d][:, :], w["outT"][:, t, :], DU[:, d, t, :], start=t == 0, stop=t == 1)
                    if t:
                        ins.then_inc(outd, 1)
    layer_norm(k, "mbn", [(X, None, None)], src=k.Z)


def project(k, tag, jobs):
    nc = k.nc
    done, by_act, by_dve = (k.sem(f"{tag}_{s}") for s in ("done", "by_act", "by_dve"))
    bank = lambda i, dst: k.ps[i % 8][:dst.shape[0], 0:dst.shape[1]]
    with nc.Block() as block:
        @block.tensor
        def _(pe):
            for i, (dst, terms) in enumerate(jobs):
                if i >= 8:
                    pe.wait_ge(by_dve if i % 2 else by_act, (i - 8) // 2 + 1)
                for n, (a, b) in enumerate(terms):
                    ins = nc.tensor.matmul(bank(i, dst), a, b, start=n == 0, stop=n == len(terms) - 1)
                ins.then_inc(done, 1)

        @block.scalar
        def _(act):
            for i in range(0, len(jobs), 2):
                act.wait_ge(done, i + 1)
                nc.scalar.activation(jobs[i][0], bank(i, jobs[i][0]), ACT.Copy).then_inc(by_act, 1)

        @block.vector
        def _(dve):
            for i in range(1, len(jobs), 2):
                dve.wait_ge(done, i + 1)
                nc.vector.tensor_copy(jobs[i][0], bank(i, jobs[i][0])).then_inc(by_dve, 1)


def mha(k, m, tag, x, xn, yn, yrows, masked, xo, parts, outs):
    nc, w = k.nc, k.w
    y = lambda t: t[0:yrows]
    with ExitStack() as ctx:
        sb = lambda n, s: ctx.enter_context(nc.sbuf_tensor(f"{tag}_{n}", s, F32))
        O = sb("o", [P, 4, CH])
        with nc.sbuf_tensor(f"{tag}_q", [P, 4, CH], F32) as Q, nc.sbuf_tensor(f"{tag}_k", [P, 4, CH], F32) as K, \
                nc.sbuf_tensor(f"{tag}_v", [P, NPAIR, 512], F32) as V:
            jobs = [(Q[:, t, :], [(w[m + "wq"][:, t * P:(t + 1) * P], xn[:, :])]) for t in range(4)]
            jobs += [(K[:, t, :], [(w[m + "wk"][:, t * P:(t + 1) * P], y(yn)[:, :])]) for t in range(4)]
            jobs += [(V[:, p, :], [(y(yn)[:, p * PAIR:(p + 1) * PAIR], w[m + "wv"])]) for p in range(NPAIR)]
            project(k, f"{tag}_in", jobs)
            attention(k, f"{tag}_at", Q, K, V, float(32 ** -0.5), False, O, masked=masked)
        with nc.Block() as block:
            @block.tensor
            def _(pe):
                for t in range(4):
                    nc.tensor.matmul(k.ps[7][:, :], w[m + "li1"][:, t, :], O[:, t, :], start=t == 0, stop=t == 3)
    with nc.sbuf_tensor(f"{tag}_hn", [P, CH], F32) as hn, nc.sbuf_tensor(f"{tag}_h", [P, 4, CH], F32) as H:
        layer_norm(k, f"{tag}_n3", [(hn, w[m + "ln3_g"], w[m + "ln3_b"])],
                   total={"z": xo, "psum": k.ps[7], "bias": w[m + "li1_b"], "parts": [x]})
        up, gelud = k.sem(f"{tag}_up"), k.sem(f"{tag}_gelud")
        with nc.Block() as block:
            @block.tensor
            def _(pe):
                for f in range(4):
                    nc.tensor.matmul(k.ps[f][:, :], w[m + "li2"][:, f * P:(f + 1) * P], hn[:, :], start=True, stop=True).then_inc(up, 1)
                for f in range(4):
                    pe.wait_ge(gelud, f + 1)
                    nc.tensor.matmul(k.ps[7][:, :], w[m + "li3"][:, f, :], H[:, f, :], start=f == 0, stop=f == 3)

            @block.scalar
            def _(act):
                for f in range(4):
                    act.wait_ge(up, f + 1)
                    nc.scalar.activation(H[:, f, :], k.ps[f][:, :], ACT.Gelu, bias=w[m + "li2_b"][:, f:f + 1]).then_inc(gelud, 1)
                nc.scalar.preload_act_table_set("natural_log_exp_and_others")
    layer_norm(k, f"{tag}_n4", outs, total={"z": k.Z, "psum": k.ps[7], "bias": w[m + "li3_b"], "parts": [xo] + parts})


def cross(k):
    nc, w, X = k.nc, k.w, k.X
    with ExitStack() as ctx:
        sb = lambda n, s: ctx.enter_context(nc.sbuf_tensor(f"ca_{n}", s, F32))
        x1, x3, xn, yn, xo, context = (sb(n, [P, CH]) for n in ("x1", "x3", "xn", "yn", "xo", "context"))
        sent = k.sem("ca_sent")
        with nc.Block() as block:
            @block.sync
            def _(sp):
                sp.dma_start(context[0:64, :], k.aps["ctxT"][:, bass.ds(k.chunk * CH, CH)]).then_inc(sent, 16)
                sp.wait_ge(sent, 16)
        layer_norm(k, "ca1", [(x1, w["ln1_g"], w["ln1_b"])], src=X)
        layer_norm(k, "ca2", [(xn, w["a1_lnx_g"], w["a1_lnx_b"]), (yn, w["a1_lny_g"], w["a1_lny_b"])], src=x1)
        mha(k, "a1_", "ca3", x1, xn, yn, P, True, xo, [x1], [(x3, w["ln2_g"], w["ln2_b"])])
        layer_norm(k, "ca4", [(xn, w["a2_lnx_g"], w["a2_lnx_b"])], src=x3)
        layer_norm(k, "ca5", [(yn, w["a2_lny_g"], w["a2_lny_b"])], src=context, rows=64)
        mha(k, "a2_", "ca6", x3, xn, yn, 64, False, xo, [x3, X], [(X, None, None)])


def similarity(k):
    nc, w, X = k.nc, k.w, k.X
    names = ("queried", "squared", "summed", "rooted", "aligned", "similar", "kept")
    queried, squared, summed, rooted, aligned, similar, kept = (k.sem(f"si_{s}") for s in names)
    cols = bass.ds(k.chunk * CH, CH)
    with nc.sbuf_tensor("si_sq", [P, CH], F32) as sq, nc.sbuf_tensor("si_r", [P, CH], F32) as root, nc.Block() as block:
        @block.tensor
        def _(pe):
            nc.tensor.matmul(k.ps[0][:, :], w["qnat"], X[:, :], start=True, stop=True).then_inc(queried, 1)
            pe.wait_ge(squared, 1)
            nc.tensor.matmul(k.ps[1][:, :], w["heads8"], sq[:, :], start=True, stop=True).then_inc(summed, 1)
            pe.wait_ge(aligned, 1)
            nc.tensor.matmul(k.ps[2][0:2, :], w["guide"][:, :], root[:, :], start=True, stop=True).then_inc(similar, 1)

        @block.scalar
        def _(act):
            act.wait_ge(queried, 1)
            nc.scalar.activation(sq[:, :], k.ps[0][:, :], ACT.Square).then_inc(squared, 1)
            act.wait_ge(summed, 1)
            nc.scalar.activation(root[:, :], k.ps[1][:, :], ACT.Ln).then_inc(rooted, 1)
            act.wait_ge(rooted, 1)
            nc.scalar.activation(root[:, :], root[:, :], ACT.Exp, scale=-0.5).then_inc(rooted, 1)

        @block.sync
        def _(sp):
            sp.dma_start(k.final[:, cols], X[:, :]).then_inc(kept, 16)
            sp.wait_ge(kept, 16)

        @block.vector
        def _(dve):
            dve.wait_ge(rooted, 2)
            nc.vector.tensor_tensor(root[:, :], root[:, :], k.ps[0][:, :], ALU.mult).then_inc(aligned, 1)
            dve.wait_ge(similar, 1)
            nc.vector.tensor_copy(k.sim[:, cols], k.ps[2][0:2, :])


def last(k):
    nc, w = k.nc, k.w
    Qx = k.keep("qx", [P, 4, BCH, 32])
    seqs = lambda t: t[:, :].rearrange("p (b q) -> p b q", q=SEQ)
    with k.stage():
        chain, cleared = k.sem("cl_chain"), k.sem("cl_cleared")
        with nc.sbuf_tensor("cl_span", [2, 4], F32) as span, nc.Block() as block:
            @block.gpsimd
            def _(pool):
                nc.gpsimd.memset(Qx[:, :, :, :].rearrange("p t b c -> p (t b c)"), 0.0)

            @block.vector
            def _(dve):
                link = Count(dve, chain)
                ts = nc.vector.tensor_scalar
                toks = seqs(k.sim)[:, :, REG:]
                link(nc.vector.tensor_reduce(span[:, 0:1], toks, mybir.AxisListType.XY, ALU.min))
                link(nc.vector.tensor_reduce(span[:, 1:2], toks, mybir.AxisListType.XY, ALU.max))
                link(nc.vector.tensor_tensor(span[:, 2:3], span[:, 1:2], span[:, 0:1], ALU.subtract))
                link(nc.vector.reciprocal(span[:, 3:4], span[:, 2:3]))
                link(ts(k.sim[:, :], k.sim[:, :], span[:, 0:1], span[:, 3:4], ALU.subtract, ALU.mult))
                link(ts(k.sim[:, :], k.sim[:, :], 0.9, None, ALU.is_gt))
                link(nc.vector.memset(seqs(k.sim)[:, :, 0:REG], 1.0))
    with nc.Fori(0, NCH) as chunk:
        with k.stage():
            cols = bass.ds(chunk * CH, CH)
            with ExitStack() as ctx:
                sb = lambda n, s: ctx.enter_context(nc.sbuf_tensor(f"la_{n}", s, F32))
                O, X, Z = sb("o", [P, 4, CH]), k.X, k.Z
                qm, km = (ctx.enter_context(nc.sbuf_tensor(f"la_{n}", [2, CH], BF16)) for n in ("qm", "km"))
                with nc.sbuf_tensor("la_q", [P, 4, CH], F32) as Q, nc.sbuf_tensor("la_k", [P, 4, CH], F32) as K, \
                        nc.sbuf_tensor("la_v", [P, NPAIR, 512], F32) as V:
                    fetched, mchain = k.sem("la_fetched"), k.sem("la_mchain")
                    with nc.Block() as block:
                        @block.sync
                        def _(sp):
                            sp.dma_start(X[:, :], k.final[:, cols]).then_inc(fetched, 16)
                            sp.wait_ge(fetched, 16)

                        @block.vector
                        def _(dve):
                            link = Count(dve, mchain)
                            ts = nc.vector.tensor_scalar
                            ts(qm[:, :], k.sim[:, cols], w["qa"], w["qc"], ALU.mult, ALU.add)
                            link(ts(km[:, :], k.sim[:, cols], w["ka"], w["kc"], ALU.mult, ALU.add))
                            nc.vector.memset(seqs(km)[:, :, 0:REG], 0.0)
                    wide = w["wide"]
                    tile = lambda n, t: wide[:, n, t * P:(t + 1) * P]
                    jobs = [(Q[:, t, :], [(tile(0, t), X[:, :]), (k.w["maskrowb"][:, :], qm[:, :])]) for t in range(4)]
                    jobs += [(K[:, t, :], [(tile(1, t), X[:, :]), (k.w["maskrowb"][:, :], km[:, :])]) for t in range(4)]
                    jobs += [(V[:, p, :], [(X[:, p * PAIR:(p + 1) * PAIR], wide[:, 2, :])]) for p in range(NPAIR)]
                    project(k, "la_in", jobs)
                    with nc.Block() as block:
                        @block.vector
                        def _(dve):
                            for j in range(4):
                                rows = slice(32 * j, 32 * j + 32)
                                src = Q[rows, :, :].rearrange("p t (b q) -> p t b q", q=SEQ)[:, :, :, 0:REG]
                                nc.vector.tensor_scalar(Qx[rows, :, :, REG * j:REG * j + REG], src, w["negclass"][rows],
                                                        None, ALU.add)
                    attention(k, "la_at", Q, K, V, float(8 ** -0.5), False, O, regs=Qx)
                with nc.Block() as block:
                    @block.tensor
                    def _(pe):
                        for t in range(4):
                            nc.tensor.matmul(k.ps[7][:, :], w["proj"][:, t, :], O[:, t, :], start=t == 0, stop=t == 3)
                layer_norm(k, "lan", [(X, None, None)], total={"z": Z, "psum": k.ps[7], "bias": w["projb"], "parts": [X]})
            stored = k.sem("stored")
            with nc.Block() as block:
                @block.sync
                def _(sp):
                    sp.dma_start(k.aps["out"][:, cols], k.X[:, :]).then_inc(stored, 16)
                    sp.wait_ge(stored, 16)


STAGES = [attn0, moe, ffn, mamba, cross, similarity]



def build(nc, where, aps, upto=99):
    with ExitStack() as ctx:
        k = Core(nc, ctx)
        psum = ctx.enter_context(nc.psum_tensor("psum", [P, 8, 512], F32))
        k.ps_all = psum
        k.ps = [psum[:, i, :] for i in range(8)]
        k.packs = {name: k.keep(f"pack_{name}", list(aps[name].shape)) for name, _ in PACKS}
        k.aps = aps
        with k.stage():
            load(k, aps, where)
            setup(k)
        k.X, k.Z = k.keep("X", [P, CH]), k.keep("Z", [P, CH])
        k.final = nc.dram_tensor("between", (P, TOK), F32, kind="Internal").ap()
        k.sim = k.keep("sim", [2, TOK])
        with nc.Fori(0, NCH) as chunk:
            k.chunk = chunk
            with k.stage():
                sent = k.sem("x_sent")
                with nc.Block() as block:
                    @block.sync
                    def _(sp):
                        sp.dma_start(k.X[:, :], aps["xT"][:, bass.ds(chunk * CH, CH)]).then_inc(sent, 16)
                        sp.wait_ge(sent, 16)

                    @block.scalar
                    def _(act):
                        nc.scalar.preload_act_table_set("natural_log_exp_and_others")
            for stage in STAGES[:upto]:
                with k.stage():
                    stage(k)
            if upto < 6:
                with k.stage():
                    stored = k.sem("x_stored")
                    with nc.Block() as block:
                        @block.sync
                        def _(sp):
                            sp.dma_start(aps["out"][:, bass.ds(chunk * CH, CH)], k.X[:, :]).then_inc(stored, 16)
                            sp.wait_ge(stored, 16)
        if upto >= 6:
            last(k)


def kernel(**inputs):
    import concourse.bacc as bacc
    from concourse.bass_utils import run_bass_kernel_spmd

    a = {n: np.asarray(v) for n, v in inputs.items()}
    arrays, where, aps = {}, {}, {}
    for name, parts in PACKS:
        arrays[f"pack_{name}_dram"], where[name] = pack(parts(a))
    arrays["xT_dram"] = np.ascontiguousarray(a["x"].reshape(TOK, P).T)
    arrays["ctxT_dram"] = np.ascontiguousarray(a["ctx_512"].reshape(TOK, 64).T)
    for n, src in (("gatew", a["ctx_512"]), ("pick", a["itok_BxS2xS_0_7"])):
        arrays[f"{n}_dram"] = np.ascontiguousarray(src.reshape(NSEQ // 2, P, SEQ).transpose(1, 0, 2).reshape(P, -1))
    nc = bacc.Bacc("TRN2", target_bir_lowering=False, num_devices=1)
    for n, arr in arrays.items():
        ap = nc.dram_tensor(n, arr.shape, mybir.dt.from_np(arr.dtype), kind="ExternalInput").ap()
        aps[n[:-5].removeprefix("pack_")] = ap
    aps["out"] = nc.dram_tensor("out_dram", (P, TOK), F32, kind="ExternalOutput").ap()
    build(nc, where, aps)
    r = run_bass_kernel_spmd(nc, [arrays], core_ids=[0])
    return np.ascontiguousarray(r.results[0]["out_dram"].T).reshape(NSEQ, SEQ, P)
```

```python
from contextlib import ExitStack, contextmanager

import numpy as np

import concourse.bass as bass
from concourse import mybir

F32 = mybir.dt.float32
F32R = mybir.dt.float32r
BF16 = mybir.dt.bfloat16
I32 = mybir.dt.int32
ALU = mybir.AluOpType
ACT = mybir.ActivationFunctionType
AX = mybir.AxisListType.X

P = 128
SEQ = 64
NSEQ = 32
TOK = SEQ * NSEQ
CH = 512
NCH = TOK // CH
HALF = CH // 2
BCH = CH // SEQ
PAIR = 2 * SEQ
NPAIR = CH // PAIR
BIG = float(2.0 ** 100)
EXPERTS = 8
STATE = 16
REG = 5
ROPE_ORDER = [0, 1, 1, 0]


def rope_tables():
    half = 16
    theta = (np.float32(1.0) / np.float32(10000.0) ** (np.float32(2.0) * np.arange(half, dtype=np.float32) / np.float32(32.0)))
    a = (np.arange(SEQ, dtype=np.float32)[None, :] * theta.astype(np.float32)[:, None]).astype(np.float64)
    c, s = np.cos(a), np.sin(a)
    return np.concatenate([c, c, -s, s]).astype(np.float32), np.concatenate([-s, -s, -c, c]).astype(np.float32)


def constants():
    p = np.arange(P)
    u, w = rope_tables()
    eye = np.eye(P, dtype=np.float32)
    row = np.zeros((2, P), np.float32)
    row[0, p % 32 == 8] = 1
    row[1, p % 32 == 9] = 1
    two = lambda a, b: np.array([[a], [b]], np.float32)
    return {
        "ident": eye,
        "center": eye - np.float32(1 / P),
        "mean": np.full((P, P), 1 / P, np.float32),
        "center64": np.eye(64, dtype=np.float32) - np.float32(1 / 64),
        "mean64": np.full((64, 64), 1 / 64, np.float32),
        "later": (np.arange(SEQ)[None, :] > (p % SEQ)[:, None]).astype(np.float32),
        "ropeU": u, "ropeW": w,
        "ones": np.ones((P, P), np.float32),
        "fold": (np.arange(96)[:, None] % 32 == np.arange(32)[None, :]).astype(np.float32),
        "fold64": (np.arange(64)[:, None] % 32 == np.arange(64)[None, :] % 32).astype(np.float32),
        "heads8": (p[:, None] // 8 == p[None, :] // 8).astype(np.float32),
        "maskrow": row,
        "negclass": np.where(p % 32 == 8, BIG, np.where(p % 32 == 9, -BIG, 0)).astype(np.float32)[:, None],
        "regscale": np.where(p % SEQ < REG, 0.5, 1.0).astype(np.float32)[:, None],
        "prio": np.broadcast_to(EXPERTS - np.arange(EXPERTS, dtype=np.float32), (P, EXPERTS)),
        "eps": np.full((P, 1), 1e-5, np.float32),
        "qa": two(-BIG, BIG), "qc": two(0, -BIG), "ka": two(-1, 1), "kc": two(1, 0),
    }


def tiles(w):
    return w.reshape(-1, P, w.shape[-1]).transpose(1, 0, 2)


def setup_parts(a):
    uq = a["L0_attn_W_uq"].reshape(64, 8, 64)
    qr = a["L0_attn_W_qr"].reshape(64, 8, 2, 16)
    return {
        "qr4": qr[:, :, ROPE_ORDER].reshape(64, 8, 64),
        "uqT": uq.transpose(2, 1, 0),
        "ukT": a["L0_attn_W_uk"].reshape(32, 8, 64).transpose(2, 1, 0),
        "uvT": a["L0_attn_W_uv"].reshape(32, 8, 64).transpose(2, 1, 0),
        "wo": a["L0_attn_W_out"].reshape(8, 64, P).transpose(1, 0, 2),
        "delta": np.concatenate([a["L0_attn_raw_delta"]] * 4)[:, None],
        "alog0": tiles(a["L1_attn_A_log"]),
        "alog1": tiles(a["L1_attn_A_b_log"]),
        "qg": a["L1_ffn_g_info"][0, 0][:, None],
    }


def attn0_parts(a):
    kr = a["L0_attn_W_kr"].reshape(P, 2, 16)
    return {
        "wdq": a["L0_attn_W_dq"],
        "wkv": np.concatenate([kr[:, ROPE_ORDER].reshape(P, 64), a["L0_attn_W_dkv"]], 1),
    }


def ffn_parts(a):
    return {
        "router": a["L0_ffn_router_w"].T,
        "router_b": np.broadcast_to(a["L0_ffn_router_b"], (P, EXPERTS)),
        "b1": a["L0_ffn_b1"].reshape(EXPERTS, 8, P).transpose(2, 0, 1),
        "b2": a["L0_ffn_b2"].T,
    }


def expert_parts(a):
    return {
        "pin": a["L0_xattn_proj_in"].reshape(EXPERTS * 256, P).T,
        "pout": a["L0_xattn_proj_out"].reshape(EXPERTS, P, 2, P).transpose(3, 0, 2, 1).reshape(P, -1),
        "w1": a["L0_ffn_w1"].reshape(EXPERTS * 1024, P).T,
        "w2": a["L0_ffn_w2"].reshape(EXPERTS, P, 4, P).transpose(3, 0, 2, 1).reshape(P, -1),
    }


def mamba_parts(a):
    out = {"inT": a["L1_attn_in_proj_w"].T,
           "outT": a["L1_attn_out_proj_w"].reshape(P, 2, P).transpose(2, 1, 0)}
    for d, (s, dp) in enumerate((("", "D"), ("b", "D_b"))):
        xp = a[f"L1_attn_x_proj_w{s}"]
        bc = xp[8:40]
        out[f"xproj{d}"] = np.concatenate([bc, bc, bc, xp[0:8]]).T.reshape(2, P, 104).transpose(1, 0, 2)
        dt = np.zeros((104, 256), np.float32)
        dt[96:104] = a[f"L1_attn_dt_proj_w{s}"].T
        out[f"dtw{d}"] = dt
        out[f"dtb{d}"] = a[f"L1_attn_dt_proj_b{s}"].reshape(2, P).T
        out[f"convw{d}"] = tiles(a[f"L1_attn_conv_w{s}"])
        out[f"convb{d}"] = a[f"L1_attn_conv_b{s}"].reshape(2, P).T
        out[f"dskip{d}"] = a["L1_attn_" + dp].reshape(2, P).T
    return out


def cross_parts(a):
    x = lambda n: a["L1_xattn_" + n]
    col = lambda n: x(n)[:, None]
    out = {"ln1_g": col("ln1_g"), "ln1_b": col("ln1_b"), "ln2_g": col("ln2_g"), "ln2_b": col("ln2_b")}
    for m in ("a1_", "a2_"):
        for n in ("wq", "wk", "wv"):
            w = x(m + n)
            out[m + n] = w.transpose(1, 0, 2).reshape(w.shape[1], 512)
        out[m + "li1"] = tiles(x(m + "li1_w"))
        out[m + "li2"] = x(m + "li2_w")
        out[m + "li3"] = tiles(x(m + "li3_w"))
        out[m + "li2_b"] = x(m + "li2_b").reshape(4, P).T
        for n in ("li1_b", "li3_b", "lnx_g", "lnx_b", "lny_g", "lny_b", "ln3_g", "ln3_b"):
            out[m + n] = col(m + n)
    return out


def last_parts(a):
    w = a["L1_ffn_W_qkv"].reshape(P, 3, 16, 8)
    wide = np.zeros((P, 3, 16, 32), np.float32)
    wide[..., :8] = w
    proj = np.zeros((16, 32, P), np.float32)
    proj[:, :8] = a["L1_ffn_W_proj"].reshape(16, 8, P)
    return {
        "qnat": w[:, 0].reshape(P, P),
        "wide": wide.reshape(P, 3, 512),
        "proj": tiles(proj.reshape(512, P)),
        "projb": a["L1_ffn_b_proj"][:, None],
    }


SPLIT = 2048
LANDINGS = 4
PACKS = [("const", lambda a: constants()), ("setup", setup_parts), ("attn0", attn0_parts), ("ffn", ffn_parts), ("experts", expert_parts),
         ("mamba", mamba_parts), ("cross", cross_parts), ("last", last_parts)]


def pack(parts):
    where, at = {}, 0
    for name, a in parts.items():
        n = int(np.prod(a.shape[1:]))
        where[name] = (a.shape[0], at, tuple(a.shape[1:]))
        at += n
    whole = np.zeros((P, at), np.float32)
    for name, a in parts.items():
        rows, c, shape = where[name]
        whole[:rows, c:c + int(np.prod(shape))] = a.reshape(rows, -1)
    return whole, where


class Core:

    def __init__(self, nc, ctx):
        self.nc, self.ctx, self.sems, self.w = nc, ctx, [], {}

    def keep(self, name, shape, dt=F32):
        return self.ctx.enter_context(self.nc.sbuf_tensor(name, shape, dt))

    def sem(self, name):
        s = self.stage_ctx.enter_context(self.nc.semaphore(name))
        self.sems.append(s)
        return s

    @contextmanager
    def stage(self):
        with ExitStack() as self.stage_ctx:
            self.sems = []
            yield
            nums = sorted(s.num for s in self.sems)
            runs = [n for n in nums if n - 1 not in nums], [n for n in nums if n + 1 not in nums]
            for a, b in zip(*runs):
                self.nc.gpsimd.sem_clear(range(a, b + 1))
            self.nc.all_engine_barrier()


class Count:

    def __init__(self, eng, sem):
        self.eng, self.sem, self.n = eng, sem, 0

    def __call__(self, ins):
        self.n += 1
        ins.then_inc(self.sem, 1)
        self.eng.wait_ge(self.sem, self.n)


def groups(ap, k=SEQ):
    return ap.rearrange("p (g k) -> p g k", k=k)


def spread(ap, n):
    return ap.unsqueeze(2).to_broadcast([ap.shape[0], ap.shape[1], n])


class Norm:

    def __init__(self, k, ctx, tag, z, outs, rows=P, banks=(0, 1, 2, 3)):
        self.k, self.z, self.outs, self.rows, self.banks = k, z, outs, rows, banks
        self.centered, self.squared, self.meaned, self.logd, self.rooted, self.chain = (k.sem(f"{tag}_{s}") for s in (
            "centered", "squared", "meaned", "logd", "rooted", "chain"))
        self.sq, self.rstd = (ctx.enter_context(k.nc.sbuf_tensor(f"{tag}_{n}", [rows, CH], F32))
                              for n in ("sq", "rstd"))
        self.links = 0

    def cut(self, t, h):
        return t[0:self.rows, h * HALF:(h + 1) * HALF]

    def bank(self, i):
        return self.k.ps[self.banks[i]][0:self.rows, 0:HALF]

    def center(self, pe, h):
        w = self.k.w["center" if self.rows == P else "center64"]
        self.k.nc.tensor.matmul(self.bank(h), w, self.cut(self.z, h), start=True, stop=True).then_inc(self.centered, 1)

    def square(self, act, h):
        act.wait_ge(self.centered, h + 1)
        self.k.nc.scalar.activation(self.cut(self.sq, h), self.bank(h), ACT.Square).then_inc(self.squared, 1)

    def mean(self, pe, h):
        w = self.k.w["mean" if self.rows == P else "mean64"]
        pe.wait_ge(self.squared, h + 1)
        self.k.nc.tensor.matmul(self.bank(2 + h), w, self.cut(self.sq, h), start=True, stop=True).then_inc(self.meaned, 1)

    def root(self, act):
        for h in range(2):
            act.wait_ge(self.meaned, h + 1)
            self.k.nc.scalar.activation(self.cut(self.rstd, h), self.bank(2 + h), ACT.Ln,
                                        bias=self.k.w["eps"][0:self.rows]).then_inc(self.logd, 1)
        for h in range(2):
            act.wait_ge(self.logd, h + 1)
            self.k.nc.scalar.activation(self.cut(self.rstd, h), self.cut(self.rstd, h), ACT.Exp,
                                        scale=-0.5).then_inc(self.rooted, 1)

    def out(self, dve, h):
        vec = self.k.nc.vector
        dve.wait_ge(self.rooted, h + 1)
        for dst, gain, shift in self.outs:
            if gain is None:
                ins = vec.tensor_tensor(self.cut(dst, h), self.bank(h), self.cut(self.rstd, h), ALU.mult)
            else:
                vec.scalar_tensor_tensor(self.cut(dst, h), self.bank(h), gain, self.cut(self.rstd, h), ALU.mult,
                                         ALU.mult).then_inc(self.chain, 1)
                self.links += 1
                dve.wait_ge(self.chain, self.links)
                ins = vec.tensor_scalar(self.cut(dst, h), self.cut(dst, h), shift, None, ALU.add)
        return ins


class Sum:

    def __init__(self, k, tag, z, first, parts, bias=None):
        self.k, self.z, self.first, self.parts, self.bias = k, z, first, parts, bias
        self.summed, self.chain, self.links = k.sem(f"{tag}_summed"), k.sem(f"{tag}_schain"), 0

    def add(self, dve, h):
        vec = self.k.nc.vector
        dst = self.z[:, h * HALF:(h + 1) * HALF]
        for i, part in enumerate(self.parts):
            part = part[:, h * HALF:(h + 1) * HALF]
            if i == 0 and self.bias is not None:
                ins = vec.scalar_tensor_tensor(dst, self.first(h), self.bias, part, ALU.add, ALU.add)
            else:
                ins = vec.tensor_tensor(dst, self.first(h) if i == 0 else dst, part, ALU.add)
            if i + 1 < len(self.parts):
                ins.then_inc(self.chain, 1)
                self.links += 1
                dve.wait_ge(self.chain, self.links)
        ins.then_inc(self.summed, 1)

    def wait(self, eng, h):
        eng.wait_ge(self.summed, h + 1)


def attention(k, tag, q, key, v, scale, narrow, out, masked=False, regs=None, before=None, after=None):
    nc, w = k.nc, k.w
    G = 8
    W = G * SEQ
    X = PAIR if regs is not None else 0
    NT = 2 if narrow else 4
    PARTS = 1 if narrow else 2
    NI = NPAIR * PARTS
    extra = lambda i: X and i % PARTS == 0
    scored, lowered, expd, maskd, normed, turned, turned_sb, added, mixed, mixed_sb, chain = (k.sem(f"{tag}_{s}") for s in (
        "scored", "lowered", "expd", "maskd", "normed", "turned", "turned_sb", "added", "mixed", "mixed_sb", "chain"))
    with ExitStack() as ctx:
        sb = lambda n, s: ctx.enter_context(nc.sbuf_tensor(f"{tag}_{n}", s, F32))
        prob = sb("prob", [P, 2, W + X])
        kept = sb("kept", [P, 2, W]) if masked else prob
        probT = sb("probT", [P, 2, W])
        extraT = sb("extraT", [P, 2, X]) if X else None
        top = sb("top", [P, 2, G + X // SEQ])
        whole = sb("whole", [P, 2, G + X // SEQ])
        block = ctx.enter_context(nc.Block())

        def scores_of(i):
            return k.ps[i % 2][:, 0:W] if narrow else k.ps_all[:, 2 * (i % 2):2 * (i % 2) + 2, 0:256]

        extra_scores, extra_turned = k.ps[0][:, 256:256 + X], k.ps[3][:, 256:256 + X]
        turn_bank = lambda i: k.ps[(2 if narrow else 4) + i % 2]

        def mix(p, b):
            bank = 4 + 2 * (p % 2) + b if narrow else 6 + b
            return k.ps[bank][:, 0:NT * SEQ].rearrange("p (t q) -> p t q", t=NT)

        @block.tensor
        def _(pe):
            def score(i):
                p, part = divmod(i, PARTS)
                if i >= 2:
                    pe.wait_ge(lowered, i - 1)
                if i >= 3 and extra(i - 3):
                    pe.wait_ge(turned_sb, i - 2)
                for b in range(2):
                    tok = slice(p * PAIR + b * SEQ, p * PAIR + (b + 1) * SEQ)
                    if narrow:
                        for hp in range(4):
                            ins = nc.tensor.matmul(k.ps[i % 2][:, hp * P + b * SEQ:hp * P + (b + 1) * SEQ],
                                                   q[:, hp, 2 * p + b].rearrange("r h q -> r (h q)"), key[:, tok],
                                                   start=True, stop=True)
                        continue
                    for t in range(4):
                        for j in range(2 * part, 2 * part + 2):
                            at = (t // 2) * P + b * SEQ
                            ins = nc.tensor.matmul(k.ps[2 * part + j % 2][t % 2 * 64:t % 2 * 64 + 64, at:at + SEQ],
                                                   q[32 * j:32 * j + 32, t, tok], key[32 * j:32 * j + 32, t, tok],
                                                   start=True, stop=True)
                        if extra(i):
                            ins = nc.tensor.matmul(extra_scores[32 * t:32 * t + 32, b * SEQ:(b + 1) * SEQ],
                                                   regs[:, t, 2 * p + b, :], key[:, t, tok], start=True, stop=True)
                ins.then_inc(scored, 1)

            def turn(i):
                pe.wait_ge(normed, i + 1)
                if i >= 2:
                    pe.wait_ge(turned_sb, i - 1)
                for c in range(4):
                    ins = nc.tensor.transpose(turn_bank(i)[:, c * P:(c + 1) * P], kept[:, i % 2, c * P:(c + 1) * P], w["ident"])
                if extra(i):
                    ins = nc.tensor.transpose(extra_turned, prob[:, i % 2, W:], w["ident"])
                ins.then_inc(turned, 1)

            def weigh(i):
                p, part = divmod(i, PARTS)
                pe.wait_ge(added if X else turned_sb, i + 1)
                before = 2 if narrow else 1
                if p >= before and part == 0:
                    pe.wait_ge(mixed_sb, p - before + 1)
                for b in range(2):
                    rows = slice(b * SEQ, (b + 1) * SEQ)
                    for t in range(NT):
                        for j in range(4) if narrow else range(2 * part, 2 * part + 2):
                            h = 4 * t + j
                            if narrow:
                                vh, c, half = v[rows, p, :], h // 2, h % 2
                            else:
                                vh, c, half = v[rows, p, 32 * h:32 * h + 32], 2 * (j % 2) + t // 2, t % 2
                            at = c * P + half * SEQ
                            o = mix(p, b)[32 * j:32 * j + 32, t, :]
                            ins = nc.tensor.matmul(o, vh, probT[rows, i % 2, at:at + SEQ], start=True, stop=True,
                                                   tile_position=(b * SEQ, 32 * j))
                ins.then_inc(mixed, 1)

            if before:
                before.products(pe)
                before.wait_queries(pe)
            score(0)
            score(1)
            if before:
                before.wait_values(pe)
            for i in range(NI):
                if i + 2 < NI:
                    score(i + 2)
                turn(i)
                if i:
                    weigh(i - 1)
            weigh(NI - 1)
            pe.wait_ge(mixed_sb, NPAIR)
            after.tensor(pe)

        @block.vector
        def _(dve):
            link = Count(dve, chain)

            def lower(i):
                dve.wait_ge(scored, i + 1)
                if i >= 2:
                    dve.wait_ge(turned, i - 1)
                    if masked:
                        dve.wait_ge(maskd, i - 1)
                n = 1 if narrow else 2
                four = lambda a: a.rearrange("p (n g k) -> p n g k", n=n, k=SEQ)
                src = four(scores_of(i)) if narrow else scores_of(i).rearrange("p n (g k) -> p n g k", k=SEQ)
                tops = top[:, i % 2, 0:G].rearrange("p (n g) -> p n g", n=n)
                ins = nc.vector.tensor_reduce(tops, src, AX, ALU.max)
                if extra(i):
                    ins = nc.vector.tensor_reduce(top[:, i % 2, G:], groups(extra_scores), AX, ALU.max)
                link(ins)
                ins = nc.vector.tensor_tensor(four(prob[:, i % 2, 0:W]), src,
                                              tops.unsqueeze(3).to_broadcast([P, n, G // n, SEQ]), ALU.subtract)
                if extra(i):
                    ins = nc.vector.tensor_tensor(groups(prob[:, i % 2, W:]), groups(extra_scores),
                                                  spread(top[:, i % 2, G:], SEQ), ALU.subtract)
                ins.then_inc(lowered, 1)

            def norm(i):
                n = W + (X if extra(i) else 0)
                g = n // SEQ
                dve.wait_ge(expd, i + 1)
                link(nc.vector.tensor_reduce(whole[:, i % 2, 0:g], groups(prob[:, i % 2, 0:n]), AX, ALU.add))
                link(nc.vector.reciprocal(whole[:, i % 2, 0:g], whole[:, i % 2, 0:g]))
                if X:
                    ins = nc.vector.tensor_scalar(whole[:, i % 2, 0:G], whole[:, i % 2, 0:G], w["regscale"], None, ALU.mult)
                    if extra(i):
                        ins = nc.vector.tensor_scalar(whole[:, i % 2, G:], whole[:, i % 2, G:], 0.5, None, ALU.mult)
                    link(ins)
                if masked:
                    dve.wait_ge(maskd, i + 1)
                nc.vector.tensor_tensor(groups(kept[:, i % 2, 0:n]), groups(kept[:, i % 2, 0:n]),
                                        spread(whole[:, i % 2, 0:g], SEQ), ALU.mult).then_inc(normed, 1)

            if before:
                before.copies_by_vector(dve)
            lower(0)
            for i in range(NI):
                if i + 1 < NI:
                    lower(i + 1)
                norm(i)
            after.vector(dve)

        @block.sync
        def _(sp):
            after.sync(sp)

        @block.gpsimd
        def _(pool):
            for i in range(NI if masked else 0):
                pool.wait_ge(expd, i + 1)
                if i >= 2:
                    pool.wait_ge(turned, i - 1)
                nc.gpsimd.tensor_tensor(groups(kept[:, i % 2, :]), groups(prob[:, i % 2, :]),
                                        w["later"].unsqueeze(1).to_broadcast([P, G, SEQ]), ALU.mult).then_inc(maskd, 1)
            for i in range(NI if X else 0):
                p, part = divmod(i, PARTS)
                main = probT[:, i % 2, :].rearrange("p (j t q) -> p j t q", j=2, q=SEQ)[:, :, :, 0:REG]
                more = extraT[:, p % 2, :].rearrange("p (t c) -> p t c", t=4)[:, :, 2 * REG * part:2 * REG * (part + 1)]
                pool.wait_ge(turned_sb, i + 1)
                nc.gpsimd.tensor_tensor(main, main, more.rearrange("p t (j r) -> p j t r", r=REG), ALU.add).then_inc(added, 1)

        def output(p, act):
            act.wait_ge(mixed, (p + 1) * PARTS)
            for b in range(2):
                ins = nc.scalar.activation(out[:, :, p * PAIR + b * SEQ:p * PAIR + (b + 1) * SEQ], mix(p, b), ACT.Copy)
            ins.then_inc(mixed_sb, 1)

        @block.scalar
        def _(act):
            def exp(i):
                n = W + (X if extra(i) else 0)
                act.wait_ge(lowered, i + 1)
                nc.scalar.activation(prob[:, i % 2, 0:n], prob[:, i % 2, 0:n], ACT.Exp, scale=scale).then_inc(expd, 1)

            if before:
                before.copies_by_scalar(act)
            exp(0)
            for i in range(NI):
                p, part = divmod(i, PARTS)
                if i + 1 < NI:
                    exp(i + 1)
                act.wait_ge(turned, i + 1)
                if i >= 2:
                    act.wait_ge(mixed, i - 1)
                if extra(i):
                    nc.scalar.activation(extraT[:, p % 2, :], extra_turned, ACT.Copy)
                nc.scalar.activation(probT[:, i % 2, :], turn_bank(i)[:, :], ACT.Copy).then_inc(turned_sb, 1)
                if i >= 1 and (i - 1) % PARTS == PARTS - 1:
                    output((i - 1) // PARTS, act)
            output(NPAIR - 1, act)
            after.scalar(act)


FIRST = ("const", "setup", "attn0", "ffn")


def load(k):
    nc = k.nc
    with nc.Block() as block:
        @block.sync
        def _(sp):
            for name in FIRST:
                sp.dma_start(k.packs[name][:, :], k.aps[name]).then_inc(k.loaded[name], 16)
            sp.dma_start(k.Xin[:, :], k.aps["xT"][:, 0:CH]).then_inc(k.loaded["tokens"], 16)
            for c in range(LANDINGS):
                load_experts(k, sp, c)
            for name in FIRST + ("tokens",):
                sp.wait_ge(k.loaded[name], 16)


def load_experts(k, sp, c):
    sp.dma_start(k.landed[:, c % LANDINGS, :], k.aps["experts"][:, c * SPLIT:(c + 1) * SPLIT]).then_inc(k.loaded[f"experts{c}"], 16)


def name_parts(k, where):
    for name in k.packs:
        for part, (rows, at, shape) in where[name].items():
            n = int(np.prod(shape))
            ap = k.packs[name][0:rows, at:at + n]
            if len(shape) == 2:
                ap = ap.rearrange("p (a b) -> p a b", b=shape[1])
            if len(shape) == 3:
                ap = ap.rearrange("p (a b c) -> p a b c", b=shape[1], c=shape[2])
            k.w[part] = ap


def split_experts(k, where):
    nc = k.nc
    high, low = k.sem("high"), k.sem("low")
    pieces = k.high.shape[1] // SPLIT
    piece = lambda t, c: t[:, c * SPLIT:(c + 1) * SPLIT]
    with nc.Block() as block:
        @block.sync
        def _(sp):
            for c in range(LANDINGS, pieces):
                sp.wait_ge(low, c - LANDINGS + 1)
                load_experts(k, sp, c)
            sp.dma_start(k.packs["mamba"][:, :], k.aps["mamba"]).then_inc(k.loaded["mamba"], 16)

        @block.scalar
        def _(act):
            for c in range(pieces):
                act.wait_ge(k.loaded[f"experts{c}"], 16)
                nc.scalar.activation(piece(k.high, c), k.landed[:, c % LANDINGS, :], ACT.Copy).then_inc(high, 1)

        @block.vector
        def _(dve):
            for c in range(pieces):
                dve.wait_ge(high, c + 1)
                nc.vector.tensor_tensor(piece(k.low, c), k.landed[:, c % LANDINGS, :], piece(k.high, c).bitcast(F32),
                                        ALU.subtract).then_inc(low, 1)
    for name, (_, at, shape) in where["experts"].items():
        k.w[name] = k.high[:, at:at + shape[0]], k.low[:, at:at + shape[0]]


def product3(nc, out, weights, cols, data, start=True, stop=True):
    at = slice(cols, cols + P)
    nc.tensor.matmul(out, weights[0][:, at], data[0], start=start, stop=False)
    nc.tensor.matmul(out, weights[1][:, at], data[0], start=False, stop=False)
    return nc.tensor.matmul(out, weights[0][:, at], data[1], start=False, stop=stop)


def setup(k):
    nc, w = k.nc, k.w
    wq, wvo, rope, decay, guide, foldb, maskrowb, onesr, identr = (w[n] for n in (
        "wq0", "wvo0", "rope", "decay", "guide", "foldb", "maskrowb", "onesr", "identr"))
    s_pe, s_act, s_dve = k.sem("setup_pe"), k.sem("setup_act"), k.sem("setup_dve")
    with nc.sbuf_tensor("turn", [64, 8], F32) as turn, nc.sbuf_tensor("unit", [P, 4], F32) as unit, \
            nc.sbuf_tensor("ropet", [64, SEQ], F32) as ropet, nc.Block() as block:
        @block.tensor
        def _(pe):
            for h in range(8):
                nc.tensor.matmul(k.ps[0][0:64, 32 * h:32 * h + 32], w["uqT"][:, h, :], w["ukT"][:, h, :], start=True, stop=True)
            for h in range(8):
                j, t = h % 4, h // 4
                ins = nc.tensor.matmul(k.ps[1][32 * j:32 * j + 32, t * P:(t + 1) * P], w["uvT"][:, h, :], w["wo"][:, h, :],
                                       start=True, stop=True)
            ins.then_inc(s_pe, 1)
            pe.wait_ge(s_act, 1)
            nc.tensor.matmul(k.ps[2][:, 0:1], w["heads8"], unit[:, 0:1], start=True, stop=True).then_inc(s_pe, 1)

        @block.scalar
        def _(act):
            link = Count(act, s_act)
            link(nc.scalar.activation(unit[:, 0:1], w["qg"], ACT.Square))
            act.wait_ge(s_pe, 2)
            link(nc.scalar.activation(unit[:, 1:2], k.ps[2][:, 0:1], ACT.Ln))
            link(nc.scalar.activation(unit[:, 2:3], unit[:, 1:2], ACT.Exp, scale=-0.5))
            for d in range(2):
                link(nc.scalar.activation(decay[:, d], w[f"alog{d}"], ACT.Exp))
            link(nc.scalar.activation(turn[:, 0:1], w["delta"], ACT.Exp, scale=-1.0))
            nc.scalar.activation(wq[:, :, 64:96], k.ps[0][0:64, 0:256].rearrange("p (h c) -> p h c", h=8), ACT.Copy)
            link(nc.scalar.activation(wvo[:, :, :], k.ps[1][:, 0:256].rearrange("p (t c) -> p t c", t=2), ACT.Copy))
            act.wait_ge(s_dve, 3)
            link(nc.scalar.activation(turn[:, 4:5], turn[:, 3:4], ACT.Sin))
            link(nc.scalar.activation(turn[:, 5:6], turn[:, 2:3], ACT.Sin, scale=3.141592))

        @block.vector
        def _(dve):
            link = Count(dve, s_dve)
            dve.wait_ge(s_act, 6)
            link(nc.vector.tensor_scalar(turn[:, 1:2], turn[:, 0:1], 1.0, None, ALU.add))
            link(nc.vector.reciprocal(turn[:, 2:3], turn[:, 1:2]))
            link(nc.vector.tensor_scalar(turn[:, 3:4], turn[:, 2:3], 2 * 3.141592, -3.141592, ALU.mult, ALU.add))
            link(nc.vector.tensor_scalar(decay[:, :], decay[:, :], -1.0, -1e-20, ALU.mult, ALU.min))
            link(nc.vector.scalar_tensor_tensor(guide[:, 0:1], w["qg"], 1.0 / 16, unit[:, 2:3], ALU.mult, ALU.mult))
            link(nc.vector.tensor_copy(guide[:, 1:2], guide[:, 0:1]))
            link(nc.vector.tensor_copy(foldb[:, :], w["fold"]))
            link(nc.vector.tensor_copy(onesr[:, :], w["ones"]))
            link(nc.vector.tensor_copy(identr[:, :], w["ident"]))
            link(nc.vector.tensor_copy(maskrowb[:, :], w["maskrow"]))
            link(nc.vector.tensor_copy(wq[:, :, 0:64], w["qr4"]))
            dve.wait_ge(s_act, 9)
            link(nc.vector.tensor_tensor(turn[:, 6:7], turn[:, 5:6], turn[:, 5:6], ALU.mult))
            link(nc.vector.tensor_scalar(turn[:, 7:8], turn[:, 6:7], -2.0, 1.0, ALU.mult, ALU.add))
            link(nc.vector.tensor_scalar(ropet[:, :], w["ropeU"], turn[:, 7:8], None, ALU.mult))
            link(nc.vector.scalar_tensor_tensor(rope[:, :], w["ropeW"], turn[:, 4:5], ropet[:, :], ALU.mult, ALU.add))


def attn0(k):
    nc, w, X = k.nc, k.w, k.Xin
    cols = bass.ds(k.chunk * 256, 256)
    slots = k.sem("a0_slots")
    with ExitStack() as ctx:
        sb = lambda n, s: ctx.enter_context(nc.sbuf_tensor(f"a0_{n}", s, F32))
        lat, Q, K, V, O = sb("lat", [64, CH]), sb("q", [96, 4, BCH, 2, SEQ]), sb("k", [96, CH]), sb("v", [P, NPAIR, 32]), sb("o", [P, 2, CH])
        with nc.sbuf_tensor("a0_soft", [64, 2, CH], F32) as soft, nc.sbuf_tensor("a0_kr", [64, CH], F32) as kr:
            raw, latd, bounded, logd, turned, vdone, folded = (k.sem(f"a0_{s}") for s in (
                "raw", "latd", "bounded", "logd", "turned", "vdone", "folded"))
            chain, achain = k.sem("a0_chain"), k.sem("a0_achain")
            table = w["rope"][:, :].unsqueeze(1).to_broadcast([64, BCH, SEQ])
            bank = lambda i: k.ps[i % 4]
            with nc.Block() as block:
                @block.sync
                def _(sp):
                    sp.dma_start(k.weight[:, :], k.aps["gatew"][:, cols]).then_inc(slots, 16)
                    sp.dma_start(k.pick[:, :], k.aps["pick"][:, cols]).then_inc(slots, 16)

                @block.tensor
                def _(pe):
                    nc.tensor.matmul(k.ps[4][0:64, :], w["wdq"], X[:, :], start=True, stop=True).then_inc(latd, 1)
                    nc.tensor.matmul(bank(0)[0:96, :], w["wkv"], X[:, :], start=True, stop=True).then_inc(raw, 1)
                    for p in range(NPAIR):
                        ins = nc.tensor.matmul(k.ps[5][:, 32 * p:32 * p + 32], X[:, p * PAIR:(p + 1) * PAIR], w["wkv"][:, 64:96],
                                               start=True, stop=True)
                    ins.then_inc(vdone, 1)
                    pe.wait_ge(latd, 2)
                    for h in range(8):
                        if h >= 3:
                            pe.wait_ge(turned, h - 2)
                        nc.tensor.matmul(bank(h + 1)[0:96, :], w["wq0"][:, h, :], lat[:, :], start=True, stop=True).then_inc(raw, 1)
                    pe.wait_ge(turned, 1)
                    nc.tensor.matmul(k.ps[6][0:64, :], w["fold64"], kr[:, :], start=True, stop=True).then_inc(folded, 1)

                @block.scalar
                def _(act):
                    act.wait_ge(latd, 1)
                    nc.scalar.activation(lat[:, :], k.ps[4][0:64, :], ACT.Copy).then_inc(latd, 1)
                    link = Count(act, achain)
                    for i in range(9):
                        dst = groups(K[64:96, :]) if i == 0 else Q[64:96, (i - 1) // 2, :, (i - 1) % 2, :]
                        act.wait_ge(bounded, i + 1)
                        link(nc.scalar.activation(soft[:, i % 2, :], soft[:, i % 2, :], ACT.Exp))
                        nc.scalar.activation(dst, groups(bank(i)[64:96, :]), ACT.Copy)
                        nc.scalar.activation(soft[:, i % 2, :], soft[:, i % 2, :], ACT.Ln, bias=1.0).then_inc(logd, 1)
                    act.wait_ge(vdone, 1)
                    nc.scalar.activation(V[:, :, :], k.ps[5][:, 0:P].rearrange("p (n c) -> p n c", c=32), ACT.Copy)
                    act.wait_ge(folded, 1)
                    nc.scalar.activation(K[0:64, :], k.ps[6][0:64, :], ACT.Copy)

                @block.vector
                def _(dve):
                    link = Count(dve, chain)

                    def bound(i):
                        dve.wait_ge(raw, i + 1)
                        nc.vector.tensor_scalar(soft[:, i % 2, :], bank(i)[0:64, :], 40.0, None, ALU.min).then_inc(bounded, 1)

                    bound(0)
                    for i in range(9):
                        if i + 1 < 9:
                            bound(i + 1)
                        dve.wait_ge(logd, i + 1)
                        link(nc.vector.tensor_tensor(soft[:, i % 2, :], bank(i)[0:64, :], soft[:, i % 2, :], ALU.max))
                        dst = groups(kr[:, :]) if i == 0 else Q[0:64, (i - 1) // 2, :, (i - 1) % 2, :]
                        ins = nc.vector.tensor_tensor(dst, groups(soft[:, i % 2, :]), table, ALU.mult)
                        ins.then_inc(turned, 1)
                        dve.wait_ge(turned, i + 1)
        attention(k, "a0a", Q, K, V, float(96 ** -0.5), True, O, after=ProductNorm(
            k, ctx, "a0n", lambda h: [(w["wvo0"][:, t, :], O[:, t, h * HALF:(h + 1) * HALF]) for t in range(2)], X, k.X, None,
            waits=[(slots, 32)]))


class ProductNorm:

    def __init__(self, k, ctx, tag, terms, x, out, bias, waits=()):
        self.k, self.terms, self.waits, self.done = k, terms, waits, k.sem(f"{tag}_done")
        self.norm = Norm(k, ctx, tag, k.Z, [(out, None, None)])
        self.total = Sum(k, tag, k.Z, lambda h: k.ps[6 + h][:, 0:HALF], [x], bias)

    def sync(self, sp):
        for sem, n in self.waits:
            sp.wait_ge(sem, n)

    def tensor(self, pe):
        for h in range(2):
            t = self.terms(h)
            for i, (a, b) in enumerate(t):
                ins = self.k.nc.tensor.matmul(self.k.ps[6 + h][:, 0:HALF], a, b, start=i == 0, stop=i == len(t) - 1)
            ins.then_inc(self.done, 1)
        for h in range(2):
            self.total.wait(pe, h)
            self.norm.center(pe, h)
        for h in range(2):
            self.norm.mean(pe, h)

    def scalar(self, act):
        for h in range(2):
            self.norm.square(act, h)
        self.norm.root(act)

    def vector(self, dve):
        for h in range(2):
            dve.wait_ge(self.done, h + 1)
            self.total.add(dve, h)
        for h in range(2):
            self.norm.out(dve, h)


def moe(k):
    nc, w, X = k.nc, k.w, k.X
    sent, picked, gated, gates_sb, hidden, scaled, high, low, given = (k.sem(f"moe_{s}") for s in (
        "sent", "picked", "gated", "gates_sb", "hidden", "scaled", "high", "low", "given"))
    xhigh, xlow, whigh, wlow = (k.sem(f"moe_{s}") for s in ("xhigh", "xlow", "whigh", "wlow"))
    NT = 2 * EXPERTS
    AHEAD = 3
    with ExitStack() as ctx:
        sb = lambda n, s, dt=F32: ctx.enter_context(nc.sbuf_tensor(f"moe_{n}", s, dt))
        weight, pick = k.weight, k.pick
        halves, mine = sb("halves", [P, 2, 256], F32R), sb("mine", [P, 2, 2, 256], F32R)
        gate, H = sb("gate", [P, 4, CH]), sb("h", [P, 3, CH])
        Hh, Hl = sb("hh", [P, 4, CH], F32R), sb("hl", [P, 4, CH], F32R)
        norm = Norm(k, ctx, "moen", k.Z, [(X, None, None)])
        Xh, Xl = (sb(n, [P, CH], F32R)[:, :] for n in ("xh", "xl"))
        total = Sum(k, "moen", k.Z, lambda h: k.ps[7][:, h * HALF:(h + 1) * HALF], [X])
        block = ctx.enter_context(nc.Block())

        @block.sync
        def _(sp):
            sp.dma_start(k.Xin[:, :], k.aps["xT"][:, bass.ds((k.chunk + 1) % NCH * CH, CH)]).then_inc(sent, 16)
            sp.wait_ge(sent, 16)

        @block.tensor
        def _(pe):
            def hide(i):
                if i >= 4:
                    pe.wait_ge(scaled, i - 3)
                product3(nc, k.ps[i % 4][:, :], w["pin"], i * P, (Xh, Xl)).then_inc(hidden, 1)

            def spread_gate(e):
                pe.wait_ge(picked, e + 1)
                if e:
                    pe.wait_ge(gates_sb, e)
                for s in range(2):
                    rows = slice(64 * s, 64 * s + 64)
                    for n in range(2):
                        ins = nc.tensor.matmul(k.ps[4 + s][:, 0:256], w["onesr"][rows, :], mine[rows, e % 2, n, :],
                                               start=n == 0, stop=n == 1, tile_position=(64 * s, 0))
                ins.then_inc(gated, 1)

            pe.wait_ge(xlow, 1)
            hide(0)
            spread_gate(0)
            hide(1)
            hide(2)
            spread_gate(1)
            for i in range(NT):
                if i + AHEAD < NT:
                    hide(i + AHEAD)
                if i % 2 == 0 and i // 2 + 2 < EXPERTS:
                    spread_gate(i // 2 + 2)
                pe.wait_ge(low, i + 1)
                product3(nc, k.ps[7][:, :], w["pout"], i * P, (Hh[:, i % 4, :], Hl[:, i % 4, :]), start=i == 0,
                         stop=i == NT - 1).then_inc(given, 1)
            for h in range(2):
                total.wait(pe, h)
                norm.center(pe, h)
            for h in range(2):
                norm.mean(pe, h)

        @block.scalar
        def _(act):
            nc.scalar.activation(Xh, X[:, :], ACT.Copy).then_inc(xhigh, 1)
            nc.scalar.activation(halves[:, 0, :], weight[:, :], ACT.Copy).then_inc(whigh, 1)

            def copy_gate(e):
                act.wait_ge(gated, e + 1)
                dst = gate[:, e % 4, :].rearrange("p (n s q) -> p s n q", s=2, q=SEQ)
                for s in range(2):
                    ins = nc.scalar.activation(dst[:, s], groups(k.ps[4 + s][:, 0:256]), ACT.Copy)
                ins.then_inc(gates_sb, 1)

            copy_gate(0)
            copy_gate(1)
            for i in range(NT):
                act.wait_ge(scaled, i + 1)
                if i >= 4:
                    act.wait_ge(given, i - 3)
                nc.scalar.activation(Hh[:, i % 4, :], H[:, i % 3, :], ACT.Copy).then_inc(high, 1)
                if i % 2 == 1 and i // 2 + 2 < EXPERTS:
                    copy_gate(i // 2 + 2)
            for h in range(2):
                norm.square(act, h)
            norm.root(act)

        @block.gpsimd
        def _(pool):
            for i in range(NT):
                pool.wait_ge(high, i + 1)
                nc.gpsimd.tensor_tensor(Hl[:, i % 4, :], H[:, i % 3, :], Hh[:, i % 4, :].bitcast(F32), ALU.subtract).then_inc(low, 1)

        @block.vector
        def _(dve):
            def choose(e):
                if e >= 2:
                    dve.wait_ge(gated, e - 1)
                nc.vector.scalar_tensor_tensor(mine[:, e % 2], pick[:, :].unsqueeze(1).to_broadcast([P, 2, 256]), float(e),
                                               halves[:, :, :].bitcast(F32), ALU.is_equal, ALU.mult).then_inc(picked, 1)

            dve.wait_ge(xhigh, 1)
            nc.vector.tensor_tensor(Xl, X[:, :], Xh.bitcast(F32), ALU.subtract).then_inc(xlow, 1)
            dve.wait_ge(whigh, 1)
            nc.vector.tensor_tensor(halves[:, 1, :], weight[:, :], halves[:, 0, :].bitcast(F32), ALU.subtract).then_inc(wlow, 1)
            dve.wait_ge(wlow, 1)
            choose(0)
            choose(1)
            for i in range(NT):
                if i % 2 == 0 and i // 2 + 2 < EXPERTS:
                    choose(i // 2 + 2)
                dve.wait_ge(hidden, i + 1)
                dve.wait_ge(gates_sb, i // 2 + 1)
                if i >= 3:
                    dve.wait_ge(low, i - 2)
                nc.vector.scalar_tensor_tensor(H[:, i % 3, :], k.ps[i % 4][:, :], 0.0, gate[:, i // 2 % 4, :], ALU.max,
                                               ALU.mult).then_inc(scaled, 1)
            dve.wait_ge(given, NT)
            for h in range(2):
                total.add(dve, h)
            for h in range(2):
                norm.out(dve, h)


def ffn(k):
    nc, w, X = k.nc, k.w, k.X
    T = CH // P
    NT = 4 * EXPERTS
    AHEAD = 3
    with ExitStack() as ctx:
        sb = lambda n, s, dt=F32: ctx.enter_context(nc.sbuf_tensor(f"ffn_{n}", s, dt))
        L, hot, eq, hot2 = (sb(n, [P, T, EXPERTS]) for n in ("l", "hot", "eq", "hot2"))
        best, second, pr, ex = (sb(n, [P, T]) for n in ("best", "second", "pr", "ex"))
        G, Gh, Gl = sb("g", [P, EXPERTS, T]), sb("gh", [P, EXPERTS, T], F32R), sb("gl", [P, EXPERTS, T], F32R)
        gate, S, H, O, acc = (sb("gate", [P, 2, CH]), sb("s", [P, 2, CH]), sb("h", [P, 2, CH]), sb("o", [P, 2, CH]),
                              sb("acc", [P, CH]))
        Hh, Hl, Xh, Xl = (sb(n, s, F32R) for n, s in (("hh", [P, 4, CH]), ("hl", [P, 4, CH]), ("xh", [P, CH]), ("xl", [P, CH])))
        high, low, given, xhigh, xlow = (k.sem(f"ffn_{s}") for s in ("high", "low", "given", "xhigh", "xlow"))
        logits, chain, raised, chosen, gated, gates_sb, up, silud, hidden, weighed, summed = (
            k.sem(f"ffn_{s}") for s in ("logits", "chain", "raised", "chosen", "gated", "gates_sb", "up", "silud", "hidden",
                                        "weighed", "summed"))
        norm = Norm(k, ctx, "ffnn", k.Z, [(k.tokens[:, bass.ds(k.chunk * CH, CH)], None, None)])
        total = Sum(k, "ffnn", k.Z, lambda h: acc[:, h * HALF:(h + 1) * HALF], [O[:, (EXPERTS - 1) % 2, :]])
        block = ctx.enter_context(nc.Block())

        @block.sync
        def _(sp):
            sp.wait_ge(k.loaded["mamba"], 16)

        @block.tensor
        def _(pe):
            def hide(i):
                e, f = divmod(i, 4)
                if i >= 2:
                    pe.wait_ge(hidden, i - 1)
                for half in range(2):
                    ins = product3(nc, k.ps[2 * half + i % 2][:, :], w["w1"], e * 1024 + (4 * half + f) * P, (Xh[:, :], Xl[:, :]))
                ins.then_inc(up, 1)

            def spread_gate(e):
                if e == 0:
                    pe.wait_ge(chosen, 1)
                if e >= 2:
                    pe.wait_ge(gates_sb, e - 1)
                for t in range(T):
                    for n, part in enumerate((Gh, Gl)):
                        ins = nc.tensor.matmul(k.ps[6 + e % 2][:, t * P:(t + 1) * P], part[:, e, t:t + 1].to_broadcast([P, P]),
                                               w["identr"][:, :], start=n == 0, stop=n == 1)
                ins.then_inc(gated, 1)

            def give(i):
                e, f = divmod(i, 4)
                pe.wait_ge(low, i + 1)
                if f == 0 and e >= 2:
                    pe.wait_ge(weighed, e - 1)
                product3(nc, k.ps[4 + e % 2][:, :], w["w2"], i * P, (Hh[:, i % 4, :], Hl[:, i % 4, :]), start=f == 0,
                         stop=f == 3).then_inc(given, 1)

            for t in range(T):
                ins = nc.tensor.matmul(k.ps[6][:, 8 * t:8 * t + 8], X[:, t * P:(t + 1) * P], w["router"], start=True, stop=True)
            ins.then_inc(logits, 1)
            pe.wait_ge(xlow, 1)
            for i in range(AHEAD):
                hide(i)
            for i in range(NT):
                if i + AHEAD < NT:
                    hide(i + AHEAD)
                if i % 4 == 3:
                    spread_gate(i // 4)
                give(i)
            for h in range(2):
                total.wait(pe, h)
                norm.center(pe, h)
            for h in range(2):
                norm.mean(pe, h)

        @block.scalar
        def _(act):
            def copy_gate(e):
                act.wait_ge(gated, e + 1)
                if e >= 2:
                    act.wait_ge(weighed, e - 1)
                nc.scalar.activation(gate[:, e % 2, :], k.ps[6 + e % 2][:, :], ACT.Copy).then_inc(gates_sb, 1)

            def round_high(i):
                act.wait_ge(hidden, i + 1)
                if i >= 4:
                    act.wait_ge(given, i - 3)
                nc.scalar.activation(Hh[:, i % 4, :], H[:, i % 2, :], ACT.Copy).then_inc(high, 1)

            nc.scalar.activation(Xh[:, :], X[:, :], ACT.Copy).then_inc(xhigh, 1)
            act.wait_ge(chain, 13)
            nc.scalar.activation(ex[:, :], ex[:, :], ACT.Exp).then_inc(raised, 1)
            for i in range(NT):
                e, f = divmod(i, 4)
                act.wait_ge(up, i + 1)
                if i >= 2:
                    act.wait_ge(hidden, i - 1)
                nc.scalar.activation(S[:, i % 2, :], k.ps[i % 2][:, :], ACT.Silu, bias=w["b1"][:, e, f:f + 1]).then_inc(silud, 1)
                if i:
                    round_high(i - 1)
                if e and f == 3:
                    copy_gate(e - 1)
            round_high(NT - 1)
            copy_gate(EXPERTS - 1)
            nc.scalar.preload_act_table_set("natural_log_exp_and_others")
            for h in range(2):
                norm.square(act, h)
            norm.root(act)

        @block.vector
        def _(dve):
            link = Count(dve, chain)
            prio = w["prio"].unsqueeze(1).to_broadcast([P, T, EXPERTS])
            tt, full = nc.vector.tensor_tensor, (lambda a: spread(a[:, :], EXPERTS))

            def first_of(m, onehot):
                link(nc.vector.tensor_reduce(m[:, :], L[:, :, :], AX, ALU.max))
                link(tt(eq[:, :, :], L[:, :, :], full(m), ALU.is_equal))
                link(tt(eq[:, :, :], eq[:, :, :], prio, ALU.mult))
                link(nc.vector.tensor_reduce(pr[:, :], eq[:, :, :], AX, ALU.max))
                link(tt(onehot[:, :, :], prio, full(pr), ALU.is_equal))

            def hide(i):
                e, f = divmod(i, 4)
                dve.wait_ge(silud, i + 1)
                if i >= 2:
                    dve.wait_ge(low, i - 1)
                nc.vector.scalar_tensor_tensor(H[:, i % 2, :], k.ps[2 + i % 2][:, :], w["b1"][:, e, 4 + f:5 + f],
                                               S[:, i % 2, :], ALU.add, ALU.mult).then_inc(hidden, 1)

            def weigh(e):
                dve.wait_ge(gates_sb, e + 1)
                dve.wait_ge(given, 4 * e + 4)
                if e >= 2:
                    dve.wait_ge(summed, e - 1)
                nc.vector.scalar_tensor_tensor(O[:, e % 2, :], k.ps[4 + e % 2][:, :], w["b2"][:, e:e + 1], gate[:, e % 2, :],
                                               ALU.add, ALU.mult).then_inc(weighed, 1)

            dve.wait_ge(xhigh, 1)
            nc.vector.tensor_tensor(Xl[:, :], X[:, :], Xh[:, :].bitcast(F32), ALU.subtract).then_inc(xlow, 1)
            dve.wait_ge(logits, 1)
            link(tt(L[:, :, :], k.ps[6][:, 0:8 * T].rearrange("p (t e) -> p t e", e=EXPERTS),
                    w["router_b"].unsqueeze(1).to_broadcast([P, T, EXPERTS]), ALU.add))
            first_of(best, hot)
            link(nc.vector.scalar_tensor_tensor(L[:, :, :], hot[:, :, :], -BIG, L[:, :, :], ALU.mult, ALU.add))
            first_of(second, hot2)
            link(tt(ex[:, :], second[:, :], best[:, :], ALU.subtract))
            dve.wait_ge(raised, 1)
            link(nc.vector.tensor_scalar(best[:, :], ex[:, :], 1.0, None, ALU.add))
            link(nc.vector.reciprocal(best[:, :], best[:, :]))
            link(tt(ex[:, :], ex[:, :], best[:, :], ALU.mult))
            link(tt(hot[:, :, :], hot[:, :, :], full(best), ALU.mult))
            link(tt(hot2[:, :, :], hot2[:, :, :], full(ex), ALU.mult))
            link(tt(G[:, :, :].rearrange("p e t -> p t e"), hot[:, :, :], hot2[:, :, :], ALU.add))
            link(nc.vector.tensor_copy(Gh[:, :, :], G[:, :, :]))
            tt(Gl[:, :, :], G[:, :, :], Gh[:, :, :].bitcast(F32), ALU.subtract).then_inc(chosen, 1)

            for i in range(4):
                hide(i)
            for e in range(1, EXPERTS):
                for f in range(4):
                    hide(4 * e + f)
                weigh(e - 1)
            weigh(EXPERTS - 1)
            dve.wait_ge(weighed, EXPERTS)
            dve.wait_ge(summed, EXPERTS - 1)
            for h in range(2):
                total.add(dve, h)
            for h in range(2):
                norm.out(dve, h)

        @block.gpsimd
        def _(pool):
            def add(e):
                pool.wait_ge(weighed, e + 1)
                if e:
                    pool.wait_ge(summed, e)
                nc.gpsimd.tensor_tensor(acc[:, :], acc[:, :] if e else X[:, :], O[:, e % 2, :], ALU.add).then_inc(summed, 1)

            for i in range(NT):
                pool.wait_ge(high, i + 1)
                nc.gpsimd.tensor_tensor(Hl[:, i % 4, :], H[:, i % 2, :], Hh[:, i % 4, :].bitcast(F32), ALU.subtract).then_inc(low, 1)
                if i >= 8 and i % 4 == 1:
                    add((i - 8) // 4)
            add(EXPERTS - 2)


def mamba(k):
    nc, w, X = k.nc, k.w, k.X
    cols = bass.ds(k.chunk * CH, CH)
    tokens, sent, taken = k.tokens[:, cols], k.sem("mb_sent"), k.sem("mb_taken")
    with ExitStack() as ctx:
        sb = lambda n, s, dt=F32: ctx.enter_context(nc.sbuf_tensor(f"mb_{n}", s, dt))
        U, ZS = sb("u", [P, 2, 2, CH]), sb("zs", [P, 2, 2, CH])
        back = lambda ap: groups(ap)[:, :, ::-1]
        turned, cleared, inx, inz, padded, convd, chain, actd = (k.sem(f"mb_{s}") for s in (
            "turned", "cleared", "inx", "inz", "padded", "convd", "chain", "actd"))
        with nc.sbuf_tensor("mb_xr", [P, CH], F32) as XR, nc.sbuf_tensor("mb_pad", [P, 4, BCH, SEQ + 3], F32) as pad, \
                nc.sbuf_tensor("mb_conv", [P, 2, CH], F32) as conv, nc.Block() as block:
            @block.tensor
            def _(pe):
                for i in range(4):
                    d, t = divmod(i, 2)
                    if i == 2:
                        pe.wait_ge(turned, 1)
                    src = XR[:, :] if d else tokens
                    nc.tensor.matmul(k.ps[i][:, :], w["inT"][:, t * P:(t + 1) * P], src, start=True, stop=True).then_inc(inx, 1)
                    nc.tensor.matmul(k.ps[4 + i][:, :], w["inT"][:, (2 + t) * P:(3 + t) * P], src, start=True,
                                     stop=True).then_inc(inz, 1)

            @block.sync
            def _(sp):
                sp.dma_start(k.context[0:64, :], k.aps["ctxT"][:, cols]).then_inc(sent, 16)

            @block.gpsimd
            def _(pool):
                nc.gpsimd.memset(pad[:, :, :, 0:3].rearrange("p i b l -> p (i b) l"), 0.0).then_inc(cleared, 1)

            @block.scalar
            def _(act):
                nc.scalar.activation(X[:, :], tokens, ACT.Copy).then_inc(taken, 1)
                for i in range(4):
                    act.wait_ge(inx, i + 1)
                    nc.scalar.activation(pad[:, i, :, 3:], groups(k.ps[i][:, :]), ACT.Copy).then_inc(padded, 1)
                for i in range(4):
                    d, t = divmod(i, 2)
                    act.wait_ge(inz, i + 1)
                    nc.scalar.activation(ZS[:, d, t, :], k.ps[4 + i][:, :], ACT.Silu)
                for i in range(4):
                    d, t = divmod(i, 2)
                    act.wait_ge(convd, i + 1)
                    nc.scalar.activation(U[:, d, t, :], conv[:, i % 2, :], ACT.Silu, bias=w[f"convb{d}"][:, t:t + 1]).then_inc(actd, 1)
                nc.scalar.preload_act_table_set("natural_log_exp_and_others")

            @block.vector
            def _(dve):
                link = Count(dve, chain)
                dve.wait_ge(taken, 1)
                nc.vector.tensor_copy(groups(XR[:, :]), back(X[:, :])).then_inc(turned, 1)
                dve.wait_ge(cleared, 1)
                for i in range(4):
                    d, t = divmod(i, 2)
                    dve.wait_ge(padded, i + 1)
                    if i >= 2:
                        dve.wait_ge(actd, i - 1)
                    cw, dst = w[f"convw{d}"], groups(conv[:, i % 2, :])
                    link(nc.vector.tensor_scalar(dst, pad[:, i, :, 0:SEQ], cw[:, t, 0:1], None, ALU.mult))
                    for j in range(1, 4):
                        ins = nc.vector.scalar_tensor_tensor(dst, pad[:, i, :, j:j + SEQ], cw[:, t, j:j + 1], dst, ALU.mult, ALU.add)
                        if j < 3:
                            link(ins)
                    ins.then_inc(convd, 1)

        DT, DU = sb("dt", [P, 2, 2, CH]), sb("du", [P, 2, 2, CH])
        BC = sb("bc", [96, 2, CH], BF16)
        low, mid = sb("low", [104, 2, CH]), sb("mid", [96, 2, CH], BF16)
        RING = 3
        dA, dBu, st, hC = (sb(n, [P, RING, 2 * CH]) for n in ("da", "dbu", "st", "hc"))
        bR = sb("br", [P, RING, CH])
        NI = 2 * STATE
        xproj, cut, split, rates, rated, soft, ready, bchain, achain = (k.sem(f"mb_{s}") for s in (
            "xproj", "cut", "split", "rates", "rated", "soft", "ready", "bchain", "achain"))
        ins_rep, outs_rep, in_sb, decayed, fed_in, ran, read, added = (k.sem(f"mb_{s}") for s in (
            "ins_rep", "outs_rep", "in_sb", "decayed", "fed_in", "ran", "read", "added"))
        rate_bank = lambda d, t: k.ps[2 + 4 * d + t]
        with nc.Block() as block:
            @block.tensor
            def _(pe):
                for d in range(2):
                    for t in range(2):
                        ins = nc.tensor.matmul(k.ps[4 + d][0:104, :], w[f"xproj{d}"][:, t, :], U[:, d, t, :], start=t == 0, stop=t == 1)
                    ins.then_inc(xproj, 1)
                for d in range(2):
                    pe.wait_ge(cut, d + 1)
                    for t in range(2):
                        nc.tensor.matmul(rate_bank(d, t)[:, :], w[f"dtw{d}"][96:104, t * P:(t + 1) * P], low[96:104, d, :],
                                         start=True, stop=True, tile_position=(96, 0)).then_inc(rates, 1)

                def rep_in(i):
                    d, n = divmod(i, STATE)
                    pe.wait_ge(split, d + 1)
                    if i >= 2:
                        pe.wait_ge(in_sb, i - 1)
                    nc.tensor.matmul(k.ps[i % 2][:, :], w["foldb"][:, n:n + 1].to_broadcast([96, P]), BC[:, d, :], start=True,
                                     stop=True).then_inc(ins_rep, 1)

                def rep_out(i):
                    d, n = divmod(i, STATE)
                    if i < 2:
                        pe.wait_ge(ready, i + 1)
                    else:
                        pe.wait_ge(read, i - 1)
                    nc.tensor.matmul(k.ps[2 + i % 2][:, :], w["foldb"][:, 16 + n:17 + n].to_broadcast([96, P]), BC[:, d, :],
                                     start=True, stop=True).then_inc(outs_rep, 1)

                def add(i):
                    d, n = divmod(i, STATE)
                    if i == 0:
                        pe.wait_ge(split, 2)
                    if i == STATE:
                        pe.wait_ge(ready, 4)
                    pe.wait_ge(read, i + 1)
                    for t in range(2):
                        ins = nc.tensor.matmul(k.ps[4 + 2 * d + t][:, :], w["ident"], hC[:, i % RING, t * CH:(t + 1) * CH],
                                               start=n == 0, stop=n == STATE - 1)
                    ins.then_inc(added, 1)

                rep_in(0)
                rep_in(1)
                rep_out(0)
                rep_out(1)
                rep_in(2)
                rep_in(3)
                for i in range(NI):
                    if i + 4 < NI:
                        rep_in(i + 4)
                    if i + 2 < NI:
                        rep_out(i + 2)
                    add(i)

            @block.scalar
            def _(act):
                link = Count(act, achain)

                def softplus(d):
                    for i in range(2 * d, 2 * d + 2):
                        act.wait_ge(rated, i + 1)
                        link(nc.scalar.activation(DT[:, d, i % 2, :], DT[:, d, i % 2, :], ACT.Exp))
                        nc.scalar.activation(DT[:, d, i % 2, :], DT[:, d, i % 2, :], ACT.Ln, bias=1.0).then_inc(soft, 1)

                for d in range(2):
                    act.wait_ge(xproj, d + 1)
                    nc.scalar.activation(low[96:104, d, :], k.ps[4 + d][96:104, :], ACT.Copy).then_inc(cut, 1)
                softplus(0)
                for i in range(NI):
                    d, n = divmod(i, STATE)
                    if i == 2:
                        softplus(1)
                    act.wait_ge(ins_rep, i + 1)
                    if i >= RING:
                        act.wait_ge(fed_in, i - RING + 1)
                    nc.scalar.activation(bR[:, i % RING, :], k.ps[i % 2][:, :], ACT.Copy).then_inc(in_sb, 1)
                    if i >= RING:
                        act.wait_ge(ran, i - RING + 1)
                    if n == 0:
                        act.wait_ge(ready, 2 * d + 2)
                    for t in range(2):
                        ins = nc.scalar.activation(dA[:, i % RING, t * CH:(t + 1) * CH], DT[:, d, t, :], ACT.Exp,
                                                   scale=w["decay"][:, d, t, n:n + 1])
                    ins.then_inc(decayed, 1)

            @block.gpsimd
            def _(pool):
                for i in range(NI):
                    d, n = divmod(i, STATE)
                    pool.wait_ge(in_sb, i + 1)
                    if n == 0:
                        pool.wait_ge(ready, 2 * d + 2)
                    if i >= RING:
                        pool.wait_ge(ran, i - RING + 1)
                    nc.gpsimd.tensor_tensor(dBu[:, i % RING, :].rearrange("p (t c) -> p t c", t=2), DU[:, d],
                                            bR[:, i % RING, :].unsqueeze(1).to_broadcast([P, 2, CH]), ALU.mult).then_inc(fed_in, 1)

            @block.vector
            def _(dve):
                def scan(i):
                    dve.wait_ge(fed_in, i + 1)
                    dve.wait_ge(decayed, i + 1)
                    if i >= RING:
                        dve.wait_ge(read, i - RING + 1)
                    nc.vector.tensor_tensor_scan(st[:, i % RING, :], dA[:, i % RING, :], dBu[:, i % RING, :], 0.0, ALU.mult,
                                                 ALU.add).then_inc(ran, 1)

                link = Count(dve, bchain)

                def take_rates(d):
                    for i in range(2 * d, 2 * d + 2):
                        t = i % 2
                        dve.wait_ge(soft, i + 1)
                        link(nc.vector.scalar_tensor_tensor(DT[:, d, t, :], rate_bank(d, t)[:, :], w[f"dtb{d}"][:, t:t + 1],
                                                            DT[:, d, t, :], ALU.add, ALU.max))
                        link(nc.vector.tensor_tensor(DU[:, d, t, :], DT[:, d, t, :], U[:, d, t, :], ALU.mult))
                        nc.vector.memset(DT[:, d, t, ::SEQ], BIG).then_inc(ready, 1)

                def split_weights(d):
                    dve.wait_ge(cut, d + 1)
                    link(nc.vector.tensor_copy(BC[:, d, :], k.ps[4 + d][0:96, :]))
                    link(nc.vector.tensor_tensor(low[0:96, d, :], k.ps[4 + d][0:96, :], BC[:, d, :], ALU.subtract))
                    nc.vector.tensor_copy(BC[32:64, d, :], low[32:64, d, :])
                    link(nc.vector.tensor_copy(mid[64:96, d, :], low[64:96, d, :]))
                    nc.vector.tensor_tensor(BC[64:96, d, :], low[64:96, d, :], mid[64:96, d, :], ALU.subtract).then_inc(split, 1)

                def bound_rates(d):
                    for i in range(2 * d, 2 * d + 2):
                        dve.wait_ge(rates, i + 1)
                        nc.vector.tensor_scalar(DT[:, d, i % 2, :], rate_bank(d, i % 2)[:, :], w[f"dtb{d}"][:, i % 2:i % 2 + 1],
                                                40.0, ALU.add, ALU.min).then_inc(rated, 1)

                split_weights(0)
                bound_rates(0)
                take_rates(0)
                split_weights(1)
                bound_rates(1)
                scan(0)
                for i in range(NI):
                    if i + 1 < NI:
                        scan(i + 1)
                    if i == 2:
                        take_rates(1)
                    dve.wait_ge(ran, i + 1)
                    dve.wait_ge(outs_rep, i + 1)
                    if i >= RING:
                        dve.wait_ge(added, i - RING + 1)
                    nc.vector.tensor_tensor(hC[:, i % RING, :].rearrange("p (t c) -> p t c", t=2),
                                            st[:, i % RING, :].rearrange("p (t c) -> p t c", t=2),
                                            k.ps[2 + i % 2][:, :].unsqueeze(1).to_broadcast([P, 2, CH]), ALU.mult).then_inc(read, 1)

        skipped, gatedy, gated0, outd, dchain = (k.sem(f"mb_{s}") for s in ("skipped", "gatedy", "gated0", "outd", "dchain"))
        norm = Norm(k, ctx, "mbn", k.Z, [(X, None, None)])
        with nc.Block() as block:
            @block.sync
            def _(sp):
                sp.wait_ge(sent, 16)
                sp.wait_ge(k.loaded["cross"], 16)
                sp.wait_ge(k.loaded["last"], 16)

            @block.vector
            def _(dve):
                for i in range(4):
                    d, t = divmod(i, 2)
                    nc.vector.scalar_tensor_tensor(DU[:, d, t, :], U[:, d, t, :], w[f"dskip{d}"][:, t:t + 1], k.ps[4 + i][:, :],
                                                   ALU.mult, ALU.add).then_inc(skipped, 1)
                    if t:
                        dve.wait_ge(skipped, i + 1)
                        nc.vector.tensor_tensor(DU[:, d, t, :], DU[:, d, t, :], ZS[:, d, t, :], ALU.mult).then_inc(gatedy, 1)
                link = Count(dve, dchain)
                dve.wait_ge(outd, 1)
                link(nc.vector.tensor_tensor(k.Z[:, :], k.ps[0][:, :], X[:, :], ALU.add))
                dve.wait_ge(outd, 2)
                nc.vector.tensor_tensor(groups(k.Z[:, :]), groups(k.Z[:, :]), back(k.ps[1][:, :]), ALU.add).then_inc(dchain, 1)
                for h in range(2):
                    norm.out(dve, h)

            @block.gpsimd
            def _(pool):
                for d in range(2):
                    pool.wait_ge(skipped, 2 * d + 1)
                    nc.gpsimd.tensor_tensor(DU[:, d, 0, :], DU[:, d, 0, :], ZS[:, d, 0, :], ALU.mult).then_inc(gated0, 1)

            @block.tensor
            def _(pe):
                for i in range(4):
                    d, t = divmod(i, 2)
                    pe.wait_ge(gatedy if t else gated0, d + 1)
                    ins = nc.tensor.matmul(k.ps[d][:, :], w["outT"][:, t, :], DU[:, d, t, :], start=t == 0, stop=t == 1)
                    if t:
                        ins.then_inc(outd, 1)
                pe.wait_ge(dchain, 2)
                for h in range(2):
                    norm.center(pe, h)
                for h in range(2):
                    norm.mean(pe, h)

            @block.scalar
            def _(act):
                for h in range(2):
                    norm.square(act, h)
                norm.root(act)


class Projections:

    def __init__(self, k, tag, jobs):
        self.k, self.jobs = k, jobs
        self.done, self.by_act, self.by_dve = (k.sem(f"{tag}_{s}") for s in ("done", "by_act", "by_dve"))

    def bank(self, i):
        return self.k.ps[i if i < 8 else i - 4]

    def products(self, pe):
        for i, (_, terms) in enumerate(self.jobs):
            if i >= 8:
                pe.wait_ge(self.by_dve if i % 2 else self.by_act, (i - 4) // 2 + 1)
            for n, (a, b) in enumerate(terms):
                ins = self.k.nc.tensor.matmul(self.bank(i)[:, :], a, b, start=n == 0, stop=n == len(terms) - 1)
            ins.then_inc(self.done, 1)

    def wait_queries(self, eng):
        eng.wait_ge(self.by_act, 4)
        eng.wait_ge(self.by_dve, 4)

    def wait_values(self, eng):
        eng.wait_ge(self.by_act, len(self.jobs) // 2)
        eng.wait_ge(self.by_dve, len(self.jobs) // 2)

    def copies_by_scalar(self, act):
        for i in range(0, len(self.jobs), 2):
            act.wait_ge(self.done, i + 1)
            self.k.nc.scalar.activation(self.jobs[i][0], self.bank(i)[:, :], ACT.Copy).then_inc(self.by_act, 1)

    def copies_by_vector(self, dve):
        for i in range(1, len(self.jobs), 2):
            dve.wait_ge(self.done, i + 1)
            self.k.nc.vector.tensor_copy(self.jobs[i][0], self.bank(i)[:, :]).then_inc(self.by_dve, 1)


class LastProjections(Projections):

    def __init__(self, k, tag, jobs, cols, qm, km, Q, Qx):
        super().__init__(k, tag, jobs)
        self.cols, self.qm, self.km, self.Q, self.Qx = cols, qm, km, Q, Qx
        self.taken, self.masks, self.masked, self.regs = (k.sem(f"{tag}_{s}") for s in ("taken", "masks", "masked", "regs"))

    def products(self, pe):
        pe.wait_ge(self.taken, 1)
        pe.wait_ge(self.masked, 1)
        super().products(pe)

    def wait_queries(self, pe):
        super().wait_queries(pe)
        pe.wait_ge(self.regs, 1)

    def copies_by_scalar(self, act):
        self.k.nc.scalar.activation(self.k.X[:, :], self.k.tokens[:, self.cols], ACT.Copy).then_inc(self.taken, 1)
        super().copies_by_scalar(act)

    def copies_by_vector(self, dve):
        k, vec = self.k, self.k.nc.vector
        link = Count(dve, self.masks)
        vec.tensor_scalar(self.qm[:, :], k.sim[:, self.cols], k.w["qa"], k.w["qc"], ALU.mult, ALU.add)
        link(vec.tensor_scalar(self.km[:, :], k.sim[:, self.cols], k.w["ka"], k.w["kc"], ALU.mult, ALU.add))
        vec.memset(self.km[:, :].rearrange("p (b q) -> p b q", q=SEQ)[:, :, 0:REG], 0.0).then_inc(self.masked, 1)
        super().copies_by_vector(dve)
        super().wait_queries(dve)
        for j in range(4):
            rows = slice(32 * j, 32 * j + 32)
            src = self.Q[rows, :, :].rearrange("p t (b q) -> p t b q", q=SEQ)[:, :, :, 0:REG]
            ins = vec.tensor_scalar(self.Qx[rows, :, :, REG * j:REG * j + REG], src, k.w["negclass"][rows], None, ALU.add)
        ins.then_inc(self.regs, 1)


def mha(k, m, tag, x, xn, yn, yrows, masked, xo, parts, outs):
    nc, w = k.nc, k.w
    y = lambda t: t[0:yrows]
    with ExitStack() as ctx:
        sb = lambda n, s: ctx.enter_context(nc.sbuf_tensor(f"{tag}_{n}", s, F32))
        O, Q, K, V = sb("o", [P, 4, CH]), sb("q", [P, 4, CH]), sb("k", [P, 4, CH]), sb("v", [P, NPAIR, 512])
        jobs = [(Q[:, t, :], [(w[m + "wq"][:, t * P:(t + 1) * P], xn[:, :])]) for t in range(4)]
        jobs += [(K[:, t, :], [(w[m + "wk"][:, t * P:(t + 1) * P], y(yn)[:, :])]) for t in range(4)]
        jobs += [(V[:, p, :], [(y(yn)[:, p * PAIR:(p + 1) * PAIR], w[m + "wv"])]) for p in range(NPAIR)]
        attention(k, f"{tag}_at", Q, K, V, float(32 ** -0.5), False, O, masked=masked,
                  before=Projections(k, f"{tag}_in", jobs), after=FeedForward(k, ctx, m, tag, O, x, xo, parts, outs))


class FeedForward:

    def __init__(self, k, ctx, m, tag, O, x, xo, parts, outs):
        w = k.w
        self.k, self.m, self.O = k, m, O
        self.hn = ctx.enter_context(k.nc.sbuf_tensor(f"{tag}_hn", [P, CH], F32))
        self.H = ctx.enter_context(k.nc.sbuf_tensor(f"{tag}_h", [P, 4, CH], F32))
        self.norm1 = Norm(k, ctx, f"{tag}_n3", xo, [(self.hn, w[m + "ln3_g"], w[m + "ln3_b"])])
        self.norm2 = Norm(k, ctx, f"{tag}_n4", k.Z, outs)
        self.sum1 = Sum(k, f"{tag}_n3", xo, self.sums, [x], w[m + "li1_b"])
        self.sum2 = Sum(k, f"{tag}_n4", k.Z, self.sums, [xo] + parts, w[m + "li3_b"])
        self.mixed, self.normed, self.up, self.gelud, self.down = (k.sem(f"{tag}_{s}") for s in (
            "li1d", "normed", "up", "gelud", "down"))

    def half(self, t, h):
        return t[..., h * HALF:(h + 1) * HALF]

    def sums(self, h):
        return self.k.ps[6 + h][:, 0:HALF]

    def hide(self, h, f):
        return self.k.ps[(4, 2)[f // 2] + h][:, f % 2 * HALF:(f % 2 + 1) * HALF]

    def sync(self, sp):
        pass

    def tensor(self, pe):
        matmul, w, m, half, both = self.k.nc.tensor.matmul, self.k.w, self.m, self.half, range(2)
        for h in both:
            for t in range(4):
                ins = matmul(self.sums(h), w[m + "li1"][:, t, :], half(self.O[:, t, :], h), start=t == 0, stop=t == 3)
            ins.then_inc(self.mixed, 1)
        for h in both:
            self.sum1.wait(pe, h)
            self.norm1.center(pe, h)
        for h in both:
            self.norm1.mean(pe, h)
        for h in both:
            pe.wait_ge(self.normed, h + 1)
            for f in range(4):
                matmul(self.hide(h, f), w[m + "li2"][:, f * P:(f + 1) * P], half(self.hn, h), start=True,
                       stop=True).then_inc(self.up, 1)
        for h in both:
            for f in range(4):
                pe.wait_ge(self.gelud, 4 * h + f + 1)
                ins = matmul(self.sums(h), w[m + "li3"][:, f, :], half(self.H[:, f, :], h), start=f == 0, stop=f == 3)
            ins.then_inc(self.down, 1)
        for h in both:
            self.sum2.wait(pe, h)
            self.norm2.center(pe, h)
        for h in both:
            self.norm2.mean(pe, h)

    def scalar(self, act):
        nc, w, both = self.k.nc, self.k.w, range(2)
        for h in both:
            self.norm1.square(act, h)
        self.norm1.root(act)
        for h in both:
            for f in range(4):
                act.wait_ge(self.up, 4 * h + 2 * (f // 2) + 2)
                nc.scalar.activation(self.half(self.H[:, f, :], h), self.hide(h, f), ACT.Gelu,
                                     bias=w[self.m + "li2_b"][:, f:f + 1]).then_inc(self.gelud, 1)
        nc.scalar.preload_act_table_set("natural_log_exp_and_others")
        for h in both:
            self.norm2.square(act, h)
        self.norm2.root(act)

    def vector(self, dve):
        for h in range(2):
            dve.wait_ge(self.mixed, h + 1)
            self.sum1.add(dve, h)
        for h in range(2):
            self.norm1.out(dve, h).then_inc(self.normed, 1)
        for h in range(2):
            dve.wait_ge(self.down, h + 1)
            self.sum2.add(dve, h)
        for h in range(2):
            self.norm2.out(dve, h)


def norms(k, jobs):
    nc = k.nc
    with ExitStack() as ctx:
        all_ = [Norm(k, ctx, tag, z, outs, rows, tuple(range(4 * i, 4 * i + 4))) for i, (tag, z, outs, rows) in enumerate(jobs)]
        block = ctx.enter_context(nc.Block())

        @block.tensor
        def _(pe):
            for h in range(2):
                for n in all_:
                    n.center(pe, h)
            for h in range(2):
                for n in all_:
                    n.mean(pe, h)

        @block.scalar
        def _(act):
            for h in range(2):
                for n in all_:
                    n.square(act, h)
            for n in all_:
                n.root(act)

        @block.vector
        def _(dve):
            for h in range(2):
                for n in all_:
                    n.out(dve, h)


def cross(k):
    nc, w, X = k.nc, k.w, k.X
    with ExitStack() as ctx:
        sb = lambda n, s: ctx.enter_context(nc.sbuf_tensor(f"ca_{n}", s, F32))
        x1, x3, xn, yn, xo = (sb(n, [P, CH]) for n in ("x1", "x3", "xn", "yn", "xo"))
        norms(k, [("ca1", X, [(x1, w["ln1_g"], w["ln1_b"])], P)])
        norms(k, [("ca2", x1, [(xn, w["a1_lnx_g"], w["a1_lnx_b"]), (yn, w["a1_lny_g"], w["a1_lny_b"])], P)])
        mha(k, "a1_", "ca3", x1, xn, yn, P, True, xo, [x1], [(x3, w["ln2_g"], w["ln2_b"])])
        norms(k, [("ca4", x3, [(xn, w["a2_lnx_g"], w["a2_lnx_b"])], P), ("ca5", k.context, [(yn, w["a2_lny_g"], w["a2_lny_b"])], 64)])
        mha(k, "a2_", "ca6", x3, xn, yn, 64, False, xo, [x3, X], [(k.tokens[:, bass.ds(k.chunk * CH, CH)], None, None)])


def similarity(k):
    nc, w = k.nc, k.w
    names = ("queried", "squared", "summed", "logd", "rooted", "aligned", "similar", "copied")
    queried, squared, summed, logd, rooted, aligned, similar, copied = (k.sem(f"si_{s}") for s in names)
    cols = lambda c: slice(c * CH, (c + 1) * CH)
    query = lambda c: k.ps[c][:, :]
    with nc.sbuf_tensor("si_sq", [P, TOK], F32) as sq, nc.sbuf_tensor("si_r", [P, TOK], F32) as root, nc.Block() as block:
        @block.tensor
        def _(pe):
            for c in range(NCH):
                nc.tensor.matmul(query(c), w["qnat"], k.tokens[:, cols(c)], start=True, stop=True).then_inc(queried, 1)
            for c in range(NCH):
                pe.wait_ge(squared, c + 1)
                if c >= 2:
                    pe.wait_ge(logd, c - 1)
                nc.tensor.matmul(k.ps[4 + c % 2][:, :], w["heads8"], sq[:, cols(c)], start=True, stop=True).then_inc(summed, 1)
            for c in range(NCH):
                pe.wait_ge(aligned, c + 1)
                if c >= 2:
                    pe.wait_ge(copied, c - 1)
                nc.tensor.matmul(k.ps[6 + c % 2][0:2, :], w["guide"][:, :], root[:, cols(c)], start=True,
                                 stop=True).then_inc(similar, 1)

        @block.scalar
        def _(act):
            for c in range(NCH):
                act.wait_ge(queried, c + 1)
                nc.scalar.activation(sq[:, cols(c)], query(c), ACT.Square).then_inc(squared, 1)
            for c in range(NCH):
                act.wait_ge(summed, c + 1)
                nc.scalar.activation(root[:, cols(c)], k.ps[4 + c % 2][:, :], ACT.Ln).then_inc(logd, 1)
                act.wait_ge(logd, c + 1)
                nc.scalar.activation(root[:, cols(c)], root[:, cols(c)], ACT.Exp, scale=-0.5).then_inc(rooted, 1)

        @block.vector
        def _(dve):
            for c in range(NCH):
                dve.wait_ge(rooted, c + 1)
                nc.vector.tensor_tensor(root[:, cols(c)], root[:, cols(c)], query(c), ALU.mult).then_inc(aligned, 1)
            for c in range(NCH):
                dve.wait_ge(similar, c + 1)
                nc.vector.tensor_copy(k.sim[:, cols(c)], k.ps[6 + c % 2][0:2, :]).then_inc(copied, 1)


def last(k):
    nc, w = k.nc, k.w
    Qx = k.keep("qx", [P, 4, BCH, 32])
    seqs = lambda t: t[:, :].rearrange("p (b q) -> p b q", q=SEQ)
    with k.stage():
        chain, cleared = k.sem("cl_chain"), k.sem("cl_cleared")
        with nc.sbuf_tensor("cl_span", [2, 4], F32) as span, nc.Block() as block:
            @block.gpsimd
            def _(pool):
                nc.gpsimd.memset(Qx[:, :, :, :].rearrange("p t b c -> p (t b c)"), 0.0)

            @block.vector
            def _(dve):
                link = Count(dve, chain)
                ts = nc.vector.tensor_scalar
                toks = seqs(k.sim)[:, :, REG:]
                link(nc.vector.tensor_reduce(span[:, 0:1], toks, mybir.AxisListType.XY, ALU.min))
                link(nc.vector.tensor_reduce(span[:, 1:2], toks, mybir.AxisListType.XY, ALU.max))
                link(nc.vector.tensor_tensor(span[:, 2:3], span[:, 1:2], span[:, 0:1], ALU.subtract))
                link(nc.vector.reciprocal(span[:, 3:4], span[:, 2:3]))
                link(ts(k.sim[:, :], k.sim[:, :], span[:, 0:1], span[:, 3:4], ALU.subtract, ALU.mult))
                link(ts(k.sim[:, :], k.sim[:, :], 0.9, None, ALU.is_gt))
                link(nc.vector.memset(seqs(k.sim)[:, :, 0:REG], 1.0))
    with nc.Fori(0, NCH) as chunk:
        with k.stage():
            cols = bass.ds(chunk * CH, CH)
            with ExitStack() as ctx:
                sb = lambda n, s: ctx.enter_context(nc.sbuf_tensor(f"la_{n}", s, F32))
                O, X, Z = sb("o", [P, 4, CH]), k.X, k.Z
                qm, km = (ctx.enter_context(nc.sbuf_tensor(f"la_{n}", [2, CH], BF16)) for n in ("qm", "km"))
                Q, K, V = sb("q", [P, 4, CH]), sb("k", [P, 4, CH]), sb("v", [P, NPAIR, 512])
                wide = w["wide"]
                tile = lambda n, t: wide[:, n, t * P:(t + 1) * P]
                jobs = [(Q[:, t, :], [(tile(0, t), X[:, :]), (k.w["maskrowb"][:, :], qm[:, :])]) for t in range(4)]
                jobs += [(K[:, t, :], [(tile(1, t), X[:, :]), (k.w["maskrowb"][:, :], km[:, :])]) for t in range(4)]
                jobs += [(V[:, p, :], [(X[:, p * PAIR:(p + 1) * PAIR], wide[:, 2, :])]) for p in range(NPAIR)]
                terms = lambda h: [(w["proj"][:, t, :], O[:, t, h * HALF:(h + 1) * HALF]) for t in range(4)]
                attention(k, "la_at", Q, K, V, float(8 ** -0.5), False, O, regs=Qx,
                          before=LastProjections(k, "la_in", jobs, cols, qm, km, Q, Qx),
                          after=ProductNorm(k, ctx, "lan", terms, X, k.tokens[:, cols], w["projb"]))
            with nc.Block() as block:
                @block.sync
                def _(sp):
                    sp.dma_start(k.aps["out"][:, cols], k.tokens[:, cols]).then_inc(k.stored, 16)
    with nc.Block() as block:
        @block.sync
        def _(sp):
            sp.wait_ge(k.stored, 16 * NCH)


def build(nc, where, aps, upto=6):
    with ExitStack() as ctx:
        k = Core(nc, ctx)
        psum = ctx.enter_context(nc.psum_tensor("psum", [P, 8, 512], F32))
        k.ps_all = psum
        k.ps = [psum[:, i, :] for i in range(8)]
        k.aps = aps
        width = lambda name: list(aps[name].shape)
        k.packs = {name: k.keep(f"pack_{name}", width(name)) for name in ("const", "attn0", "ffn", "mamba")}
        expert_cols = aps["experts"].shape[1]
        names = [n for n, _ in PACKS] + [f"experts{c}" for c in range(expert_cols // SPLIT)] + ["tokens"]
        k.loaded = {name: ctx.enter_context(nc.semaphore(f"loaded_{name}")) for name in names}
        k.stored = ctx.enter_context(nc.semaphore("stored"))
        k.X, k.Z, k.Xin = (k.keep(n, [P, CH]) for n in ("X", "Z", "Xin"))
        k.slots = k.keep("slots", [P, CH])
        k.weight, k.pick = k.slots[:, 0:256], k.slots[:, 256:512].bitcast(I32)
        k.tokens = k.keep("tokens", [P, TOK])
        for name, shape, dt in (("wq0", [64, 8, 96], F32), ("wvo0", [P, 2, P], F32), ("rope", [64, SEQ], F32),
                                ("decay", [P, 2, 2, STATE], F32), ("guide", [P, 2], F32), ("foldb", [96, 32], BF16),
                                ("maskrowb", [2, P], BF16), ("onesr", [P, P], F32R), ("identr", [P, P], F32R)):
            k.w[name] = k.keep(name, shape, dt)

        with ExitStack() as layer0:
            k.high, k.low = (layer0.enter_context(nc.sbuf_tensor(n, [P, expert_cols], F32R)) for n in ("high", "low"))
            with k.stage(), nc.sbuf_tensor("pack_setup", width("setup"), F32) as k.packs["setup"], \
                    nc.sbuf_tensor("landed", [P, LANDINGS, SPLIT], F32) as k.landed:
                load(k)
                name_parts(k, where)
                setup(k)
                split_experts(k, where)
                with nc.Block() as block:
                    @block.scalar
                    def _(act):
                        nc.scalar.preload_act_table_set("natural_log_exp_and_others")
            with nc.Fori(0, NCH) as k.chunk:
                for stage in (attn0, moe, ffn):
                    with k.stage():
                        stage(k)

        k.packs = {name: k.keep(f"pack_{name}", width(name)) for name in ("cross", "last")}
        name_parts(k, where)
        k.context, k.sim = k.keep("context", [P, CH]), k.keep("sim", [2, TOK])
        with nc.Block() as block:
            @block.sync
            def _(sp):
                for name in ("cross", "last"):
                    sp.dma_start(k.packs[name][:, :], k.aps[name]).then_inc(k.loaded[name], 16)
        with nc.Fori(0, NCH) as k.chunk:
            for stage in (mamba, cross):
                with k.stage():
                    stage(k)
        with k.stage():
            similarity(k)
        last(k)


def kernel(**inputs):
    import concourse.bacc as bacc
    from concourse.bass_utils import run_bass_kernel_spmd

    a = {n: np.asarray(v) for n, v in inputs.items()}
    arrays, where, aps = {}, {}, {}
    for name, parts in PACKS:
        arrays[f"pack_{name}_dram"], where[name] = pack(parts(a))
    arrays["xT_dram"] = np.ascontiguousarray(a["x"].reshape(TOK, P).T)
    arrays["ctxT_dram"] = np.ascontiguousarray(a["ctx_512"].reshape(TOK, 64).T)
    for n, src in (("gatew", a["ctx_512"]), ("pick", a["itok_BxS2xS_0_7"])):
        arrays[f"{n}_dram"] = np.ascontiguousarray(src.reshape(NSEQ // 2, P, SEQ).transpose(1, 0, 2).reshape(P, -1))
    nc = bacc.Bacc("TRN2", target_bir_lowering=False, num_devices=1)
    for n, arr in arrays.items():
        ap = nc.dram_tensor(n, arr.shape, mybir.dt.from_np(arr.dtype), kind="ExternalInput").ap()
        aps[n[:-5].removeprefix("pack_")] = ap
    aps["out"] = nc.dram_tensor("out_dram", (P, TOK), F32, kind="ExternalOutput").ap()
    build(nc, where, aps)
    r = run_bass_kernel_spmd(nc, [arrays], core_ids=[0])
    return np.ascontiguousarray(r.results[0]["out_dram"].T).reshape(NSEQ, SEQ, P)
```
